# Optimizing a Trainium2 kernel written in Bass

```python
import numpy as np
import jax
import jax.numpy as jnp

def _softmax(x, axis=-1):
    return jax.nn.softmax(x, axis=axis)

def _gelu(x):
    return jax.nn.gelu(x, approximate=True)

def _silu(x):
    return jax.nn.silu(x)

def _sigmoid(x):
    return jax.nn.sigmoid(x)

def _layernorm(x, axis=-1, eps=1e-05):
    m = jnp.mean(x, axis=axis, keepdims=True)
    v = jnp.var(x, axis=axis, keepdims=True)
    return (x - m) / jnp.sqrt(v + eps)

def _scatter_add(tgt, idx, src, axis=0):
    return tgt.at[idx].add(src)

def _segment_sum(src, seg, n):
    return jax.ops.segment_sum(src, seg, n)
kernel_name = 'mk_gnn_ffn_d2_gnn_r32_83e154'

def setup_inputs(seed: int=0):
    np.random.seed(seed)
    _w = jnp.asarray

    def _rec_inputs():
        import jax
        import jax.numpy as jnp
        _gk = jax.random.key(seed)
        x = -8.776e-05 + 1 * jax.random.normal(jax.random.fold_in(_gk, 1), (3125, 256), jnp.float32)
        _s = jax.random.randint(jax.random.fold_in(_gk, 2), (25000,), 0, 3125, jnp.int32)
        _d = jax.random.randint(jax.random.fold_in(_gk, 3), (25000,), 0, 3125, jnp.int32)
        _loop = jnp.arange(3125, dtype=jnp.int32)
        src = jnp.concatenate([_s, _d, _loop])
        dst = jnp.concatenate([_d, _s, _loop])
        _o = jnp.argsort(dst, stable=True)
        src = src[_o]
        dst = dst[_o]
        edge_attr_32 = 0.000216709 + 1.00012 * jax.random.normal(jax.random.fold_in(_gk, 12), (53125, 32), jnp.float32)
        return (x, src, dst, edge_attr_32)
    x, src, dst, edge_attr_32 = _rec_inputs()

    def _L0_gnn_setup():
        import jax, jax.numpy as jnp
        import numpy as np
        N = 625
        E = 10000
        HID = 256
        HEADS = 8
        HD = HID // HEADS
        key = jax.random.key(seed)
        ks = jax.random.split(key, 12)
        scale = 1.0 / np.sqrt(HID).astype(np.float32)

        def lin_w(k):
            return jax.random.normal(k, (HID, HID), jnp.float32) * scale

        def lin_b(k):
            return jax.random.normal(k, (HID,), jnp.float32) * 0.01
        return {'h': jax.random.normal(ks[0], (N, HID), jnp.float32), 'Wq': lin_w(ks[1]), 'bq': lin_b(ks[2]), 'Wk': lin_w(ks[3]), 'bk': lin_b(ks[4]), 'Wv': lin_w(ks[5]), 'bv': lin_b(ks[6]), 'Wo': lin_w(ks[7]), 'bo': lin_b(ks[8]), 'rows': jax.random.randint(ks[9], (E,), 0, N), 'cols': jax.random.randint(ks[10], (E,), 0, N)}
    _L0_gnn_all = _L0_gnn_setup()
    _L0_gnn_in = {k: v for k, v in _L0_gnn_all.items() if k in ('Wq', 'bq', 'Wk', 'bk', 'Wv', 'bv', 'Wo', 'bo')}
    del _L0_gnn_all

    def _L0_ffn_setup():
        import jax, jax.numpy as jnp
        import numpy as np
        TOP_K = 2
        LN_EPS = 1e-05
        key = jax.random.key(seed)
        ks = jax.random.split(key, 8)
        B, S, D, E, H = (16, 1024, 256, 8, 1024)
        x = jax.random.normal(ks[0], (B, S, D), dtype=jnp.float32)
        Wr = jax.random.normal(ks[1], (D, E), dtype=jnp.float32) * 0.1
        br = jnp.zeros((E,), dtype=jnp.float32)
        ln_g = jnp.ones((E, D), dtype=jnp.float32)
        ln_b = jnp.zeros((E, D), dtype=jnp.float32)
        W1 = jax.random.normal(ks[2], (E, D, H), dtype=jnp.float32) * (1.0 / np.sqrt(D))
        b1 = jnp.zeros((E, H), dtype=jnp.float32)
        W2 = jax.random.normal(ks[3], (E, H, D), dtype=jnp.float32) * (1.0 / np.sqrt(H))
        b2 = jnp.zeros((E, D), dtype=jnp.float32)
        return {'x': x, 'Wr': Wr, 'br': br, 'ln_g': ln_g, 'ln_b': ln_b, 'W1': W1, 'b1': b1, 'W2': W2, 'b2': b2}
    _L0_ffn_all = _L0_ffn_setup()
    _L0_ffn_in = {k: v for k, v in _L0_ffn_all.items() if k in ('Wr', 'br', 'ln_g', 'ln_b', 'W1', 'b1', 'W2', 'b2')}
    del _L0_ffn_all

    def _L1_gnn_setup():
        import jax, jax.numpy as jnp
        import numpy as np
        N, E, D, H, C = (50000, 25000, 256, 4, 64)

        def _gat_layer(h_in, W, a_s, a_d, b, src, dst, n):
            Hh, Cc = a_s.shape
            h = (h_in @ W).reshape(n, Hh, Cc)
            alpha_s = jnp.sum(h * a_s, axis=-1)
            alpha_d = jnp.sum(h * a_d, axis=-1)
            e = jax.nn.leaky_relu(alpha_s[src] + alpha_d[dst], 0.2)
            m = jax.lax.stop_gradient(jax.ops.segment_max(e, dst, num_segments=n))
            ex = jnp.exp(e - m[dst])
            alpha = ex / jax.ops.segment_sum(ex, dst, num_segments=n)[dst]
            out = jax.ops.segment_sum(h[src] * alpha[:, :, None], dst, num_segments=n)
            return out.reshape(n, Hh * Cc) + b
        key = jax.random.key(seed)
        ks = jax.random.split(key, 12)
        x = jax.random.normal(ks[0], (N, D), dtype=jnp.float32)
        src = jax.random.randint(ks[1], (E,), 0, N, dtype=jnp.int32)
        dst = jax.random.randint(ks[2], (E,), 0, N, dtype=jnp.int32)
        dst = jnp.where(dst == src, (dst + 1) % N, dst)
        edge_index = jnp.stack([src, dst], axis=0)
        edge_attr = jax.random.normal(ks[3], (E, 32), dtype=jnp.float32)
        s = 1.0 / np.sqrt(D)
        sc = 1.0 / np.sqrt(C)
        return {'x': x, 'edge_index': edge_index, 'edge_attr': edge_attr, 'W0': jax.random.normal(ks[4], (D, H * C), dtype=jnp.float32) * s, 'a_src0': jax.random.normal(ks[5], (H, C), dtype=jnp.float32) * sc, 'a_dst0': jax.random.normal(ks[6], (H, C), dtype=jnp.float32) * sc, 'b0': jnp.zeros((H * C,), dtype=jnp.float32), 'W1': jax.random.normal(ks[7], (H * C, H * C), dtype=jnp.float32) * s, 'a_src1': jax.random.normal(ks[8], (H, C), dtype=jnp.float32) * sc, 'a_dst1': jax.random.normal(ks[9], (H, C), dtype=jnp.float32) * sc, 'b1': jnp.zeros((H * C,), dtype=jnp.float32)}
    _L1_gnn_all = _L1_gnn_setup()
    _L1_gnn_in = {k: v for k, v in _L1_gnn_all.items() if k in ('W0', 'a_src0', 'a_dst0', 'b0', 'W1', 'a_src1', 'a_dst1', 'b1')}
    del _L1_gnn_all

    def _L1_ffn_setup():
        import jax, jax.numpy as jnp
        import numpy as np
        B, A = (128, 8)
        IN, OUT = (256, 256)
        SH1, SH2 = (256, 128)
        EH1, EH2 = (128, 64)
        E, TOPK = (4, 2)

        def _shared_mlp(x, W1, b1, W2, b2, W3, b3):
            h = jax.nn.relu(x @ W1 + b1)
            h = jax.nn.relu(h @ W2 + b2)
            return h @ W3 + b3

        def _experts_mlp(x, eW1, eb1, eW2, eb2, eW3, eb3):
            h = jax.nn.relu(jnp.einsum('baf,efh->ebah', x, eW1) + eb1[:, None, None, :])
            h = jax.nn.relu(jnp.einsum('ebah,ehg->ebag', h, eW2) + eb2[:, None, None, :])
            o = jnp.einsum('ebag,ego->ebao', h, eW3) + eb3[:, None, None, :]
            return jnp.moveaxis(o, 0, -1)
        key = jax.random.key(seed)
        ks = jax.random.split(key, 16)
        s = 0.05
        return {'x': jax.random.normal(ks[0], (B, A, IN), jnp.float32), 'sW1': jax.random.normal(ks[1], (IN, SH1), jnp.float32) * s, 'sb1': jnp.zeros((SH1,), jnp.float32), 'sW2': jax.random.normal(ks[2], (SH1, SH2), jnp.float32) * s, 'sb2': jnp.zeros((SH2,), jnp.float32), 'sW3': jax.random.normal(ks[3], (SH2, OUT), jnp.float32) * s, 'sb3': jnp.zeros((OUT,), jnp.float32), 'eW1': jax.random.normal(ks[4], (E, IN, EH1), jnp.float32) * s, 'eb1': jnp.zeros((E, EH1), jnp.float32), 'eW2': jax.random.normal(ks[5], (E, EH1, EH2), jnp.float32) * s, 'eb2': jnp.zeros((E, EH2), jnp.float32), 'eW3': jax.random.normal(ks[6], (E, EH2, OUT), jnp.float32) * s, 'eb3': jnp.zeros((E, OUT), jnp.float32), 'gW': jax.random.normal(ks[7], (IN, E), jnp.float32) * s, 'gb': jnp.zeros((E,), jnp.float32)}
    _L1_ffn_all = _L1_ffn_setup()
    _L1_ffn_in = {k: v for k, v in _L1_ffn_all.items() if k in ('sW1', 'sb1', 'sW2', 'sb2', 'sW3', 'sb3', 'eW1', 'eb1', 'eW2', 'eb2', 'eW3', 'eb3', 'gW', 'gb')}
    del _L1_ffn_all
    return {'x': x, 'src': src, 'dst': dst, 'edge_attr_32': edge_attr_32, 'L0_gnn_Wq': _L0_gnn_in['Wq'], 'L0_gnn_bq': _L0_gnn_in['bq'], 'L0_gnn_Wk': _L0_gnn_in['Wk'], 'L0_gnn_bk': _L0_gnn_in['bk'], 'L0_gnn_Wv': _L0_gnn_in['Wv'], 'L0_gnn_bv': _L0_gnn_in['bv'], 'L0_gnn_Wo': _L0_gnn_in['Wo'], 'L0_gnn_bo': _L0_gnn_in['bo'], 'L0_ffn_Wr': _L0_ffn_in['Wr'], 'L0_ffn_br': _L0_ffn_in['br'], 'L0_ffn_ln_g': _L0_ffn_in['ln_g'], 'L0_ffn_ln_b': _L0_ffn_in['ln_b'], 'L0_ffn_W1': _L0_ffn_in['W1'], 'L0_ffn_b1': _L0_ffn_in['b1'], 'L0_ffn_W2': _L0_ffn_in['W2'], 'L0_ffn_b2': _L0_ffn_in['b2'], 'L1_gnn_W0': _L1_gnn_in['W0'], 'L1_gnn_a_src0': _L1_gnn_in['a_src0'], 'L1_gnn_a_dst0': _L1_gnn_in['a_dst0'], 'L1_gnn_b0': _L1_gnn_in['b0'], 'L1_gnn_W1': _L1_gnn_in['W1'], 'L1_gnn_a_src1': _L1_gnn_in['a_src1'], 'L1_gnn_a_dst1': _L1_gnn_in['a_dst1'], 'L1_gnn_b1': _L1_gnn_in['b1'], 'L1_ffn_sW1': _L1_ffn_in['sW1'], 'L1_ffn_sb1': _L1_ffn_in['sb1'], 'L1_ffn_sW2': _L1_ffn_in['sW2'], 'L1_ffn_sb2': _L1_ffn_in['sb2'], 'L1_ffn_sW3': _L1_ffn_in['sW3'], 'L1_ffn_sb3': _L1_ffn_in['sb3'], 'L1_ffn_eW1': _L1_ffn_in['eW1'], 'L1_ffn_eb1': _L1_ffn_in['eb1'], 'L1_ffn_eW2': _L1_ffn_in['eW2'], 'L1_ffn_eb2': _L1_ffn_in['eb2'], 'L1_ffn_eW3': _L1_ffn_in['eW3'], 'L1_ffn_eb3': _L1_ffn_in['eb3'], 'L1_ffn_gW': _L1_ffn_in['gW'], 'L1_ffn_gb': _L1_ffn_in['gb']}

def reference(x, src, dst, edge_attr_32, L0_gnn_Wq, L0_gnn_bq, L0_gnn_Wk, L0_gnn_bk, L0_gnn_Wv, L0_gnn_bv, L0_gnn_Wo, L0_gnn_bo, L0_ffn_Wr, L0_ffn_br, L0_ffn_ln_g, L0_ffn_ln_b, L0_ffn_W1, L0_ffn_b1, L0_ffn_W2, L0_ffn_b2, L1_gnn_W0, L1_gnn_a_src0, L1_gnn_a_dst0, L1_gnn_b0, L1_gnn_W1, L1_gnn_a_src1, L1_gnn_a_dst1, L1_gnn_b1, L1_ffn_sW1, L1_ffn_sb1, L1_ffn_sW2, L1_ffn_sb2, L1_ffn_sW3, L1_ffn_sb3, L1_ffn_eW1, L1_ffn_eb1, L1_ffn_eW2, L1_ffn_eb2, L1_ffn_eW3, L1_ffn_eb3, L1_ffn_gW, L1_ffn_gb):
    import jax
    import jax.numpy as jnp

    def _L0_gnn_ref(h, Wq, bq, Wk, bk, Wv, bv, Wo, bo, rows, cols):
        import jax, jax.numpy as jnp
        import numpy as np
        N = 625
        E = 10000
        HID = 256
        HEADS = 8
        HD = HID // HEADS
        n = h.shape[0]
        scaling = HD ** (-0.5)
        q = (h @ Wq + bq).reshape(n, HD, HEADS) * scaling
        k = (h @ Wk + bk).reshape(n, HD, HEADS)
        v = (h @ Wv + bv).reshape(n, HD, HEADS)
        s = jnp.einsum('edh,edh->eh', q[rows], k[cols])
        m = jax.ops.segment_max(s, rows, num_segments=n)
        e = jnp.exp(s - m[rows])
        z = jax.ops.segment_sum(e, rows, num_segments=n)
        attn = e / z[rows]
        out = jax.ops.segment_sum(attn[:, None, :] * v[cols], rows, num_segments=n)
        return out.reshape(n, -1) @ Wo + bo

    def _L0_ffn_ref(x, Wr, br, ln_g, ln_b, W1, b1, W2, b2):
        import jax, jax.numpy as jnp
        import numpy as np
        TOP_K = 2
        LN_EPS = 1e-05
        B, S, D = x.shape
        N = B * S
        xt = x.reshape(N, D)
        logits = xt @ Wr + br
        probs = jax.nn.softmax(logits, axis=-1)
        top_p, top_idx = jax.lax.top_k(probs, TOP_K)
        weights = top_p / top_p.sum(axis=-1, keepdims=True)
        mu = xt.mean(axis=-1, keepdims=True)
        var = ((xt - mu) ** 2).mean(axis=-1, keepdims=True)
        xn = (xt - mu) * jax.lax.rsqrt(var + LN_EPS)
        xe = xn[None, :, :] * ln_g[:, None, :] + ln_b[:, None, :]
        h = jax.nn.gelu(jnp.einsum('end,edh->enh', xe, W1) + b1[:, None, :], approximate=False)
        y = jnp.einsum('enh,ehd->end', h, W2) + b2[:, None, :]
        y_tok = jnp.transpose(y, (1, 0, 2))
        sel = jnp.take_along_axis(y_tok, top_idx[:, :, None], axis=1)
        out = (weights[:, :, None] * sel).sum(axis=1)
        return out.reshape(B, S, D)

    def _L1_gnn_ref(x, edge_index, edge_attr, W0, a_src0, a_dst0, b0, W1, a_src1, a_dst1, b1):
        import jax, jax.numpy as jnp
        import numpy as np
        N, E, D, H, C = (50000, 25000, 256, 4, 64)

        def _gat_layer(h_in, W, a_s, a_d, b, src, dst, n):
            Hh, Cc = a_s.shape
            h = (h_in @ W).reshape(n, Hh, Cc)
            alpha_s = jnp.sum(h * a_s, axis=-1)
            alpha_d = jnp.sum(h * a_d, axis=-1)
            e = jax.nn.leaky_relu(alpha_s[src] + alpha_d[dst], 0.2)
            m = jax.lax.stop_gradient(jax.ops.segment_max(e, dst, num_segments=n))
            ex = jnp.exp(e - m[dst])
            alpha = ex / jax.ops.segment_sum(ex, dst, num_segments=n)[dst]
            out = jax.ops.segment_sum(h[src] * alpha[:, :, None], dst, num_segments=n)
            return out.reshape(n, Hh * Cc) + b
        n = x.shape[0]
        loops = jnp.arange(n, dtype=edge_index.dtype)
        src = jnp.concatenate([edge_index[0], loops])
        dst = jnp.concatenate([edge_index[1], loops])
        h = jax.nn.gelu(_gat_layer(x, W0, a_src0, a_dst0, b0, src, dst, n), approximate=False)
        h = jax.nn.gelu(_gat_layer(h, W1, a_src1, a_dst1, b1, src, dst, n), approximate=False)
        return h

    def _L1_ffn_ref(x, sW1, sb1, sW2, sb2, sW3, sb3, eW1, eb1, eW2, eb2, eW3, eb3, gW, gb):
        import jax, jax.numpy as jnp
        import numpy as np
        B, A = (128, 8)
        IN, OUT = (256, 256)
        SH1, SH2 = (256, 128)
        EH1, EH2 = (128, 64)
        E, TOPK = (4, 2)

        def _shared_mlp(x, W1, b1, W2, b2, W3, b3):
            h = jax.nn.relu(x @ W1 + b1)
            h = jax.nn.relu(h @ W2 + b2)
            return h @ W3 + b3

        def _experts_mlp(x, eW1, eb1, eW2, eb2, eW3, eb3):
            h = jax.nn.relu(jnp.einsum('baf,efh->ebah', x, eW1) + eb1[:, None, None, :])
            h = jax.nn.relu(jnp.einsum('ebah,ehg->ebag', h, eW2) + eb2[:, None, None, :])
            o = jnp.einsum('ebag,ego->ebao', h, eW3) + eb3[:, None, None, :]
            return jnp.moveaxis(o, 0, -1)
        all_out = _experts_mlp(x, eW1, eb1, eW2, eb2, eW3, eb3)
        shared = _shared_mlp(x, sW1, sb1, sW2, sb2, sW3, sb3)
        gates = jax.nn.softmax(x @ gW + gb, axis=-1)
        topv, topi = jax.lax.top_k(gates, TOPK)
        topw = jax.nn.softmax(topv, axis=-1)
        sel = jnp.take_along_axis(all_out, topi[:, :, None, :], axis=-1)
        gated = jnp.sum(sel * topw[:, :, None, :], axis=-1)
        return shared + gated
    edge_index = jnp.stack([src, dst])
    x = x + _L0_gnn_ref(_layernorm(x, axis=-1), L0_gnn_Wq, L0_gnn_bq, L0_gnn_Wk, L0_gnn_bk, L0_gnn_Wv, L0_gnn_bv, L0_gnn_Wo, L0_gnn_bo, src, dst)
    x = x + _L0_ffn_ref(_layernorm(x, axis=-1)[None], L0_ffn_Wr, L0_ffn_br, L0_ffn_ln_g, L0_ffn_ln_b, L0_ffn_W1, L0_ffn_b1, L0_ffn_W2, L0_ffn_b2)[0]
    x = x + _L1_gnn_ref(_layernorm(x, axis=-1), edge_index, edge_attr_32, L1_gnn_W0, L1_gnn_a_src0, L1_gnn_a_dst0, L1_gnn_b0, L1_gnn_W1, L1_gnn_a_src1, L1_gnn_a_dst1, L1_gnn_b1)
    x = x + _L1_ffn_ref(_layernorm(x, axis=-1)[None], L1_ffn_sW1, L1_ffn_sb1, L1_ffn_sW2, L1_ffn_sb2, L1_ffn_sW3, L1_ffn_sb3, L1_ffn_eW1, L1_ffn_eb1, L1_ffn_eW2, L1_ffn_eb2, L1_ffn_eW3, L1_ffn_eb3, L1_ffn_gW, L1_ffn_gb)[0]
    return x

_drawn_inputs = setup_inputs


def setup_inputs(seed=0):
    import zlib

    import numpy as np

    out = dict(_drawn_inputs(seed))
    spreads = {'L0_ffn_br': (0.0, 0.1),
     'L0_ffn_ln_g': (1.0, 0.2),
     'L0_ffn_ln_b': (0.0, 0.1),
     'L0_ffn_b1': (0.0, 0.1),
     'L0_ffn_b2': (0.0, 0.1),
     'L1_gnn_b0': (0.0, 0.309),
     'L1_gnn_b1': (0.0, 0.1),
     'L1_ffn_sb1': (0.0, 0.456),
     'L1_ffn_sb2': (0.0, 0.1),
     'L1_ffn_sb3': (0.0, 0.1),
     'L1_ffn_eb1': (0.0, 0.8),
     'L1_ffn_eb2': (0.0, 0.54),
     'L1_ffn_eb3': (0.0, 0.1),
     'L1_ffn_gb': (0.0, 0.436)}
    factors = {'L0_gnn_bq': 3.549,
     'L0_gnn_bk': 8.0,
     'L1_gnn_a_dst0': 8.0,
     'L1_gnn_a_src1': 8.0,
     'L1_gnn_a_dst1': 8.0}
    for name, (base, spread) in spreads.items():
        noise = np.random.default_rng([zlib.crc32(name.encode()), seed]).standard_normal(out[name].shape)
        drawn = base * np.exp(spread * noise) if base else spread * noise
        out[name] = jnp.asarray(drawn.astype(out[name].dtype))
    for name, factor in factors.items():
        out[name] = (out[name] * factor).astype(out[name].dtype)
    return out
```

```python
import concourse.bass as bass
from concourse import mybir
from contextlib import ExitStack
import numpy as np

F32, BF16, F16, I32 = mybir.dt.float32, mybir.dt.bfloat16, mybir.dt.float16, mybir.dt.int32
ALU, ACT, AX = mybir.AluOpType, mybir.ActivationFunctionType, mybir.AxisListType

P = 128
N_NODES, N_EDGES = 3125, 53125
NT = -(-N_NODES // P)
NPAD = NT * P
DUMMY = 15 * P
TABLE_ROWS = NPAD + P
ROUNDS = 4
ROWE = 512
EROWS = -(-N_EDGES // ROWE)
EX = ROWE // P
CHAINS = 8
EU = EROWS // CHAINS
ETILES = EROWS * EX
WIN = 512
MAX_CHUNKS = (N_EDGES + 3 * NT + 8 * NT) // ROUNDS + 1
MAX_WIN = -(-MAX_CHUNKS * ROUNDS // WIN)
MAX_CHUNKS = MAX_WIN * WIN // ROUNDS
KEY_PAD = 4095
RMAX = bass.bass_isa.ReduceOp.max


def table_row(t):
    return (t + (1 if t >= DUMMY // P else 0)) * P


MANY_SEMS = 100


class Mem:

    past = []

    def __init__(self, nc, name):
        self.nc, self.name, self.stack, self.sems = nc, name, ExitStack(), []

    def __enter__(self):
        self.stack.__enter__()
        return self

    def __exit__(self, *a):
        self.past.extend(self.sems)
        if len(self.past) > MANY_SEMS:
            self.nc.clear_and_free_semaphores(self.past)
            self.nc.all_engine_barrier()
            self.past.clear()
        return self.stack.__exit__(*a)

    def sb(self, name, shape, dt=F32):
        return self.stack.enter_context(self.nc.sbuf_tensor(f"{self.name}_{name}", shape, dt))

    def ps(self, name, shape, dt=F32):
        return self.stack.enter_context(self.nc.psum_tensor(f"{self.name}_{name}", shape, dt))

    def sem(self, name):
        self.sems.append(self.nc.alloc_semaphore(name=f"{self.name}_{name}"))
        return self.sems[-1]


def build_constants(nc, c):
    with Mem(nc, "cst") as m:
        made, seen = m.sem("made"), m.sem("seen")
        with nc.Block() as block:
            @block.gpsimd
            def _(pool):
                pool.iota(c.lane_f[:, :], pattern=[[0, 1]], base=0, channel_multiplier=1,
                          allow_small_or_imprecise_dtypes=True).then_inc(made, 1)
                pool.iota(c.iota_f[:, :], pattern=[[1, WIN]], base=0, channel_multiplier=0,
                          allow_small_or_imprecise_dtypes=True).then_inc(made, 1)
                pool.memset(c.ident[:, :], 0.0).then_inc(made, 1)
                pool.memset(c.order_bias[:, :], 0.0).then_inc(made, 1)
                pool.memset(c.ones[:, :], 1.0).then_inc(made, 1)
                pool.memset(c.ones_b[:, :], 1.0).then_inc(made, 1)
                pool.memset(c.before[:, :], 1.0).then_inc(made, 1)
                pool.memset(c.zeros[:, :], 0.0).then_inc(made, 1)
                pool.wait_ge(made, 8)
                pool.affine_select(out=c.ident[:, :], in_=c.ident[:, :], compare_op=ALU.not_equal, fill=1.0,
                                   base=0, pattern=[[-1, P]], channel_multiplier=1).then_inc(made, 1)
                pool.affine_select(out=c.order_bias[:, :], in_=c.order_bias[:, :], compare_op=ALU.is_gt, fill=-2.0,
                                   base=0, pattern=[[1, P]], channel_multiplier=-1).then_inc(made, 1)
                pool.affine_select(out=c.before[:, :], in_=c.before[:, :], compare_op=ALU.is_gt, fill=0.0,
                                   base=0, pattern=[[1, P]], channel_multiplier=-1).then_inc(made, 1)

            @block.vector
            def _(dve):
                dve.wait_ge(made, 11)
                dve.tensor_copy(c.ident_b[:, :], c.ident[:, :]).then_inc(seen, 1)
                dve.tensor_copy(c.iota_b[:, :], c.iota_f[:, 0:P]).then_inc(seen, 1)
                dve.tensor_copy(c.iota_h[:, :], c.iota_f[:, :]).then_inc(seen, 1)


def build_neighbour_table(nc, c, g, key_in, val_in):
    with Mem(nc, f"ix{g.name}") as m:
        lo_c = m.sb("lo_c", [P, EU, EX, CHAINS], BF16)
        hi_c = m.sb("hi_c", [P, EU, EX, CHAINS], BF16)
        val_c = m.sb("val_c", [P, EU, EX, CHAINS])
        oh_lo = m.sb("oh_lo", [P, EU, EX * CHAINS, P], BF16)
        oh_hi = m.sb("oh_hi", [P, EU, EX * CHAINS, NT], BF16)
        zeros = m.sb("zeros", [P, WIN], BF16)
        place = m.sb("place", [P, EU, EX, CHAINS, 3])
        col = m.sb("col", [P, EU, EX, CHAINS])
        start = m.sb("start", [P, CHAINS, NT])
        lane_of = m.sb("lane_of", [P, NT])

        edges_in, parts, split, turned, evacuated = (m.sem(x) for x in ("edges_in", "parts", "split", "turned", "evac"))
        ohs, counted, padded = m.sem("ohs"), m.sem("counted"), m.sem("padded")

        full = EROWS - 1
        rest = N_EDGES - full * ROWE
        with Mem(nc, f"ixa{g.name}") as a:
            turn = [a.ps(f"turn{k}", [P, EX, P]) for k in range(3)]
            hist = a.ps("hist", [P, 512])
            with Mem(nc, f"ixr{g.name}") as r:
                key_i, val_i = r.sb("key_i", [EROWS, ROWE], I32), r.sb("val_i", [EROWS, ROWE], I32)
                lo_i, hi_i = r.sb("lo_i", [EROWS, ROWE], I32), r.sb("hi_i", [EROWS, ROWE], I32)
                part_f = r.sb("part_f", [EROWS, 3, ROWE])
                part_b = r.sb("part_b", [EROWS, 2, ROWE], BF16)
                above = r.sb("above", [EROWS, ROWE])
                with nc.Block() as block:
                    @block.sync
                    def _(sp):
                        sp.wait_ge(padded, 2)
                        for src, dst in ((key_in, key_i), (val_in, val_i)):
                            sp.dma_start(dst[0:full, :], src[0:full * ROWE].rearrange("(p e) -> p e", e=ROWE)).then_inc(edges_in, 16)
                            sp.dma_start(dst[full:EROWS, 0:rest], src[full * ROWE:N_EDGES].rearrange("(p e) -> p e", p=1)).then_inc(edges_in, 16)
                        sp.wait_ge(split, 1)
                        sp.dma_start(g.key_parts.rearrange("h (p e) -> p h e", e=ROWE), part_b[:, :, :]).then_inc(parts, 16)
                        sp.wait_ge(parts, 16)

                    @block.vector
                    def _(dve):
                        dve.memset(key_i[:, :], KEY_PAD).then_inc(padded, 1)
                        dve.memset(val_i[:, :], 0).then_inc(padded, 1)
                        dve.memset(zeros[:, :], 0.0).then_inc(padded, 1)
                        dve.wait_ge(edges_in, 64)
                        dve.tensor_single_scalar(lo_i[:, :], key_i[:, :], P - 1, ALU.bitwise_and).then_inc(counted, 1)
                        dve.tensor_single_scalar(hi_i[:, :], key_i[:, :], 7, ALU.logical_shift_right).then_inc(counted, 1)
                        dve.tensor_scalar(above[:, :], val_i[:, :], float(DUMMY), float(P), ALU.is_ge, ALU.mult).then_inc(counted, 1)
                        dve.wait_ge(counted, 3)
                        dve.tensor_copy(part_f[:, 0, :], lo_i[:, :]).then_inc(counted, 1)
                        dve.tensor_copy(part_f[:, 1, :], hi_i[:, :]).then_inc(counted, 1)
                        dve.scalar_tensor_tensor(part_f[:, 2, :], above[:, :], -float(DUMMY), val_i[:, :],
                                                 ALU.add, ALU.add).then_inc(counted, 1)
                        dve.wait_ge(counted, 6)
                        dve.scalar_tensor_tensor(part_f[:, 2, :], key_i[:, :], float(NPAD), part_f[:, 2, :],
                                                 ALU.is_lt, ALU.mult).then_inc(counted, 1)
                        dve.tensor_copy(part_b[:, :, :], part_f[:, 0:2, :]).then_inc(split, 1)
                        dve.wait_ge(turned, 1)
                        for k, out in enumerate((lo_c, hi_c, val_c)):
                            for x in range(EX):
                                dve.tensor_copy(out[:, :, x, :],
                                                turn[k][:, x, 0:EROWS].rearrange("p (q u) -> p u q", u=EU)).then_inc(evacuated, 1)
                        dve.wait_ge(evacuated, 3 * EX)
                        with dve.Fori(0, EU) as u:
                            dve.tensor_tensor(oh_lo[:, bass.ds(u, 1), :, :].rearrange("p a t l -> p (a t) l"),
                                              lo_c[:, bass.ds(u, 1), :, :].rearrange("p a x q -> p (a x q)").unsqueeze(2).to_broadcast([P, EX * CHAINS, P]),
                                              c.iota_b[:, :].unsqueeze(1).to_broadcast([P, EX * CHAINS, P]),
                                              ALU.is_equal).then_inc(ohs, 1)
                            dve.tensor_tensor(oh_hi[:, bass.ds(u, 1), :, :].rearrange("p a t l -> p (a t) l"),
                                              hi_c[:, bass.ds(u, 1), :, :].rearrange("p a x q -> p (a x q)").unsqueeze(2).to_broadcast([P, EX * CHAINS, NT]),
                                              c.iota_b[:, 0:NT].unsqueeze(1).to_broadcast([P, EX * CHAINS, NT]),
                                              ALU.is_equal).then_inc(ohs, 1)

                    @block.tensor
                    def _(pe):
                        pe.wait_ge(counted, 7)
                        for k in range(3):
                            for x in range(EX):
                                last = pe.transpose(turn[k][:, x, 0:EROWS], part_f[:, k, x * P:(x + 1) * P], c.ident[0:EROWS, 0:EROWS])
                        last.then_inc(turned, 1)
                        pe.wait_ge(padded, 3)
                        pe.matmul(hist[:, 0:CHAINS * NT], zeros[:, 0:P], zeros[:, 0:CHAINS * NT], start=True, stop=True)
                        with pe.Fori(0, EU) as u:
                            pe.wait_ge(ohs, u * 2 + 2)
                            for t in range(EX * CHAINS):
                                q = t % CHAINS
                                last = pe.matmul(hist[:, q * NT:(q + 1) * NT],
                                                 oh_lo[:, bass.ds(u, 1), t, :].rearrange("p a l -> p (a l)"),
                                                 oh_hi[:, bass.ds(u, 1), t, :].rearrange("p a l -> p (a l)"),
                                                 start=False, stop=True, skip_group_check=True)
                            last.then_inc(g.hist_done, 1)

            counts = a.sb("counts", [P, CHAINS, NT])
            deg = a.sb("deg", [P, NT])
            skey = a.sb("skey", [P, NT])
            keys_bc = a.sb("keys_bc", [P, NPAD])
            junk = [a.sb(f"junk{k}", [P, NPAD], BF16) for k in range(2)]
            above_v, sign_v = a.sb("above_v", [P, NT]), a.sb("sign_v", [P, NT])
            nskey = a.sb("nskey", [P, NT])
            node_f = a.sb("node_f", [P, NT])
            rank_i = a.sb("rank_i", [P, 3, NT], I32)
            rank_f = a.sb("rank_f", [P, 3, NT])
            oh_lane = a.sb("oh_lane", [P, NT, P])
            oh_tile = a.sb("oh_tile", [P, NT, NT])
            oh_val = a.sb("oh_val", [P, NT, 2, NT])
            sorted_ps = a.ps("sorted", [P, 2 * NT])
            sdeg, mdeg = a.sb("sdeg", [P, NT]), a.sb("mdeg", [P, NT])
            ch_i, ch_f = a.sb("ch_i", [P, NT], I32), a.sb("ch_f", [P, NT])
            cum = a.sb("cum", [P, NT + 1])
            pick = a.sb("pick", [P, NT, NT])
            base_of = a.sb("base_of", [P, NT])
            above_n = a.sb("above_n", [P, NT])
            n_dve = NT // 2 + 1
            chain, keyed, key_out, key_bc, signs, ranked, sums, maxed = (
                a.sem(x) for x in ("chain", "keyed", "key_out", "key_bc", "signs", "ranked", "sums", "maxed"))
            with nc.Block() as block:
                @block.gpsimd
                def _(pool):
                    pool.iota(node_f[:, :], pattern=[[P, NT]], base=0, channel_multiplier=1,
                              allow_small_or_imprecise_dtypes=True).then_inc(keyed, 1)
                    pool.wait_ge(maxed, 1)
                    pool.partition_all_reduce(mdeg[:, :], sdeg[:, :], P, RMAX).then_inc(maxed, 1)

                @block.vector
                def _(dve):
                    n = [0]

                    def step(ins):
                        n[0] += 1
                        ins.then_inc(chain, 1)
                        dve.wait_ge(chain, n[0])

                    dve.wait_ge(g.hist_done, EU)
                    step(dve.tensor_copy(counts[:, :, :], hist[:, 0:CHAINS * NT].rearrange("p (q t) -> p q t", t=NT)))
                    step(dve.tensor_reduce(deg[:, :], counts[:, :, :].rearrange("p q t -> p t q"), AX.X, ALU.add))
                    dve.wait_ge(keyed, 1)
                    step(dve.tensor_scalar(skey[:, :], deg[:, :], 4000.0, 4096.0, ALU.min, ALU.mult))
                    step(dve.tensor_tensor(skey[:, :], skey[:, :], node_f[:, :], ALU.add))
                    dve.tensor_scalar(nskey[:, :], skey[:, :], -1.0, None, ALU.mult).then_inc(keyed, 1)
                    step(dve.memset(start[:, 0, :], 0.0))
                    for q in range(1, CHAINS):
                        step(dve.tensor_tensor(start[:, q, :], start[:, q - 1, :], counts[:, q - 1, :], ALU.add))
                    dve.wait_ge(key_bc, 16)
                    for t in range(n_dve):
                        if t >= 2:
                            dve.wait_ge(ranked, t - 1)
                        dve.tensor_scalar(junk[0][:, :], keys_bc[:, :], skey[:, t:t + 1], 0.0, ALU.is_gt, ALU.add,
                                          accum_out=above_v[:, t:t + 1]).then_inc(ranked, 1)
                        dve.wait_ge(ranked, t + 1)
                    dve.wait_ge(signs, NT - n_dve)
                    step(dve.tensor_scalar(above_v[:, n_dve:NT], sign_v[:, n_dve:NT], float(NPAD - 1), 0.5, ALU.add, ALU.mult))
                    step(dve.tensor_copy(rank_i[:, 0, :], above_v[:, :]))
                    step(dve.tensor_single_scalar(rank_i[:, 1, :], rank_i[:, 0, :], P - 1, ALU.bitwise_and))
                    step(dve.tensor_single_scalar(rank_i[:, 2, :], rank_i[:, 0, :], 7, ALU.logical_shift_right))
                    step(dve.tensor_copy(rank_f[:, :, :], rank_i[:, :, :]))
                    step(dve.tensor_copy(lane_of[:, :], rank_f[:, 1, :]))
                    step(dve.tensor_tensor(oh_lane[:, :, :], rank_f[:, 1, :].unsqueeze(2).to_broadcast([P, NT, P]),
                                           c.iota_f[:, 0:P].unsqueeze(1).to_broadcast([P, NT, P]), ALU.is_equal))
                    step(dve.tensor_tensor(oh_tile[:, :, :], rank_f[:, 2, :].unsqueeze(2).to_broadcast([P, NT, NT]),
                                           c.iota_f[:, 0:NT].unsqueeze(1).to_broadcast([P, NT, NT]), ALU.is_equal))
                    step(dve.tensor_scalar(above_n[:, :], node_f[:, :], float(DUMMY), float(P), ALU.is_ge, ALU.mult))
                    step(dve.tensor_tensor(above_n[:, :], above_n[:, :], node_f[:, :], ALU.add))
                    step(dve.tensor_tensor(oh_val[:, :, 0, :], oh_tile[:, :, :],
                                           above_n[:, :].unsqueeze(2).to_broadcast([P, NT, NT]), ALU.mult))
                    step(dve.tensor_tensor(oh_val[:, :, 1, :], oh_tile[:, :, :],
                                           deg[:, :].unsqueeze(2).to_broadcast([P, NT, NT]), ALU.mult))
                    dve.sem_inc(ranked, 1)
                    dve.wait_ge(sums, 1)
                    step(dve.tensor_copy(g.order[:, :], sorted_ps[:, 0:NT]))
                    dve.tensor_copy(sdeg[:, :], sorted_ps[:, NT:2 * NT]).then_inc(maxed, 1)
                    dve.wait_ge(maxed, 2)
                    step(dve.tensor_scalar(ch_f[:, :], mdeg[:, :], float(ROUNDS - 1), float(2 * ROUNDS), ALU.add, ALU.max))
                    step(dve.tensor_copy(ch_i[:, :], ch_f[:, :]))
                    step(dve.tensor_single_scalar(ch_i[:, :], ch_i[:, :], 2, ALU.logical_shift_right))
                    step(dve.tensor_copy(ch_f[:, :], ch_i[:, :]))
                    step(dve.memset(cum[:, 0:1], 0.0))
                    step(dve.tensor_tensor_scan(cum[:, 1:NT + 1], c.ones[:, 0:NT], ch_f[:, :], 0.0, ALU.mult, ALU.add))
                    step(dve.tensor_copy(g.first_chunk[:, :], cum[:, :]))
                    step(dve.tensor_scalar(cum[:, :], cum[:, :], float(ROUNDS), None, ALU.mult))
                    step(dve.tensor_tensor(pick[:, :, :], oh_tile[:, :, :],
                                           cum[:, 0:NT].unsqueeze(1).to_broadcast([P, NT, NT]), ALU.mult))
                    step(dve.tensor_reduce(base_of[:, :], pick[:, :, :], AX.X, ALU.add))
                    step(dve.tensor_tensor(start[:, :, :], start[:, :, :],
                                           base_of[:, :].unsqueeze(1).to_broadcast([P, CHAINS, NT]), ALU.add))

                @block.sync
                def _(sp):
                    sp.wait_ge(keyed, 2)
                    sp.dma_start(g.sort_keys.rearrange("(p t) -> p t", t=NT), skey[:, :]).then_inc(key_out, 16)
                    sp.wait_ge(key_out, 16)
                    sp.dma_start(keys_bc[:, :], g.sort_keys.rearrange("(a n) -> a n", a=1).to_broadcast([P, NPAD])).then_inc(key_bc, 16)

                @block.scalar
                def _(act):
                    act.wait_ge(keyed, 2)
                    act.wait_ge(key_bc, 16)
                    for k, t in enumerate(range(n_dve, NT)):
                        act.activation(junk[1][:, :], keys_bc[:, :], ACT.Sign, bias=nskey[:, t:t + 1],
                                       accum_out=sign_v[:, t:t + 1]).then_inc(signs, 1)
                        act.wait_ge(signs, k + 1)

                @block.tensor
                def _(pe):
                    pe.wait_ge(ranked, n_dve + 1)
                    for t in range(NT):
                        last = pe.matmul(sorted_ps[:, :], oh_lane[:, t, :], oh_val[:, t, :, :].rearrange("p a b -> p (a b)"),
                                         start=(t == 0), stop=(t == NT - 1))
                    last.then_inc(sums, 1)

        with Mem(nc, f"ixb{g.name}") as b:
            run = b.ps("run", [P, 512])
            same = b.ps("same", [P, CHAINS, P])
            found = b.ps("found", [P, 2, 512])
            parts_bc = b.sb("parts_bc", [P, 2, CHAINS, ROWE], BF16)
            ohT_lo = b.sb("ohT_lo", [P, 2, CHAINS, ROWE], BF16)
            ohT_hi = b.sb("ohT_hi", [NT, 2, CHAINS, ROWE], BF16)
            snap = b.sb("snap", [P, 2, CHAINS, 3 * NT], BF16)
            earlier = b.sb("earlier", [P, 2, CHAINS, P], BF16)
            pick = b.sb("pick", [P, 2, CHAINS, 3, NT])
            bc_in = b.sem("bc_in")
            (begun, ohT_ready, snap_hi, snap_lo, same_ready, earlier_ready, found_ready,
             picked, reduced, advanced, filled) = (
                b.sem(x) for x in ("begun", "ohT_ready", "snap_hi", "snap_lo", "same_ready",
                                   "earlier_ready", "found_ready", "picked", "reduced", "advanced", "filled"))
            kp = g.key_parts.rearrange("h (q u e) -> h q u e", q=CHAINS, e=ROWE)
            with nc.Block() as block:
                @block.sync
                def _(sp):
                    with sp.Fori(0, EU) as u:
                        sp.wait_ge(ohT_ready, u * 2 + 3)
                        for h in range(2):
                            sp.dma_start(parts_bc[:, h, :, :],
                                         kp[h, :, bass.ds(u, 1), :].rearrange("q a e -> (q a) e").unsqueeze(0).to_broadcast([P, CHAINS, ROWE])).then_inc(bc_in, 16)

                @block.scalar
                def _(act):
                    act.wait_ge(begun, 1)
                    with act.Fori(0, EU) as u:
                        for x in range(EX):
                            s = u * EX + (x + 1)
                            k = x % 2
                            act.wait_ge(advanced, s)
                            act.activation(snap[:, k, :, 0:NT], run[:, 0:CHAINS * NT].rearrange("p (q t) -> p q t", t=NT),
                                           ACT.Copy).then_inc(snap_hi, 1)
                            act.wait_ge(same_ready, s)
                            act.activation(earlier[:, k, :, :], same[:, :, :], ACT.Relu, bias=c.minus1[:, 0:1]).then_inc(earlier_ready, 1)

                @block.vector
                def _(dve):
                    dve.memset(c.minus1[:, :], -1.0).then_inc(filled, 1)
                    for k in range(2):
                        dve.tensor_copy(snap[:, k, :, 2 * NT:3 * NT],
                                        lane_of[:, :].unsqueeze(1).to_broadcast([P, CHAINS, NT])).then_inc(filled, 1)
                    dve.wait_ge(filled, 3)
                    dve.sem_inc(begun, 1)
                    dve.sem_inc(picked, 2)

                    dve.sem_inc(ohT_ready, 3)
                    with dve.Fori(0, EU) as u:
                        uk = u % 2
                        dve.wait_ge(found_ready, u * EX + 1)
                        dve.wait_ge(bc_in, u * 32 + 32)
                        dve.tensor_scalar(ohT_lo[:, bass.ds(uk, 1), :, :].rearrange("p a q e -> p (a q) e"),
                                          parts_bc[:, 0, :, :],
                                          c.lane_f[:, 0:1], None, ALU.is_equal).then_inc(ohT_ready, 1)
                        dve.tensor_scalar(ohT_hi[:, bass.ds(uk, 1), :, :].rearrange("p a q e -> p (a q) e"),
                                          parts_bc[0:NT, 1, :, :],
                                          c.lane_f[0:NT, 0:1], None, ALU.is_equal).then_inc(ohT_ready, 1)
                        for x in range(EX):
                            s = u * EX + (x + 1)
                            k = x % 2
                            dve.wait_ge(snap_hi, s)
                            dve.tensor_tensor(snap[:, k, :, NT:2 * NT], run[:, 0:CHAINS * NT].rearrange("p (q t) -> p q t", t=NT),
                                              snap[:, k, :, 0:NT], ALU.subtract).then_inc(snap_lo, 1)
                            dve.wait_ge(found_ready, s + 1)
                            for half in range(2):
                                oh = oh_hi[:, bass.ds(u, 1), x * CHAINS + 4 * half:x * CHAINS + 4 * half + 4, :]
                                oh = oh.rearrange("p a t l -> p (a t) l").unsqueeze(2).to_broadcast([P, 4, 3, NT])
                                dve.tensor_tensor(pick[:, k, 4 * half:4 * half + 4, :, :],
                                                  found[:, half, 0:4 * 3 * NT].rearrange("p (q r t) -> p q r t", r=3, t=NT),
                                                  oh, ALU.mult).then_inc(picked, 1)
                            dve.wait_ge(picked, s * 2 + 2)
                            dve.tensor_reduce(place[:, bass.ds(u, 1), x, :, :].rearrange("p a q r -> p (a q) r"),
                                              pick[:, k, :, :, :].rearrange("p q r t -> p (q r) t"), AX.X, ALU.add).then_inc(reduced, 1)

                @block.tensor
                def _(pe):
                    pe.matmul(run[:, 0:CHAINS * NT], c.ident[:, :], start[:, :, :].rearrange("p q t -> p (q t)"),
                              start=True, stop=True).then_inc(advanced, 1)
                    pe.sem_inc(found_ready, 1)
                    pe.wait_ge(filled, 3)
                    pe.sem_inc(earlier_ready, 1)
                    with pe.Fori(0, EU) as u:
                        uk = u % 2
                        pe.wait_ge(ohT_ready, u * 2 + 5)
                        for x in range(EX):
                            s = u * EX + x
                            k = x % 2
                            pe.wait_ge(earlier_ready, s + 1)
                            for q in range(CHAINS):
                                tl = ohT_lo[:, bass.ds(uk, 1), q, x * P:(x + 1) * P].rearrange("p a e -> p (a e)")
                                th = ohT_hi[:, bass.ds(uk, 1), q, x * P:(x + 1) * P].rearrange("p a e -> p (a e)")
                                pe.matmul(same[:, q, :], tl, tl, start=True, stop=False, skip_group_check=True)
                                pe.matmul(same[:, q, :], th, th, start=False, stop=False, skip_group_check=True)
                                last = pe.matmul(same[:, q, :], c.ident_b[:, :], c.order_bias[:, :], start=False, stop=True, skip_group_check=True)
                            last.then_inc(same_ready, 1)
                            pe.wait_ge(snap_lo, s + 1)
                            for q in range(CHAINS):
                                last = pe.matmul(run[:, q * NT:(q + 1) * NT], oh_lo[:, bass.ds(u, 1), x * CHAINS + q, :].rearrange("p a l -> p (a l)"),
                                                 oh_hi[:, bass.ds(u, 1), x * CHAINS + q, :].rearrange("p a l -> p (a l)"), start=False, stop=True, skip_group_check=True)
                            last.then_inc(advanced, 1)
                            pe.wait_ge(earlier_ready, s + 2)
                            pe.wait_ge(picked, s * 2 + 2)
                            for q in range(CHAINS):
                                out = found[:, q // 4, (q % 4) * 3 * NT:(q % 4 + 1) * 3 * NT]
                                tl = ohT_lo[:, bass.ds(uk, 1), q, x * P:(x + 1) * P].rearrange("p a e -> p (a e)")
                                pe.matmul(out, tl, snap[:, k, q, :], start=True, stop=False, skip_group_check=True)
                                last = pe.matmul(out[:, NT:2 * NT], earlier[:, k, q, :], c.ones_b[:, 0:NT], start=False, stop=True, skip_group_check=True)
                            last.then_inc(found_ready, 1)

        with Mem(nc, f"ixc{g.name}") as d:
            window = d.ps("window", [P, WIN])
            RING = 4
            oh_p = [d.sb(f"oh_p{k}", [P, P], F16) for k in range(RING)]
            oh_c = [d.sb(f"oh_c{k}", [P, WIN], F16) for k in range(RING)]
            lane_e = d.sb("lane_e", [P, ETILES])
            table_i = d.sb("table_i", [P, WIN], I32)
            n_win = d.sb("n_win", [P, 1], I32)
            seq, made, summed, stored = (d.sem(x) for x in ("seq", "made", "summed", "stored"))
            flat = lambda t: t[:, :, :, :].rearrange("p u x q -> p (u x q)")
            max_w = MAX_WIN
            with nc.Block() as block:
                @block.vector
                def _(dve):
                    dve.tensor_tensor(col[:, :, :, :], place[:, :, :, :, 0], place[:, :, :, :, 1], ALU.add).then_inc(seq, 1)
                    dve.tensor_copy(lane_e[:, :].rearrange("p (u x q) -> p u x q", u=EU, x=EX), place[:, :, :, :, 2]).then_inc(seq, 1)
                    dve.tensor_single_scalar(n_win[:, :], g.first_chunk[:, NT:NT + 1], WIN // ROUNDS - 1, ALU.add).then_inc(seq, 1)
                    dve.wait_ge(seq, 3)
                    dve.tensor_single_scalar(n_win[:, :], n_win[:, :], 7, ALU.logical_shift_right).then_inc(seq, 1)
                    dve.wait_ge(seq, 4)
                    dve.sem_inc(g.windows_known, 1)
                    wins = dve.value_load(n_win[0:1, 0:1], min_val=1, max_val=max_w)
                    with dve.Fori(0, wins) as w:
                        dve.wait_ge(seq, w + 4)
                        dve.sem_inc(g.passed, 1)
                        with dve.Fori(0, ETILES // RING) as i:
                            for k in range(RING):
                                n = w * ETILES + i * RING + k
                                col_e = flat(col)[:, bass.ds(i * RING + k, 1)]
                                dve.wait_ge(summed, n + 1)
                                dve.tensor_scalar(oh_p[k][:, :], c.iota_h[:, 0:P], lane_e[:, bass.ds(i * RING + k, 1)], None, ALU.is_equal).then_inc(made, 1)
                                dve.tensor_scalar(oh_c[k][:, :], c.iota_h[:, :], col_e, flat(val_c)[:, bass.ds(i * RING + k, 1)],
                                                  ALU.is_equal, ALU.mult).then_inc(made, 1)
                        dve.wait_ge(summed, w * ETILES + (ETILES + RING))
                        dve.wait_ge(stored, w * 16 + 16)
                        dve.tensor_scalar(table_i[:, :], window[:, :], float(DUMMY), None, ALU.add).then_inc(g.window_ready, 1)
                        dve.tensor_scalar(col[:, :, :, :], col[:, :, :, :], -float(WIN), None, ALU.add).then_inc(seq, 1)

                @block.tensor
                def _(pe):
                    pe.sem_inc(summed, RING)
                    pe.wait_ge(g.windows_known, 1)
                    wins = pe.value_load(n_win[0:1, 0:1], min_val=1, max_val=max_w)
                    pe.sem_inc(g.window_ready, 1)
                    with pe.Fori(0, wins) as w:
                        pe.wait_ge(g.window_ready, w + 1)
                        pe.matmul(window[:, :], zeros[:, 0:P].bitcast(F16), zeros[:, :].bitcast(F16), start=True, stop=True)
                        with pe.Fori(0, ETILES // RING) as i:
                            for k in range(RING):
                                n = w * ETILES + i * RING + k
                                pe.wait_ge(made, n * 2 + 2)
                                pe.matmul(window[:, :], oh_p[k][:, :], oh_c[k][:, :], start=False, stop=True,
                                          skip_group_check=True).then_inc(summed, 1)

                @block.sync
                def _(sp):
                    sp.sem_inc(stored, 16)
                    sp.wait_ge(g.windows_known, 1)
                    wins = sp.value_load(n_win[0:1, 0:1], min_val=1, max_val=max_w)
                    with sp.Fori(0, wins) as w:
                        sp.wait_ge(g.window_ready, w + 2)
                        sp.sem_inc(g.passed, 1)
                        sp.dma_start(g.neighbours[bass.ds(w, 1), :, :].rearrange("a p c -> (a p) c"), table_i[:, :]).then_inc(stored, 16)
                    sp.wait_ge(stored, 16 * wins + 16)
                    sp.sem_inc(g.passed, 1)


D = 256
KC = D // P
GROUP = 5
EPS = 1e-5


def each_tile(eng, body, peel=1):
    with eng.Fori(0, (NT - peel) // 2) as i:
        for s in range(2):
            body(i * 2 + s, s)
    for t in range(NT - peel, NT):
        body(t, t % 2)


def norm_stats(nc, c, name, x, mean, inv):
    with Mem(nc, name) as m:
        stats = m.sb("stats", [P, NT, 6])
        std = m.sb("std", [P, NT])
        stat_done, aggr_done, std_done, inv_done = (m.sem(s) for s in ("stat", "aggr", "std", "inv"))
        with nc.Block() as block:
            @block.vector
            def _(dve):
                with dve.Fori(0, NT) as t:
                    dve.bn_stats(stats[:, bass.ds(t, 1), :].rearrange("p a f -> p (a f)"),
                                 x[:, bass.ds(t, 1), :].rearrange("p a f -> p (a f)")).then_inc(stat_done, 1)
                dve.wait_ge(stat_done, NT)
                for t in range(NT):
                    dve.bn_aggr(mean[:, t, :], stats[:, t, :]).then_inc(aggr_done, 1)
                dve.wait_ge(std_done, 1)
                dve.reciprocal(inv[:, :], std[:, :]).then_inc(inv_done, 1)
                dve.wait_ge(inv_done, 1)

            @block.scalar
            def _(act):
                act.wait_ge(aggr_done, NT)
                act.activation(std[:, :], mean[:, :, 1], ACT.Sqrt, bias=c.eps[:, 0:1]).then_inc(std_done, 1)


def normalise(dve, out, x, mean, inv, t):
    return dve.tensor_scalar(out, x[:, bass.ds(t, 1), :].rearrange("p a f -> p (a f)"),
                             mean[:, bass.ds(t, 1), 0:1].rearrange("p a f -> p (a f)"), inv[:, bass.ds(t, 1)],
                             ALU.subtract, ALU.mult)


def layernorm(nc, c, name, x, out):
    with Mem(nc, name) as m:
        mean, inv = m.sb("mean", [P, NT, 2]), m.sb("inv", [P, NT])
        norm_stats(nc, c, name + "s", x, mean, inv)
        normed = m.sem("normed")
        with nc.Block() as block:
            @block.vector
            def _(dve):
                with dve.Fori(0, NT) as t:
                    normalise(dve, out[:, bass.ds(t, 1), :].rearrange("p a f -> p (a f)"), x, mean, inv, t).then_inc(normed, 1)
                dve.wait_ge(normed, NT)


def project(nc, c, name, weights, bias, n_out, banks, a=None, norm=None, take_act=None, take_dve=None, store=None, n_stores=0, load=None):
    with Mem(nc, name) as m:
        rows = m.sb("rows", [P, 2, D])
        a_t = m.sb("a_t", [P, 2, KC, P])
        turn = m.ps("turn", [P, 2, 512])
        prod = m.ps("prod", [P, 2, banks, 512])
        per = n_out // banks
        loaded = [m.sem(f"loaded{k}") for k in range(NT // GROUP)]
        tiles_in, staged, turned, copied, multiplied, out_dve, out_act, stored = (
            m.sem(s) for s in ("tiles_in", "staged", "turned", "copied", "mult", "out_dve", "out_act", "stored"))

        def stage(eng, t, s):
            eng.wait_ge(turned, t + 1)
            if norm is not None:
                normalise(eng, rows[:, s, :], *norm, t).then_inc(staged, 1)
                return
            if load is not None:
                eng.wait_ge(tiles_in, t + 1)
            eng.activation(rows[:, s, :], a[:, bass.ds(t, 1), :].rearrange("p a f -> p (a f)"), ACT.Copy).then_inc(staged, 1)

        with nc.Block() as block:
            @block.sync
            def _(sp):
                if load is not None:
                    for k in range(NT // GROUP):
                        load(sp, k).then_inc(loaded[k], 16)
                    for k in range(NT // GROUP):
                        sp.wait_ge(loaded[k], 16)
                        sp.sem_inc(tiles_in, GROUP)
                if store is not None:
                    for k in range(NT // GROUP):
                        if take_dve is not None:
                            sp.wait_ge(out_dve, GROUP * (k + 1) + 2)
                        if take_act is not None:
                            sp.wait_ge(out_act, GROUP * (k + 1) + 2)
                        for ins in store(sp, k):
                            ins.then_inc(stored, 16)
                    sp.wait_ge(stored, 16 * (NT // GROUP) * n_stores)

            @block.tensor
            def _(pe):
                pe.sem_inc(multiplied, 2)
                pe.sem_inc(turned, 2)

                def turn_tile(t, s):
                    pe.wait_ge(staged, t + 1)
                    pe.wait_ge(copied, t + 1)
                    for h in range(KC):
                        last = pe.transpose(turn[:, s, h * P:(h + 1) * P], rows[:, s, h * P:(h + 1) * P], c.ident[:, :])
                    last.then_inc(turned, 1)

                def multiply(t, s):
                    pe.wait_ge(copied, t + 3)
                    if take_dve is not None:
                        pe.wait_ge(out_dve, t + 1)
                    if take_act is not None:
                        pe.wait_ge(out_act, t + 1)
                    for b in range(banks):
                        out = prod[:, s, b, 0:per]
                        for h in range(KC):
                            last = pe.matmul(out, a_t[:, s, h, :], weights[:, h, b * per:(b + 1) * per],
                                             start=(h == 0), stop=(bias is None and h == KC - 1))
                        if bias is not None:
                            last = pe.matmul(out, c.ones[0:1, :], bias[0:1, b * per:(b + 1) * per], start=False, stop=True)
                    last.then_inc(multiplied, 1)

                def tile(t, s):
                    if not (isinstance(t, int) and t == NT - 1):
                        turn_tile(t + 1, 1 - s)
                    multiply(t, s)

                turn_tile(0, 0)
                each_tile(pe, tile)

            @block.scalar
            def _(act):
                act.sem_inc(copied, 2)
                act.sem_inc(out_act, 2)

                def tile(t, s):
                    act.wait_ge(turned, t + 3)
                    act.wait_ge(multiplied, t + 1)
                    act.activation(a_t[:, s, :, :].rearrange("p h n -> p (h n)"), turn[:, s, 0:D], ACT.Copy).then_inc(copied, 1)
                    if norm is None and not (isinstance(t, int) and t + 2 >= NT):
                        stage(act, t + 2, s)
                    if take_act is not None:
                        act.wait_ge(multiplied, t + 3)
                        take_act(act, t, prod[:, s, :, :]).then_inc(out_act, 1)

                if norm is None:
                    for t in range(2):
                        stage(act, t, t)
                each_tile(act, tile, peel=3)

            @block.vector
            def _(dve):
                dve.sem_inc(out_dve, 2)

                def tile(t, s):
                    if norm is not None and not (isinstance(t, int) and t + 2 >= NT):
                        stage(dve, t + 2, s)
                    if take_dve is not None:
                        dve.wait_ge(multiplied, t + 3)
                        take_dve(dve, t, prod[:, s, :, :]).then_inc(out_dve, 1)

                if norm is not None:
                    for t in range(2):
                        stage(dve, t, t)
                each_tile(dve, tile, peel=3)


SLOTS = 4


def attend(nc, c, g, name, heads, own_table, table, width, dim_val, out_table, qk, bias_row=None, order=None):
    h, dh = heads, D // heads
    av = dh + 1
    own_w = D if qk else width
    with Mem(nc, name) as m:
        rows = m.sb("rows", [P, SLOTS, ROUNDS, width])
        own = m.sb("own", [P, NT, own_w])
        outs = m.sb("outs", [P, NT, D])
        idx = m.sb("idx", [P, SLOTS, ROUNDS], I32)
        score = m.sb("score", [P, 2, ROUNDS + 1, h])
        wv = m.sb("wv", [P, 2, ROUNDS + 1, h, av])
        acc = m.sb("acc", [P, h, av])
        self_z = m.sb("self_z", [P, 2, h])
        recip = m.sb("recip", [P, 2, h])
        part = m.ps("part", [P, 2, 512])
        prod = m.sb("prod", [P, 2, ROUNDS, D]) if qk else m.sb("prod", [P, 2, ROUNDS, h])
        bias_bc = None if qk else m.sb("bias_bc", [P, D])
        idx_in = [m.sem(f"idx_in{k}") for k in range(SLOTS)]
        gathered = [m.sem(f"gathered{k}") for k in range(SLOTS)]
        (own_in, chunk_ready, multiplied, summed, scored, leaked, maxed, shifted, exped, weighted, rows_free, part_sum,
         rescaled, added, tile_max, tile_acc, normed, nodes_done, scattered, passed, biased, gelued, bias_in, den) = (
            m.sem(s) for s in ("own_in", "chunk_ready", "multiplied", "summed", "scored", "leaked", "maxed", "shifted",
                               "exped", "weighted", "rows_free", "part_sum", "rescaled", "added", "tile_max", "tile_acc",
                               "normed", "nodes_done", "scattered", "passed", "biased", "gelued", "bias_in", "den"))

        def chunks(eng):
            return eng.snap((eng.value_load(g.first_chunk[0:1, NT:NT + 1], min_val=2 * NT, max_val=MAX_CHUNKS - SLOTS) + (SLOTS - 1)) // SLOTS)

        with nc.Block() as block:
            @block.sync
            def _(sp):
                def load_idx(j, k):
                    sp.dma_start(idx[:, k, :], g.neighbours[bass.ds(j // (WIN // ROUNDS), 1), :, bass.ds((j % (WIN // ROUNDS)) * ROUNDS, ROUNDS)]
                                 .rearrange("a p c -> (a p) c")).then_inc(idx_in[k], 16)

                if not qk:
                    sp.dma_start(bias_bc[:, :], bias_row.rearrange("(a n) -> a n", a=1).to_broadcast([P, D])).then_inc(bias_in, 16)
                for k in range(SLOTS):
                    load_idx(k, k)
                blocks = chunks(sp)
                with sp.Fori(1, blocks) as i:
                    for k in range(SLOTS):
                        sp.wait_ge(gathered[k], i * (16 * ROUNDS))
                        sp.sem_inc(chunk_ready, 1)
                        load_idx(i * SLOTS + k, k)
                for k in range(SLOTS):
                    sp.wait_ge(gathered[k], blocks * (16 * ROUNDS))
                    sp.sem_inc(chunk_ready, 1)

            @block.gpsimd
            def _(pool):
                for t in range(NT):
                    pool.indirect_dma_start(out=own[:, t, :], out_offset=None, in_=own_table,
                                            in_offset=bass.IndirectOffsetOnAxis(ap=g.order[:, t:t + 1], axis=0)).then_inc(own_in, 16)
                blocks = chunks(pool)
                with pool.Fori(0, blocks) as i:
                    for k in range(SLOTS):
                        pool.wait_ge(idx_in[k], i * 16 + 16)
                        pool.wait_ge(rows_free, i * SLOTS + (k + 1))
                        pool.sem_inc(passed, 1)
                        for r in range(ROUNDS):
                            pool.indirect_dma_start(out=rows[:, k, r, :], out_offset=None, in_=table,
                                                    in_offset=bass.IndirectOffsetOnAxis(ap=idx[:, k, r:r + 1], axis=0)).then_inc(gathered[k], 16)
                if qk:
                    pool.wait_ge(normed, NT)
                else:
                    pool.wait_ge(gelued, NT // GROUP)
                for t in range(NT):
                    pool.indirect_dma_start(out=out_table, out_offset=bass.IndirectOffsetOnAxis(ap=g.order[:, t:t + 1], axis=0),
                                            in_=outs[:, t, :], in_offset=None).then_inc(scattered, 16)
                pool.wait_ge(scattered, 16 * NT)

            @block.vector
            def _(dve):
                dve.sem_inc(rows_free, SLOTS)
                dve.wait_ge(own_in, 16 * NT)

                def slot2(buf, j):
                    return buf[:, bass.ds(j % 2, 1)]

                def score_chunk(j, t):
                    row = rows[:, bass.ds(j % SLOTS, 1), :, :].rearrange("p a r w -> p (a r) w")
                    s = slot2(score, j).rearrange("p a r h -> p (a r) h")
                    dve.wait_ge(chunk_ready, j + 1)
                    if qk:
                        pr = slot2(prod, j).rearrange("p a r f -> p (a r) f")
                        q = own[:, bass.ds(t, 1), :].to_broadcast([P, ROUNDS, D])
                        dve.tensor_tensor(pr, row[:, :, 0:D], q, ALU.mult).then_inc(multiplied, 1)
                        dve.wait_ge(multiplied, j + 1)
                        dve.tensor_reduce(s[:, 0:ROUNDS, :], pr.rearrange("p r (h d) -> p r h d", d=dh), AX.X, ALU.add).then_inc(summed, 1)
                        dve.wait_ge(summed, j + 1)
                        dve.tensor_tensor(s[:, 0:ROUNDS, :], s[:, 0:ROUNDS, :], row[:, :, 2 * D:2 * D + 1].to_broadcast([P, ROUNDS, h]),
                                          ALU.add).then_inc(scored, 1)
                    else:
                        z = slot2(prod, j).rearrange("p a r f -> p (a r) f")
                        dve.tensor_tensor(z, row[:, :, D:D + h], own[:, bass.ds(t, 1), D + h:D + 2 * h].to_broadcast([P, ROUNDS, h]),
                                          ALU.add).then_inc(summed, 1)
                        dve.wait_ge(summed, j + 1)
                        dve.scalar_tensor_tensor(s[:, 0:ROUNDS, :], z, 0.2, z, ALU.mult, ALU.max).then_inc(scored, 1)
                    dve.wait_ge(scored, j + 1)
                    s_next = slot2(score, j + 1).rearrange("p a r h -> p (a r) h")
                    dve.tensor_reduce(s_next[:, ROUNDS, :], s.rearrange("p r h -> p h r"), AX.X, ALU.max).then_inc(maxed, 1)
                    dve.wait_ge(maxed, j + 1)
                    dve.tensor_tensor(s, s, s_next[:, ROUNDS:ROUNDS + 1, :].to_broadcast([P, ROUNDS + 1, h]), ALU.subtract).then_inc(shifted, 1)

                def weight_chunk(j):
                    row = rows[:, bass.ds(j % SLOTS, 1), :, :].rearrange("p a r w -> p (a r) w")
                    w = slot2(wv, j).rearrange("p a r h f -> p (a r) h f")
                    val = row[:, :, D:2 * D] if qk else row[:, :, 0:D]
                    dve.wait_ge(exped, j + 1)
                    dve.tensor_tensor(w[:, 0:ROUNDS, :, 0:dh], val.rearrange("p r (h d) -> p r h d", d=dh),
                                      w[:, 0:ROUNDS, :, dh:dh + 1].to_broadcast([P, ROUNDS, h, dh]), ALU.mult).then_inc(weighted, 1)
                    dve.wait_ge(weighted, j + 1)
                    dve.sem_inc(rows_free, 1)

                def accumulate(j):
                    w = slot2(wv, j).rearrange("p a r h f -> p (a r) h f")
                    dve.tensor_tensor(acc[:, :, :], acc[:, :, :], w[:, ROUNDS, :, dh:dh + 1].to_broadcast([P, h, av]),
                                      ALU.mult).then_inc(rescaled, 1)
                    dve.wait_ge(rescaled, j + 1)
                    dve.wait_ge(part_sum, j + 1)
                    dve.tensor_tensor(acc[:, :, :].rearrange("p h f -> p (h f)"), acc[:, :, :].rearrange("p h f -> p (h f)"),
                                      part[:, bass.ds(j % 2, 1), 0:h * av].rearrange("p a f -> p (a f)"), ALU.add).then_inc(added, 1)
                    dve.wait_ge(added, j + 1)

                with dve.Fori(0, NT) as t:
                    j0 = dve.value_load(g.first_chunk[0:1, bass.ds(t, 1)], min_val=0, max_val=MAX_CHUNKS - 2)
                    j1 = dve.value_load(g.first_chunk[0:1, bass.ds(t + 1, 1)], min_val=2, max_val=MAX_CHUNKS)
                    s0 = slot2(score, j0).rearrange("p a r h -> p (a r) h")[:, ROUNDS, :]
                    if qk:
                        dve.tensor_scalar(s0, c.zeros[:, 0:h], -1.0e30, None, ALU.add).then_inc(tile_max, 2)
                        dve.memset(acc[:, :, :], 0.0).then_inc(tile_acc, 2)
                    else:
                        own_t = own[:, bass.ds(t, 1), :].rearrange("p a w -> p (a w)")
                        dve.tensor_tensor(self_z[:, 0, :], own_t[:, D:D + h], own_t[:, D + h:D + 2 * h], ALU.add).then_inc(tile_max, 1)
                        dve.wait_ge(tile_max, t * 2 + 1)
                        dve.scalar_tensor_tensor(s0, self_z[:, 0, :], 0.2, self_z[:, 0, :], ALU.mult, ALU.max).then_inc(tile_max, 1)
                        dve.tensor_copy(acc[:, :, 0:dh], own_t[:, 0:D].rearrange("p (h d) -> p h d", d=dh)).then_inc(tile_acc, 1)
                        dve.memset(acc[:, :, dh:av], 1.0).then_inc(tile_acc, 1)
                    dve.wait_ge(tile_max, t * 2 + 2)
                    dve.wait_ge(tile_acc, t * 2 + 2)
                    score_chunk(j0, t)
                    weight_chunk(j0)
                    with dve.Fori(j0 + 1, j1) as j:
                        score_chunk(j, t)
                        accumulate(j - 1)
                        weight_chunk(j)
                    accumulate(j1 - 1)
                    dve.tensor_scalar(recip[:, 0, :], acc[:, :, dh], 1.0e-30, None, ALU.max).then_inc(den, 1)
                    dve.wait_ge(den, t * 2 + 1)
                    dve.reciprocal(recip[:, 1, :], recip[:, 0, :]).then_inc(den, 1)
                    dve.wait_ge(den, t * 2 + 2)
                    dve.tensor_tensor(outs[:, bass.ds(t, 1), :].rearrange("p a (h d) -> p (a h) d", d=dh), acc[:, :, 0:dh],
                                      recip[:, 1, :].unsqueeze(2).to_broadcast([P, h, dh]), ALU.mult).then_inc(normed, 1)
                    dve.wait_ge(normed, t + 1)
                    dve.sem_inc(passed, 1)
                if not qk:
                    dve.wait_ge(normed, NT)
                    dve.wait_ge(bias_in, 16)
                    for k in range(NT // GROUP):
                        part_outs = outs[:, GROUP * k:GROUP * (k + 1), :]
                        dve.tensor_tensor(part_outs, part_outs, bias_bc[:, :].unsqueeze(1).to_broadcast([P, GROUP, D]), ALU.add).then_inc(biased, 1)

            @block.scalar
            def _(act):
                total = act.value_load(g.first_chunk[0:1, NT:NT + 1], min_val=2 * NT, max_val=MAX_CHUNKS)
                with act.Fori(0, total) as j:
                    act.wait_ge(shifted, j + 1)
                    act.activation(wv[:, bass.ds(j % 2, 1), :, :, dh].rearrange("p a r h -> p (a r) h"),
                                   score[:, bass.ds(j % 2, 1), :, :].rearrange("p a r h -> p (a r) h"), ACT.Exp).then_inc(exped, 1)
                if not qk:
                    for k in range(NT // GROUP):
                        act.wait_ge(biased, k + 1)
                        part_outs = outs[:, GROUP * k:GROUP * (k + 1), :]
                        act.activation(part_outs, part_outs, ACT.Gelu).then_inc(gelued, 1)

            @block.tensor
            def _(pe):
                total = pe.value_load(g.first_chunk[0:1, NT:NT + 1], min_val=2 * NT, max_val=MAX_CHUNKS)
                with pe.Fori(0, total) as j:
                    pe.wait_ge(weighted, j + 1)
                    for r in range(ROUNDS):
                        last = pe.matmul(part[:, bass.ds(j % 2, 1), 0:h * av].rearrange("p a f -> p (a f)"), c.ident[:, :],
                                         wv[:, bass.ds(j % 2, 1), r, :, :].rearrange("p a h f -> p (a h f)"),
                                         start=(r == 0), stop=(r == ROUNDS - 1))
                    last.then_inc(part_sum, 1)


def load_weights(nc, name, loads):
    with Mem(nc, name) as m:
        loaded = m.sem("loaded")
        with nc.Block() as block:
            @block.sync
            def _(sp):
                for dst, src in loads:
                    sp.dma_start(dst, src).then_inc(loaded, 16)
                sp.wait_ge(loaded, 16 * len(loads))


def tiles(table, w):
    return table.rearrange("(t p) w -> p t w", p=P)


def table_tiles(k):
    t = GROUP * k
    s = t + (1 if t >= DUMMY // P else 0)
    return slice(s, s + GROUP)


def load_nodes(nc, c, x_in, x):
    full = N_NODES // P
    rest = N_NODES - full * P
    with Mem(nc, "ldx") as m:
        cleared, loaded = m.sem("cleared"), m.sem("loaded")
        with nc.Block() as block:
            @block.vector
            def _(dve):
                dve.memset(x[:, full, :], 0.0).then_inc(cleared, 1)
                dve.memset(c.eps[:, :], EPS).then_inc(cleared, 1)
                dve.wait_ge(cleared, 2)

            @block.sync
            def _(sp):
                sp.dma_start(x[:, 0:full, :], x_in[0:full * P, :].rearrange("(t p) f -> p t f", p=P)).then_inc(loaded, 16)
                sp.wait_ge(cleared, 2)
                sp.dma_start(x[0:rest, full, :], x_in[full * P:N_NODES, :]).then_inc(loaded, 16)
                sp.wait_ge(loaded, 32)


def fill_rows(nc, name, rows, width, low_cols=None):
    with Mem(nc, name) as m:
        fill = m.sb("fill", [P, width])
        filled, stored = m.sem("filled"), m.sem("stored")
        with nc.Block() as block:
            @block.vector
            def _(dve):
                dve.memset(fill[:, :], 0.0).then_inc(filled, 1)
                if low_cols is not None:
                    dve.wait_ge(filled, 1)
                    dve.memset(fill[:, low_cols], -3.0e38).then_inc(filled, 1)

            @block.sync
            def _(sp):
                sp.wait_ge(filled, 1 if low_cols is None else 2)
                n = rows.shape[0] // P
                for t in range(n):
                    sp.dma_start(rows[t * P:(t + 1) * P, :], fill[:, :]).then_inc(stored, 16)
                sp.wait_ge(stored, 16 * n)


NE, HID = 8, 1024
HC = HID // P
A_ROWS = 2 * NPAD
MAX_SLOT_TILES = 57
SLOT_COLS = 60


def top_two(nc, c, name, logits, n_exp, padded, top, idx_f):
    with Mem(nc, name) as m:
        top8, idx8 = m.sb("top8", [P, NT, 8]), m.sb("idx8", [P, NT, 8], mybir.dt.uint32)
        maxed, found, copied = m.sem("maxed"), m.sem("found"), m.sem("copied")
        with nc.Block() as block:
            @block.vector
            def _(dve):
                for t in range(NT):
                    dve.max(top8[:, t, :], logits[:, t, :]).then_inc(maxed, 1)
                dve.wait_ge(maxed, NT)
                for t in range(NT):
                    dve.max_index(idx8[:, t, :], top8[:, t, :], logits[:, t, :]).then_inc(found, 1)
                dve.wait_ge(found, NT)
                dve.tensor_copy(idx_f[:, :, :], idx8[:, :, 0:2]).then_inc(copied, 1)
                dve.tensor_copy(top[:, :, :], top8[:, :, 0:2]).then_inc(copied, 1)
                dve.wait_ge(copied, 2)


def route(nc, c, r, logits):
    with Mem(nc, "rt") as m:
        top, idx_f = m.sb("top", [P, NT, 2]), m.sb("idx_f", [P, NT, 2])
        top_two(nc, c, "rt2", logits, NE, NE, top, idx_f)
        diff, e2, den = m.sb("diff", [P, NT]), m.sb("e2", [P, NT]), m.sb("den", [P, NT])
        chosen = m.sb("chosen", [P, 3, NT, NE])
        node_f = m.sb("node_f", [P, NT])
        counts_ps, before_ps = m.ps("counts", [P, 512]), m.ps("before", [P, 512])
        cum = m.sb("cum", [P, NE, NT + 1])
        last_of = m.sb("last_of", [P, NE + 1])
        n_i, n_f = m.sb("n_i", [P, NE], I32), m.sb("n_f", [P, NE])
        slot_all = m.sb("slot_all", [P, NT, NE])
        pick = m.sb("pick", [P, 2, NT, NE])
        slot_f = m.sb("slot_f", [P, 2, NT])
        sl_i = m.sb("sl_i", [P, 2, 2, NT], I32)
        sl_f = m.sb("sl_f", [P, 2, 2, NT])
        oh_lane, oh_tile = m.sb("oh_lane", [P, 2, P]), m.sb("oh_tile", [P, 2, SLOT_COLS])
        slots_ps = m.ps("slots", [P, SLOT_COLS])
        past = m.sb("past", [P, SLOT_COLS, NE])
        exp_f = m.sb("exp_f", [P, SLOT_COLS])
        chain, ready, expd, summed, made, placed = (m.sem(x) for x in ("chain", "ready", "expd", "summed", "made", "placed"))
        with nc.Block() as block:
            @block.gpsimd
            def _(pool):
                pool.iota(node_f[:, :], pattern=[[P, NT]], base=0, channel_multiplier=1,
                          allow_small_or_imprecise_dtypes=True).then_inc(ready, 1)

            @block.scalar
            def _(act):
                act.wait_ge(ready, 2)
                act.activation(e2[:, :], diff[:, :], ACT.Exp).then_inc(expd, 1)

            @block.vector
            def _(dve):
                n = [0]

                def step(ins):
                    n[0] += 1
                    ins.then_inc(chain, 1)
                    dve.wait_ge(chain, n[0])

                dve.wait_ge(ready, 1)
                dve.tensor_tensor(diff[:, :], top[:, :, 1], top[:, :, 0], ALU.subtract).then_inc(ready, 1)
                for k in range(2):
                    step(dve.tensor_tensor(chosen[:, k, :, :], idx_f[:, :, k:k + 1].to_broadcast([P, NT, NE]),
                                           c.iota_f[:, 0:NE].unsqueeze(1).to_broadcast([P, NT, NE]), ALU.is_equal))
                step(dve.tensor_tensor(chosen[:, 2, :, :], chosen[:, 0, :, :], chosen[:, 1, :, :], ALU.add))
                dve.sem_inc(ready, 1)
                dve.wait_ge(expd, 1)
                step(dve.tensor_scalar(den[:, :], e2[:, :], 1.0, None, ALU.add))
                step(dve.reciprocal(r.weight[:, 0, :], den[:, :]))
                step(dve.tensor_tensor(r.weight[:, 1, :], r.weight[:, 0, :], e2[:, :], ALU.mult))
                dve.wait_ge(summed, 1)
                step(dve.memset(cum[:, :, 0:1], 0.0))
                for e in range(NE):
                    step(dve.tensor_tensor_scan(cum[:, e, 1:NT + 1], c.ones[:, 0:NT],
                                                counts_ps[:, 0:NT * NE].rearrange("p (t e) -> p e t", e=NE)[:, e, :], 0.0, ALU.mult, ALU.add))
                step(dve.tensor_scalar(n_f[:, :], cum[:, :, NT], float(P - 1), float(P), ALU.add, ALU.max))
                step(dve.tensor_copy(n_i[:, :], n_f[:, :]))
                step(dve.tensor_single_scalar(n_i[:, :], n_i[:, :], 7, ALU.logical_shift_right))
                step(dve.tensor_copy(n_f[:, :], n_i[:, :]))
                step(dve.memset(last_of[:, 0:1], 0.0))
                step(dve.tensor_tensor_scan(last_of[:, 1:NE + 1], c.ones[:, 0:NE], n_f[:, :], 0.0, ALU.mult, ALU.add))
                step(dve.tensor_copy(r.first_tile[:, :], last_of[:, :]))
                step(dve.tensor_scalar(n_f[:, :], last_of[:, 0:NE], float(P), None, ALU.mult))
                step(dve.tensor_tensor(slot_all[:, :, :], cum[:, :, 0:NT].rearrange("p e t -> p t e"),
                                       n_f[:, :].unsqueeze(1).to_broadcast([P, NT, NE]), ALU.add))
                step(dve.tensor_tensor(slot_all[:, :, :], slot_all[:, :, :],
                                       before_ps[:, 0:NT * NE].rearrange("p (t e) -> p t e", e=NE), ALU.add))
                for k in range(2):
                    step(dve.tensor_tensor(pick[:, k, :, :], chosen[:, k, :, :], slot_all[:, :, :], ALU.mult))
                    step(dve.tensor_reduce(slot_f[:, k, :], pick[:, k, :, :], AX.X, ALU.add))
                step(dve.tensor_copy(r.slot[:, :, :], slot_f[:, :, :]))
                step(dve.tensor_single_scalar(sl_i[:, :, 0, :], r.slot[:, :, :], P - 1, ALU.bitwise_and))
                step(dve.tensor_single_scalar(sl_i[:, :, 1, :], r.slot[:, :, :], 7, ALU.logical_shift_right))
                step(dve.tensor_copy(sl_f[:, :, :, :], sl_i[:, :, :, :]))
                step(dve.tensor_tensor(past[:, :, :], c.iota_f[:, 0:SLOT_COLS].unsqueeze(2).to_broadcast([P, SLOT_COLS, NE]),
                                       last_of[:, 1:NE + 1].unsqueeze(1).to_broadcast([P, SLOT_COLS, NE]), ALU.is_ge))
                step(dve.tensor_reduce(exp_f[:, :], past[:, :, :], AX.X, ALU.add))
                step(dve.tensor_scalar(exp_f[:, :], exp_f[:, :], float(NE - 1), None, ALU.min))
                step(dve.tensor_copy(r.expert[:, :], exp_f[:, :]))
                with dve.Fori(0, NT) as t:
                    for k in range(2):
                        dve.wait_ge(placed, t * 2 + (k + 1))
                        dve.tensor_scalar(oh_lane[:, k, :], c.iota_f[:, 0:P], sl_f[:, k, 0, bass.ds(t, 1)], None, ALU.is_equal).then_inc(made, 1)
                        dve.tensor_scalar(oh_tile[:, k, :], c.iota_f[:, 0:SLOT_COLS], sl_f[:, k, 1, bass.ds(t, 1)], node_f[:, bass.ds(t, 1)],
                                          ALU.is_equal, ALU.mult).then_inc(made, 1)
                dve.wait_ge(placed, 2 * NT + 2)
                step(dve.tensor_copy(r.node[:, :], slots_ps[:, :]))

            @block.tensor
            def _(pe):
                pe.wait_ge(ready, 3)
                flat = chosen[:, 2, :, :].rearrange("p t e -> p (t e)")
                pe.matmul(counts_ps[:, 0:NT * NE], c.ones[:, :], flat, start=True, stop=True)
                pe.matmul(before_ps[:, 0:NT * NE], c.before[:, :], flat, start=True, stop=True).then_inc(summed, 1)
                pe.matmul(slots_ps[:, :], c.zeros[:, 0:P], c.zeros[:, 0:SLOT_COLS], start=True, stop=True).then_inc(placed, 2)
                with pe.Fori(0, NT) as t:
                    for k in range(2):
                        pe.wait_ge(made, t * 4 + 2 * (k + 1))
                        pe.matmul(slots_ps[:, :], oh_lane[:, k, :], oh_tile[:, k, :], start=False, stop=True,
                                  skip_group_check=True).then_inc(placed, 1)


def experts(nc, c, r, xn_rows, y_rows, w):
    with Mem(nc, "ex") as m:
        w1, w2 = m.sb("w1", [P, 2, KC, HID]), m.sb("w2", [P, 2, HC, D])
        b1, b2 = m.sb("b1", [P, NE, HC]), m.sb("b2", [1, NE, D])
        ln_g, ln_b = m.sb("ln_g", [P, NE, KC]), m.sb("ln_b", [P, NE, KC])
        node_at = m.sb("node_at", [P, 1], I32)
        x_in = m.sb("x_in", [P, D])
        xe = m.sb("xe", [P, KC, P])
        hid = m.sb("hid", [P, HC, P])
        y = m.sb("y", [P, 2, D])
        turn, up, down = m.ps("turn", [P, 512]), m.ps("up", [P, HC // 2, 512]), m.ps("down", [P, 2, 512])
        w_in = [m.sem(f"w_in{k}") for k in range(2)]
        (arrived, node_set, turned, scaled, up_done, act_done, down_done, y_ready, y_stored, bias_in, passed) = (
            m.sem(s) for s in ("arrived", "node_set", "turned", "scaled", "up_done", "act_done", "down_done",
                               "y_ready", "y_stored", "bias_in", "passed"))

        def first_tile(eng, e):
            return eng.value_load(r.first_tile[0:1, bass.ds(e, 1)], min_val=0, max_val=MAX_SLOT_TILES)

        with nc.Block() as block:
            @block.sync
            def _(sp):
                def load_expert(e, k):
                    sp.dma_start(w1[:, k, :, :], w.w1[bass.ds(e, 1), :, :].rearrange("a (k p) n -> p (a k) n", p=P)).then_inc(w_in[k], 16)
                    sp.dma_start(w2[:, k, :, :], w.w2[bass.ds(e, 1), :, :].rearrange("a (k p) n -> p (a k) n", p=P)).then_inc(w_in[k], 16)

                load_expert(0, 0)
                with nc.allow_non_contiguous_dma(reason="per-partition biases, a few thousand numbers"):
                    sp.dma_start(b1[:, :, :], w.b1.rearrange("e (c p) -> p e c", p=P)).then_inc(bias_in, 16)
                    sp.dma_start(ln_g[:, :, :], w.ln_g.rearrange("e (c p) -> p e c", p=P)).then_inc(bias_in, 16)
                    sp.dma_start(ln_b[:, :, :], w.ln_b.rearrange("e (c p) -> p e c", p=P)).then_inc(bias_in, 16)
                sp.dma_start(b2[:, :, :], w.b2.rearrange("(a e) f -> a e f", a=1)).then_inc(bias_in, 16)
                load_expert(1, 1)
                with sp.Fori(1, NE // 2) as i:
                    for k in range(2):
                        sp.wait_ge(down_done, first_tile(sp, i * 2 + k - 1))
                        sp.sem_inc(passed, 1)
                        load_expert(i * 2 + k, k)

            @block.gpsimd
            def _(pool):
                with pool.Fori(0, pool.snap(first_tile(pool, NE) + 1)) as n:
                    pool.wait_ge(turned, n + 1)
                    pool.tensor_copy(node_at[:, :], r.node[:, bass.ds(n, 1)]).then_inc(node_set, 1)
                    pool.wait_ge(node_set, n + 1)
                    pool.sem_inc(passed, 1)
                    pool.indirect_dma_start(out=x_in[:, :], out_offset=None, in_=xn_rows,
                                            in_offset=bass.IndirectOffsetOnAxis(ap=node_at[:, :], axis=0)).then_inc(arrived, 16)

            @block.vector
            def _(dve):
                total = first_tile(dve, NE)
                dve.wait_ge(bias_in, 64)

                def scale(n):
                    e = dve.value_load(r.expert[0:1, bass.ds(n, 1)], min_val=0, max_val=NE - 1)
                    dve.wait_ge(turned, n + 2)
                    for h in range(KC):
                        dve.tensor_scalar(xe[:, h, :], turn[:, h * P:(h + 1) * P],
                                          ln_g[:, bass.ds(e, 1), h], ln_b[:, bass.ds(e, 1), h], ALU.mult, ALU.add).then_inc(scaled, 1)

                dve.sem_inc(y_ready, 2)
                scale(0)
                with dve.Fori(0, total) as n:
                    scale(n + 1)
                    dve.wait_ge(down_done, n + 1)
                    dve.wait_ge(y_stored, n * 16 + 16)
                    dve.tensor_copy(y[:, bass.ds(n % 2, 1), :].rearrange("p a f -> p (a f)"),
                                    down[:, bass.ds(n % 2, 1), 0:D].rearrange("p a f -> p (a f)")).then_inc(y_ready, 1)

            @block.tensor
            def _(pe):
                def turn_tile(n):
                    pe.wait_ge(arrived, n * 16 + 16)
                    for h in range(KC):
                        last = pe.transpose(turn[:, h * P:(h + 1) * P], x_in[:, h * P:(h + 1) * P], c.ident[:, :])
                    last.then_inc(turned, 1)

                pe.sem_inc(turned, 1)
                turn_tile(0)
                pe.wait_ge(bias_in, 64)
                with pe.Fori(0, NE // 2) as i:
                    for k in range(2):
                        e = i * 2 + k
                        pe.wait_ge(w_in[k], i * 32 + 32)
                        pe.sem_inc(passed, 1)
                        with pe.Fori(first_tile(pe, e), first_tile(pe, e + 1)) as n:
                            pe.wait_ge(scaled, n * KC + KC)
                            for q in range(HC):
                                for h in range(KC):
                                    last = pe.matmul(up[:, q // 2, (q % 2) * P:(q % 2 + 1) * P], w1[:, k, h, q * P:(q + 1) * P], xe[:, h, :], start=(h == 0), stop=(h == KC - 1))
                                if q % 2:
                                    last.then_inc(up_done, 1)
                            turn_tile(n + 1)
                            pe.wait_ge(y_ready, n + 1)
                            out = down[:, bass.ds(n % 2, 1), 0:D].rearrange("p a f -> p (a f)")
                            pe.matmul(out, c.ones[0:1, :], b2[0:1, bass.ds(e, 1), :].rearrange("p a f -> p (a f)"), start=True, stop=False)
                            for q in range(HC):
                                pe.wait_ge(act_done, n * HC + (q + 1))
                                last = pe.matmul(out, hid[:, q, :], w2[:, k, q, :], start=False, stop=(q == HC - 1))
                            last.then_inc(down_done, 1)

            @block.scalar
            def _(act):
                total = first_tile(act, NE)
                act.sem_inc(y_stored, 32)
                act.wait_ge(bias_in, 64)
                with act.Fori(0, total) as n:
                    e = act.value_load(r.expert[0:1, bass.ds(n, 1)], min_val=0, max_val=NE - 1)
                    for q in range(HC):
                        if q % 2 == 0:
                            act.wait_ge(up_done, n * (HC // 2) + (q // 2 + 1))
                        act.activation(hid[:, q, :], up[:, q // 2, (q % 2) * P:(q % 2 + 1) * P], ACT.Gelu, bias=b1[:, bass.ds(e, 1), q]).then_inc(act_done, 1)
                    act.wait_ge(y_ready, n + 3)
                    act.wait_ge(y_stored, n * 16 + 32)
                    act.dma_start(y_rows[bass.ds(n, 1), :, :].rearrange("a p f -> (a p) f"),
                                  y[:, bass.ds(n % 2, 1), :].rearrange("p a f -> p (a f)")).then_inc(y_stored, 16)
                act.wait_ge(y_stored, total * 16 + 32)
                act.sem_inc(passed, 1)


def combine(nc, c, r, y_rows, x):
    with Mem(nc, "cb") as m:
        ys = m.sb("ys", [P, 2, NT, D])
        arrived = [m.sem(f"arrived{k}") for k in range(NT // GROUP)]
        added = m.sem("added")
        with nc.Block() as block:
            @block.gpsimd
            def _(pool):
                for t in range(NT):
                    for k in range(2):
                        pool.indirect_dma_start(out=ys[:, k, t, :], out_offset=None, in_=y_rows,
                                                in_offset=bass.IndirectOffsetOnAxis(ap=r.slot[:, k, t:t + 1], axis=0)).then_inc(arrived[t // GROUP], 16)

            @block.vector
            def _(dve):
                for j in range(NT // GROUP):
                    dve.wait_ge(arrived[j], 32 * GROUP)
                    for k in range(2):
                        for t in range(GROUP * j, GROUP * (j + 1)):
                            dve.scalar_tensor_tensor(x[:, t, :], ys[:, k, t, :], r.weight[:, k, t:t + 1], x[:, t, :],
                                                     ALU.mult, ALU.add).then_inc(added, 1)
                        dve.wait_ge(added, GROUP * (2 * j + k + 1))


GH, GC = 4, 64
GW = D + 2 * GH
QH = 8
KVW = 2 * D + 4
E2, SH2, EH1, EH2 = 4, 128, 128, 64


def gat_weights(nc, c, name, w_ext, w_in, a_src, a_dst):
    with Mem(nc, name) as m:
        att = m.sb("att", [P, KC, 2 * GH])
        w_t = m.sb("w_t", [P, KC, KC, P])
        turn, prod = m.ps("turn", [P, KC, KC, P]), m.ps("prod", [P, KC, 2 * GH])
        cleared, loaded, turned, copied, mult, done = (m.sem(s) for s in ("cleared", "loaded", "turned", "copied", "mult", "done"))
        with nc.Block() as block:
            @block.sync
            def _(sp):
                sp.dma_start(w_ext[:, :, 0:D], w_in.rearrange("(k p) n -> p k n", p=P)).then_inc(loaded, 16)
                sp.wait_ge(cleared, 1)
                for k, a in enumerate((a_src, a_dst)):
                    for h in range(GH):
                        sp.dma_start(att[(h % 2) * GC:(h % 2 + 1) * GC, h // 2, k * GH + h:k * GH + h + 1],
                                     a[h, :].rearrange("(c o) -> c o", o=1)).then_inc(loaded, 16)

            @block.vector
            def _(dve):
                dve.memset(att[:, :, :], 0.0).then_inc(cleared, 1)
                dve.wait_ge(turned, 1)
                dve.tensor_copy(w_t[:, :, :, :], turn[:, :, :, :]).then_inc(copied, 1)
                dve.wait_ge(mult, 1)
                dve.tensor_copy(w_ext[:, :, D:GW], prod[:, :, :]).then_inc(done, 1)
                dve.wait_ge(done, 1)

            @block.tensor
            def _(pe):
                pe.wait_ge(loaded, 16 * (1 + 2 * GH))
                for k in range(KC):
                    for f in range(KC):
                        last = pe.transpose(turn[:, f, k, :], w_ext[:, k, f * P:(f + 1) * P], c.ident[:, :])
                last.then_inc(turned, 1)
                pe.wait_ge(copied, 1)
                for k in range(KC):
                    for f in range(KC):
                        last = pe.matmul(prod[:, k, :], w_t[:, f, k, :], att[:, f, :], start=(f == 0), stop=(f == KC - 1))
                last.then_inc(mult, 1)


def gates_to_weights(nc, c, raw, w5):
    with Mem(nc, "gw") as m:
        gates = m.sb("gates", [P, NT, 8])
        peak, total = m.sb("peak", [P, NT]), m.sb("total", [P, NT])
        top, idx_f = m.sb("top", [P, NT, 2]), m.sb("idx_f", [P, NT, 2])
        wt = m.sb("wt", [P, 3, NT])
        chosen = m.sb("chosen", [P, 2, NT, E2])
        chain, ready, expd = m.sem("chain"), m.sem("ready"), m.sem("expd")
        with nc.Block() as block:
            @block.vector
            def _(dve):
                n = [0]

                def step(ins):
                    n[0] += 1
                    ins.then_inc(chain, 1)
                    dve.wait_ge(chain, n[0])

                step(dve.memset(gates[:, :, :], -1.0))
                step(dve.tensor_reduce(peak[:, :], raw[:, :, :], AX.X, ALU.max))
                dve.tensor_tensor(raw[:, :, :], raw[:, :, :], peak[:, :].unsqueeze(2).to_broadcast([P, NT, E2]), ALU.subtract).then_inc(ready, 1)
                dve.wait_ge(expd, 1)
                step(dve.tensor_reduce(total[:, :], gates[:, :, 0:E2], AX.X, ALU.add))
                step(dve.reciprocal(total[:, :], total[:, :]))
                step(dve.tensor_tensor(gates[:, :, 0:E2], gates[:, :, 0:E2], total[:, :].unsqueeze(2).to_broadcast([P, NT, E2]), ALU.mult))

            @block.scalar
            def _(act):
                act.wait_ge(ready, 1)
                act.activation(gates[:, :, 0:E2], raw[:, :, :], ACT.Exp).then_inc(expd, 1)

        top_two(nc, c, "gt2", gates, E2, 8, top, idx_f)
        chain2, ready2, expd2 = m.sem("chain2"), m.sem("ready2"), m.sem("expd2")
        with nc.Block() as block:
            @block.vector
            def _(dve):
                n = [0]

                def step(ins):
                    n[0] += 1
                    ins.then_inc(chain2, 1)
                    dve.wait_ge(chain2, n[0])

                dve.tensor_tensor(wt[:, 0, :], top[:, :, 1], top[:, :, 0], ALU.subtract).then_inc(ready2, 1)
                for k in range(2):
                    step(dve.tensor_tensor(chosen[:, k, :, :], idx_f[:, :, k:k + 1].to_broadcast([P, NT, E2]),
                                           c.iota_f[:, 0:E2].unsqueeze(1).to_broadcast([P, NT, E2]), ALU.is_equal))
                dve.wait_ge(expd2, 1)
                step(dve.tensor_scalar(wt[:, 2, :], wt[:, 1, :], 1.0, None, ALU.add))
                step(dve.reciprocal(wt[:, 0, :], wt[:, 2, :]))
                step(dve.tensor_tensor(wt[:, 1, :], wt[:, 0, :], wt[:, 1, :], ALU.mult))
                for k in range(2):
                    step(dve.tensor_tensor(chosen[:, k, :, :], chosen[:, k, :, :], wt[:, k, :].unsqueeze(2).to_broadcast([P, NT, E2]), ALU.mult))
                step(dve.memset(w5[:, :, E2:E2 + 1], 1.0))
                step(dve.tensor_tensor(w5[:, :, 0:E2], chosen[:, 0, :, :], chosen[:, 1, :, :], ALU.add))

            @block.scalar
            def _(act):
                act.wait_ge(ready2, 1)
                act.activation(wt[:, 1, :], wt[:, 0, :], ACT.Exp).then_inc(expd2, 1)


def shared_and_experts(nc, c, norm, x, w5, w, out):
    with Mem(nc, "f2") as m:
        sw1, sw2, sw3 = m.sb("sw1", [P, KC, D]), m.sb("sw2", [P, KC, SH2]), m.sb("sw3", [P, D])
        ew1, ew2 = m.sb("ew1", [P, E2, KC, EH1]), m.sb("ew2", [P, E2, EH2])
        ew3 = m.sb("ew3", [P, E2 // 2, D])
        bias1 = m.sb("bias1", [P, KC + E2])
        bias2 = m.sb("bias2", [P, 1 + E2 // 2])
        bias3 = m.sb("bias3", [E2 + 1, D])
        pair = m.sb("pair", [E2, E2 // 2, P])
        rows = m.sb("rows", [P, 2, D + E2 + 1])
        x_t = m.sb("x_t", [P, 2, KC, P])
        w_t = m.sb("w_t", [E2 + 1, 2, P])
        h1 = m.sb("h1", [P, 2, KC + E2, P])
        h2 = m.sb("h2", [P, 2, 1 + E2 // 2, P])
        turn = m.ps("turn", [P, 512])
        p1 = m.ps("p1", [P, (KC + E2) // 2, 512])
        p2 = m.ps("p2", [P, 4, P])
        pw = m.ps("pw", [P, 4, P])
        p3 = m.ps("p3", [P, 2, 512])
        loads = m.sem("loads")
        outd = [m.sem(f"outd{k}") for k in range(NT // GROUP)]
        (built, staged, turned, x_copied, w_copied, up1, act1, up2, act2, scaled, down, added) = (
            m.sem(s) for s in ("built", "staged", "turned", "x_copied", "w_copied", "up1", "act1", "up2", "act2", "scaled", "down", "added"))
        with nc.Block() as block:
            @block.sync
            def _(sp):
                with nc.allow_non_contiguous_dma(reason="per-partition biases, about a thousand numbers"):
                    sp.dma_start(sw1[:, :, :], w.sW1.rearrange("(k p) n -> p k n", p=P)).then_inc(loads, 16)
                    sp.dma_start(sw2[:, :, :], w.sW2.rearrange("(k p) n -> p k n", p=P)).then_inc(loads, 16)
                    sp.dma_start(sw3[:, :], w.sW3).then_inc(loads, 16)
                    sp.dma_start(ew2[:, :, :], w.eW2.rearrange("e p n -> p e n")).then_inc(loads, 16)
                    for t in range(2):
                        sp.dma_start(ew3[t * EH2:(t + 1) * EH2, :, :], w.eW3.rearrange("(j t) p n -> t p j n", t=2)[t]).then_inc(loads, 16)
                        sp.dma_start(bias2[t * EH2:(t + 1) * EH2, 1:1 + E2 // 2], w.eb2.rearrange("(j t) p -> t p j", t=2)[t]).then_inc(loads, 16)
                    sp.dma_start(bias1[:, 0:KC], w.sb1.rearrange("(k p) -> p k", p=P)).then_inc(loads, 16)
                    sp.dma_start(bias1[:, KC:KC + E2], w.eb1.rearrange("e p -> p e")).then_inc(loads, 16)
                    sp.dma_start(bias2[:, 0:1], w.sb2.rearrange("(p o) -> p o", o=1)).then_inc(loads, 16)
                    sp.dma_start(bias3[0:E2, :], w.eb3).then_inc(loads, 16)
                    sp.dma_start(bias3[E2:E2 + 1, :], w.sb3.rearrange("(o n) -> o n", o=1)).then_inc(loads, 16)
                    for e in range(E2):
                        sp.dma_start(ew1[:, e, :, :], w.eW1[e].rearrange("(k p) n -> p k n", p=P)).then_inc(loads, 16)
                for k in range(NT // GROUP):
                    sp.wait_ge(added, GROUP * (k + 1) + 2)
                    full = min(GROUP * (k + 1), N_NODES // P)
                    sp.dma_start(out[GROUP * k * P:full * P, :].rearrange("(t p) f -> p t f", p=P), x[:, GROUP * k:full, :]).then_inc(outd[k], 16)
                rest = N_NODES - (N_NODES // P) * P
                sp.dma_start(out[N_NODES - rest:N_NODES, :], x[0:rest, NT - 1, :]).then_inc(outd[0], 16)
                sp.wait_ge(outd[0], 32)
                for k in range(1, NT // GROUP):
                    sp.wait_ge(outd[k], 16)

            @block.gpsimd
            def _(pool):
                pool.memset(pair[:, :, :], 1.0).then_inc(built, 1)
                pool.wait_ge(built, 1)
                pool.affine_select(out=pair[:, :, :], in_=pair[:, :, :], compare_op=ALU.is_ge, fill=0.0, base=0,
                                   pattern=[[P, E2 // 2], [1, P]], channel_multiplier=-EH2).then_inc(built, 1)
                pool.wait_ge(built, 2)
                pool.affine_select(out=pair[:, :, :], in_=pair[:, :, :], compare_op=ALU.is_ge, fill=0.0, base=EH2 - 1,
                                   pattern=[[-P, E2 // 2], [-1, P]], channel_multiplier=EH2).then_inc(built, 1)

            @block.tensor
            def _(pe):
                pe.sem_inc(down, 2)
                pe.wait_ge(built, 3)
                pe.wait_ge(loads, 16 * N_LOADS)

                def tile(t, s):
                    pe.wait_ge(staged, (t + 1) * 2)
                    pe.wait_ge(x_copied, t + 1)
                    pe.wait_ge(w_copied, t + 1)
                    for h in range(KC):
                        pe.transpose(turn[:, h * P:(h + 1) * P], rows[:, s, h * P:(h + 1) * P], c.ident[:, :])
                    pe.wait_ge(scaled, (t + 1) * (E2 // 2))
                    pe.transpose(pw[0:E2 + 1, 3, :], rows[:, s, D:], c.ident[:, :]).then_inc(turned, 1)
                    pe.wait_ge(x_copied, t + 2)
                    pe.wait_ge(act1, (t + 1) * (KC + E2))
                    xt = [x_t[:, s, h, :] for h in range(KC)]
                    for q in range(KC + E2):
                        for h in range(KC):
                            lhs = sw1[:, h, q * P:(q + 1) * P] if q < KC else ew1[:, q - KC, h, :]
                            last = pe.matmul(p1[:, q // 2, (q % 2) * P:(q % 2 + 1) * P], lhs, xt[h], start=(h == 0), stop=(h == KC - 1))
                        if q % 2:
                            last.then_inc(up1, 1)
                    pe.wait_ge(w_copied, t + 2)
                    for j in range(E2 // 2):
                        last = pe.matmul(pw[:, j, :], pair[:, j, :], w_t[0:E2, s, :], start=True, stop=True)
                    hh = lambda q: h1[:, s, q, :]
                    pe.wait_ge(act2, (t + 1) * (1 + E2 // 2))
                    for k in range(KC):
                        pe.wait_ge(act1, (t + 1) * (KC + E2) + (k + 1))
                        last = pe.matmul(p2[:, 0, :], sw2[:, k, :], hh(k), start=(k == 0), stop=(k == KC - 1))
                    for e in range(E2):
                        pe.wait_ge(act1, (t + 1) * (KC + E2) + (KC + e + 1))
                        r0 = (e % 2) * EH2
                        last = pe.matmul(p2[r0:r0 + EH2, 1 + e // 2, :], ew2[:, e, :], hh(KC + e), start=True, stop=True)
                    last.then_inc(up2, 1)
                    o = p3[:, s, 0:D]
                    pe.wait_ge(down, t + 1)
                    pe.wait_ge(added, t + 1)
                    pe.matmul(o, w_t[:, s, :], bias3[:, :], start=True, stop=False)
                    pe.wait_ge(act2, (t + 1) * (1 + E2 // 2) + 1)
                    pe.matmul(o, h2[:, s, 0, :], sw3[:, :], start=False, stop=False)
                    for j in range(E2 // 2):
                        pe.wait_ge(scaled, (t + 1) * (E2 // 2) + (j + 1))
                        last = pe.matmul(o, h2[:, s, 1 + j, :], ew3[:, j, :], start=False, stop=(j == E2 // 2 - 1))
                    last.then_inc(down, 1)

                each_tile(pe, tile)

            @block.scalar
            def _(act):
                act.sem_inc(x_copied, 1)
                act.sem_inc(act1, KC + E2)
                act.sem_inc(act2, 1 + E2 // 2)
                act.wait_ge(loads, 16 * N_LOADS)

                def tile(t, s):
                    act.wait_ge(turned, t + 1)
                    act.activation(x_t[:, s, :, :].rearrange("p k n -> p (k n)"), turn[:, 0:D], ACT.Copy).then_inc(x_copied, 1)
                    for q in range(KC + E2):
                        if q % 2 == 0:
                            act.wait_ge(up1, t * ((KC + E2) // 2) + (q // 2 + 1))
                        act.activation(h1[:, s, q, :], p1[:, q // 2, (q % 2) * P:(q % 2 + 1) * P], ACT.Relu,
                                       bias=bias1[:, q:q + 1]).then_inc(act1, 1)
                    act.wait_ge(up2, t + 1)
                    for j in range(1 + E2 // 2):
                        act.activation(h2[:, s, j, :], p2[:, j, :], ACT.Relu,
                                       bias=bias2[:, j:j + 1]).then_inc(act2, 1)

                each_tile(act, tile)

            @block.vector
            def _(dve):
                dve.sem_inc(w_copied, 1)
                dve.sem_inc(scaled, E2 // 2)
                dve.sem_inc(added, 2)

                def stage(t, s):
                    normalise(dve, rows[:, s, 0:D], *norm, t).then_inc(staged, 1)
                    dve.tensor_copy(rows[:, s, D:], w5[:, bass.ds(t, 1), :].rearrange("p a n -> p (a n)")).then_inc(staged, 1)

                def tile(t, s):
                    dve.wait_ge(turned, t + 1)
                    dve.tensor_copy(w_t[:, s, :], pw[0:E2 + 1, 3, :]).then_inc(w_copied, 1)
                    if not (isinstance(t, int) and t == NT - 1):
                        stage(t + 1, 1 - s)
                    for j in range(E2 // 2):
                        dve.wait_ge(act2, (t + 1) * (1 + E2 // 2) + (j + 2))
                        h = h2[:, s, 1 + j, :]
                        dve.tensor_tensor(h, h, pw[:, j, :], ALU.mult).then_inc(scaled, 1)
                    dve.wait_ge(down, t + 3)
                    xt = x[:, bass.ds(t, 1), :].rearrange("p a f -> p (a f)")
                    dve.tensor_tensor(xt, xt, p3[:, s, 0:D], ALU.add).then_inc(added, 1)

                stage(0, 0)
                each_tile(dve, tile)


N_LOADS = 4 + 4 + 5 + E2


class Names:
    pass


def program(nc, a, out):
    Mem.past.clear()
    dram = lambda name, shape, dt=F32: nc.dram_tensor(name, shape, dt, kind="Internal").ap()
    with Mem(nc, "all") as m:
        c = Names()
        c.lane_f, c.iota_f = m.sb("lane_f", [P, 1]), m.sb("iota_f", [P, WIN])
        c.ident, c.before, c.ones, c.zeros = (m.sb(x, [P, P]) for x in ("ident", "before", "ones", "zeros"))
        c.order_bias, c.ones_b, c.ident_b, c.iota_b = (m.sb(x, [P, P], BF16) for x in ("order_bias", "ones_b", "ident_b", "iota_b"))
        c.iota_h = m.sb("iota_h", [P, WIN], F16)
        c.minus1, c.eps = m.sb("minus1", [P, 1]), m.sb("eps", [P, 1])
        build_constants(nc, c)

        graphs = []
        for name, key, val in (("s", a.src, a.dst), ("d", a.dst, a.src)):
            g = Names()
            g.name = name
            g.order, g.first_chunk = m.sb(f"order_{name}", [P, NT], I32), m.sb(f"first_chunk_{name}", [P, NT + 1], I32)
            g.key_parts, g.sort_keys = dram(f"key_parts_{name}", (2, EROWS * ROWE), BF16), dram(f"sort_keys_{name}", (NPAD,))
            g.neighbours = dram(f"neighbours_{name}", (MAX_WIN, P, WIN), I32)
            g.hist_done, g.windows_known, g.window_ready, g.passed = (
                m.sem(f"{x}_{name}") for x in ("hist_done", "windows_known", "window_ready", "passed"))
            build_neighbour_table(nc, c, g, key, val)
            graphs.append(g)

        x = m.sb("x", [P, NT, D])
        load_nodes(nc, c, a.x, x)

        q_rows, kv_rows, att_rows = dram("q_rows", (TABLE_ROWS, D)), dram("kv_rows", (TABLE_ROWS, KVW)), dram("attended_rows", (TABLE_ROWS, D))
        project_qkv(nc, c, a, x, q_rows, kv_rows)
        with Mem(nc, "at") as p:
            fill_rows(nc, "fdk", kv_rows[DUMMY:DUMMY + P, :], KVW, slice(2 * D, 2 * D + 1))
            fill_rows(nc, "fdq", q_rows[DUMMY:DUMMY + P, :], D)
            attend(nc, c, graphs[0], "att", QH, q_rows, kv_rows, KVW, None, att_rows, True)
        with Mem(nc, "wo") as p:
            att, wt, bias = p.sb("att", [P, NT, D]), p.sb("w", [P, KC, D]), p.sb("bias", [1, D])
            load_weights(nc, "wol", [(wt[:, :, :], a.Wo.rearrange("(k p) n -> p k n", p=P)), (bias[:, :], a.bo.rearrange("(o n) -> o n", o=1))])
            add_product(nc, c, "wop", att, att_rows, wt, bias, x)

        xn_rows, y_rows = dram("xn_rows", (NPAD, D)), dram("y_rows", (MAX_SLOT_TILES + 1, P, D))
        r = Names()
        r.weight, r.slot = m.sb("r_weight", [P, 2, NT]), m.sb("r_slot", [P, 2, NT], I32)
        r.node, r.expert, r.first_tile = m.sb("r_node", [P, SLOT_COLS], I32), m.sb("r_expert", [P, SLOT_COLS], I32), m.sb("r_first_tile", [P, NE + 1], I32)
        with Mem(nc, "ro") as p:
            xt, xn, wr, br = p.sb("xt", [P, NT, D]), p.sb("xn", [P, NT, D]), p.sb("wr", [P, KC, NE]), p.sb("br", [1, NE])
            logits = p.sb("logits", [P, NT, NE])
            load_weights(nc, "rol", [(wr[:, :, :], a.Wr.rearrange("(k p) n -> p k n", p=P)), (br[:, :], a.br.rearrange("(o n) -> o n", o=1))])
            layernorm(nc, c, "ln1", x, xt)
            layernorm(nc, c, "ln1i", xt, xn)
            project(nc, c, "rop", wr, br, NE, 1, a=xt,
                    take_dve=lambda dve, t, prod: dve.tensor_copy(logits[:, bass.ds(t, 1), :], prod[:, :, 0:NE]),
                    store=lambda sp, k: [sp.dma_start(xn_rows[GROUP * k * P:GROUP * (k + 1) * P, :].rearrange("(t p) f -> p t f", p=P),
                                                      xn[:, GROUP * k:GROUP * (k + 1), :])], n_stores=1)
            route(nc, c, r, logits)
        w = Names()
        w.w1, w.w2, w.b1, w.b2, w.ln_g, w.ln_b = a.W1, a.W2, a.b1, a.b2, a.ln_g, a.ln_b
        fill_rows(nc, "fdy", y_rows.rearrange("t p f -> (t p) f")[A_ROWS:(MAX_SLOT_TILES + 1) * P, :], D)
        experts(nc, c, r, xn_rows, y_rows, w)
        combine(nc, c, r, y_rows.rearrange("t p f -> (t p) f"), x)

        h_rows = [dram(f"h_rows{i}", (TABLE_ROWS, GW)) for i in range(2)]
        g_rows = [dram(f"g_rows{i}", (TABLE_ROWS, D)) for i in range(2)]
        for i, (w_in, a_src, a_dst, b) in enumerate(((a.gW0, a.a_src0, a.a_dst0, a.gb0), (a.gW1, a.a_src1, a.a_dst1, a.gb1))):
            with Mem(nc, f"gat{i}") as p:
                wt, h_in, h_out = p.sb("w", [P, KC, GW]), p.sb("h_in", [P, NT, D]), p.sb("h_out", [P, NT, GW])
                gat_weights(nc, c, f"gaw{i}", wt, w_in, a_src, a_dst)
                fill_rows(nc, f"fdg{i}", h_rows[i][DUMMY:DUMMY + P, :], GW, slice(D, D + GH))
                mean, inv = p.sb("mean", [P, NT, 2]), p.sb("inv", [P, NT])
                if i == 0:
                    norm_stats(nc, c, "ln2", x, mean, inv)
                project(nc, c, f"gap{i}", wt, None, GW, 1, a=h_in, norm=(x, mean, inv) if i == 0 else None,
                        take_dve=lambda dve, t, prod: dve.tensor_copy(h_out[:, bass.ds(t, 1), :], prod[:, :, 0:GW]),
                        store=lambda sp, k: [sp.dma_start(tiles(h_rows[i], GW)[:, table_tiles(k), :], h_out[:, GROUP * k:GROUP * (k + 1), :])], n_stores=1,
                        load=None if i == 0 else (lambda sp, k: sp.dma_start(h_in[:, GROUP * k:GROUP * (k + 1), :], tiles(g_rows[0], D)[:, table_tiles(k), :])))
            attend(nc, c, graphs[1], f"gt{i}", GH, h_rows[i], h_rows[i], GW, None, g_rows[i], False, bias_row=b)

        with Mem(nc, "last") as p:
            mean, inv = p.sb("mean", [P, NT, 2]), p.sb("inv", [P, NT])
            gw, gb = p.sb("gw", [P, KC, E2]), p.sb("gb", [1, E2])
            raw, w5 = p.sb("raw", [P, NT, E2]), p.sb("w5", [P, NT, E2 + 1])
            load_weights(nc, "lal", [(gw[:, :, :], a.gW.rearrange("(k p) n -> p k n", p=P)), (gb[:, :], a.gb.rearrange("(o n) -> o n", o=1))])
            add_rows(nc, c, "addg", x, g_rows[1])
            norm_stats(nc, c, "ln3", x, mean, inv)
            project(nc, c, "gap", gw, gb, E2, 1, norm=(x, mean, inv),
                    take_dve=lambda dve, t, prod: dve.tensor_copy(raw[:, bass.ds(t, 1), :], prod[:, :, 0:E2]))
            gates_to_weights(nc, c, raw, w5)
            shared_and_experts(nc, c, (x, mean, inv), x, w5, a, out)


def project_qkv(nc, c, a, x, q_rows, kv_rows):
    with Mem(nc, "qkv") as p:
        mean, inv = p.sb("mean", [P, NT, 2]), p.sb("inv", [P, NT])
        wt, bias = p.sb("w", [P, KC, 3 * D]), p.sb("bias", [1, 3 * D])
        q_all, kv_all = p.sb("q_all", [P, NT, D]), p.sb("kv_all", [P, NT, KVW])
        load_weights(nc, "qkvl", [(wt[:, :, i * D:(i + 1) * D], w.rearrange("(k p) n -> p k n", p=P)) for i, w in enumerate((a.Wq, a.Wk, a.Wv))]
                     + [(bias[:, i * D:(i + 1) * D], b.rearrange("(o n) -> o n", o=1)) for i, b in enumerate((a.bq, a.bk, a.bv))])
        norm_stats(nc, c, "ln0", x, mean, inv)
        cleared = p.sem("cleared")
        with nc.Block() as block:
            @block.vector
            def _(dve):
                dve.memset(kv_all[:, :, 2 * D:KVW], 0.0).then_inc(cleared, 1)
                dve.wait_ge(cleared, 1)
        half = 3 * D // 2
        q_scale = float((D // QH) ** -0.5)

        def take_act(act, t, prod):
            return act.activation(kv_all[:, bass.ds(t, 1), half - D:2 * D].rearrange("p a n -> p (a n)"), prod[:, 1, 0:half], ACT.Copy)

        def take_dve(dve, t, prod):
            dve.tensor_scalar(q_all[:, bass.ds(t, 1), :].rearrange("p a n -> p (a n)"), prod[:, 0, 0:D], q_scale, None, ALU.mult)
            return dve.tensor_copy(kv_all[:, bass.ds(t, 1), 0:half - D].rearrange("p a n -> p (a n)"), prod[:, 0, D:half])

        project(nc, c, "qkp", wt, bias, 3 * D, 2, norm=(x, mean, inv), take_act=take_act, take_dve=take_dve,
                store=lambda sp, k: [sp.dma_start(tiles(q_rows, D)[:, table_tiles(k), :], q_all[:, GROUP * k:GROUP * (k + 1), :]),
                                     sp.dma_start(tiles(kv_rows, KVW)[:, table_tiles(k), :], kv_all[:, GROUP * k:GROUP * (k + 1), :])], n_stores=2)


def add_product(nc, c, name, att, att_rows, wt, bias, x):
    def take_dve(dve, t, prod):
        xt = x[:, bass.ds(t, 1), :].rearrange("p a n -> p (a n)")
        return dve.tensor_tensor(xt, xt, prod[:, 0, 0:D], ALU.add)

    project(nc, c, name, wt, bias, D, 1, a=att, take_dve=take_dve,
            load=lambda sp, k: sp.dma_start(att[:, GROUP * k:GROUP * (k + 1), :], tiles(att_rows, D)[:, table_tiles(k), :]))


def add_rows(nc, c, name, x, rows):
    with Mem(nc, name) as m:
        buf = m.sb("buf", [P, NT, D])
        loaded = [m.sem(f"loaded{k}") for k in range(NT // GROUP)]
        added = m.sem("added")
        with nc.Block() as block:
            @block.sync
            def _(sp):
                for k in range(NT // GROUP):
                    sp.dma_start(buf[:, GROUP * k:GROUP * (k + 1), :], tiles(rows, D)[:, table_tiles(k), :]).then_inc(loaded[k], 16)

            @block.vector
            def _(dve):
                for k in range(NT // GROUP):
                    dve.wait_ge(loaded[k], 16)
                    part = x[:, GROUP * k:GROUP * (k + 1), :]
                    dve.tensor_tensor(part, part, buf[:, GROUP * k:GROUP * (k + 1), :], ALU.add).then_inc(added, 1)
                dve.wait_ge(added, NT // GROUP)


ARRAYS = {
    "x": "x", "src": "src", "dst": "dst",
    "Wq": "L0_gnn_Wq", "bq": "L0_gnn_bq", "Wk": "L0_gnn_Wk", "bk": "L0_gnn_bk", "Wv": "L0_gnn_Wv", "bv": "L0_gnn_bv",
    "Wo": "L0_gnn_Wo", "bo": "L0_gnn_bo",
    "Wr": "L0_ffn_Wr", "br": "L0_ffn_br", "ln_g": "L0_ffn_ln_g", "ln_b": "L0_ffn_ln_b",
    "W1": "L0_ffn_W1", "b1": "L0_ffn_b1", "W2": "L0_ffn_W2", "b2": "L0_ffn_b2",
    "gW0": "L1_gnn_W0", "a_src0": "L1_gnn_a_src0", "a_dst0": "L1_gnn_a_dst0", "gb0": "L1_gnn_b0",
    "gW1": "L1_gnn_W1", "a_src1": "L1_gnn_a_src1", "a_dst1": "L1_gnn_a_dst1", "gb1": "L1_gnn_b1",
    "sW1": "L1_ffn_sW1", "sb1": "L1_ffn_sb1", "sW2": "L1_ffn_sW2", "sb2": "L1_ffn_sb2", "sW3": "L1_ffn_sW3", "sb3": "L1_ffn_sb3",
    "eW1": "L1_ffn_eW1", "eb1": "L1_ffn_eb1", "eW2": "L1_ffn_eW2", "eb2": "L1_ffn_eb2", "eW3": "L1_ffn_eW3", "eb3": "L1_ffn_eb3",
    "gW": "L1_ffn_gW", "gb": "L1_ffn_gb",
}


def head_major(v, axis):
    v = np.moveaxis(v, axis, -1)
    v = v.reshape(v.shape[:-1] + (D // QH, QH)).swapaxes(-1, -2).reshape(v.shape)
    return np.ascontiguousarray(np.moveaxis(v, -1, axis))


def kernel(**inputs):
    import concourse.bacc as bacc
    from concourse.bass_utils import run_bass_kernel_spmd

    nc = bacc.Bacc("TRN2", target_bir_lowering=False, num_devices=1)
    arrays, a = {}, Names()
    for name, full in ARRAYS.items():
        v = np.ascontiguousarray(inputs[full])
        if name in ("Wq", "Wk", "Wv", "bq", "bk", "bv"):
            v = head_major(v, v.ndim - 1)
        if name == "Wo":
            v = head_major(v, 0)
        arrays[f"in_{name}"] = v
        vars(a)[name] = nc.dram_tensor(f"in_{name}", v.shape, mybir.dt.from_np(v.dtype), kind="ExternalInput").ap()
    out = nc.dram_tensor("out", (N_NODES, D), F32, kind="ExternalOutput").ap()
    program(nc, a, out)
    r = run_bass_kernel_spmd(nc, [arrays], core_ids=[0])
    return r.results[0]["out"]
```

```python
import concourse.bass as bass
from concourse import mybir
from contextlib import ExitStack
import numpy as np

F32, BF16, F16, I32 = mybir.dt.float32, mybir.dt.bfloat16, mybir.dt.float16, mybir.dt.int32
ALU, ACT, AX = mybir.AluOpType, mybir.ActivationFunctionType, mybir.AxisListType

P = 128
N_NODES, N_EDGES = 3125, 53125
NT = -(-N_NODES // P)
NPAD = NT * P
DUMMY = 15 * P
TABLE_ROWS = NPAD + P
ROUNDS = 4
ROWE = 512
EROWS = -(-N_EDGES // ROWE)
EX = ROWE // P
CHAINS = 8
EU = EROWS // CHAINS
ETILES = EROWS * EX
WIN = 512
MAX_CHUNKS = (N_EDGES + 3 * NT + 4 * NT) // ROUNDS + 1
MAX_WIN = -(-MAX_CHUNKS * ROUNDS // WIN)
MAX_CHUNKS = MAX_WIN * WIN // ROUNDS
KEY_PAD = 4095
RMAX = bass.bass_isa.ReduceOp.max


def table_row(t):
    return (t + (1 if t >= DUMMY // P else 0)) * P


MANY_SEMS = 100


class Mem:

    past = []

    def __init__(self, nc, name):
        self.nc, self.name, self.stack, self.sems = nc, name, ExitStack(), []

    def __enter__(self):
        self.stack.__enter__()
        return self

    def __exit__(self, *a):
        self.past.extend(self.sems)
        if len(self.past) > MANY_SEMS:
            self.nc.clear_and_free_semaphores(self.past)
            self.nc.all_engine_barrier()
            self.past.clear()
        return self.stack.__exit__(*a)

    def sb(self, name, shape, dt=F32):
        return self.stack.enter_context(self.nc.sbuf_tensor(f"{self.name}_{name}", shape, dt))

    def ps(self, name, shape, dt=F32):
        return self.stack.enter_context(self.nc.psum_tensor(f"{self.name}_{name}", shape, dt))

    def sem(self, name):
        self.sems.append(self.nc.alloc_semaphore(name=f"{self.name}_{name}"))
        return self.sems[-1]


def build_constants(nc, c):
    with Mem(nc, "cst") as m:
        made, seen = m.sem("made"), m.sem("seen")
        with nc.Block() as block:
            @block.gpsimd
            def _(pool):
                pool.iota(c.lane_f[:, :], pattern=[[0, 1]], base=0, channel_multiplier=1,
                          allow_small_or_imprecise_dtypes=True).then_inc(made, 1)
                pool.iota(c.iota_f[:, :], pattern=[[1, WIN]], base=0, channel_multiplier=0,
                          allow_small_or_imprecise_dtypes=True).then_inc(made, 1)
                pool.memset(c.ident[:, :], 0.0).then_inc(made, 1)
                pool.memset(c.order_bias[:, :], 0.0).then_inc(made, 1)
                pool.memset(c.ones[:, :], 1.0).then_inc(made, 1)
                pool.memset(c.ones_b[:, :], 1.0).then_inc(made, 1)
                pool.memset(c.before[:, :], 1.0).then_inc(made, 1)
                pool.memset(c.zeros[:, :], 0.0).then_inc(made, 1)
                pool.wait_ge(made, 8)
                pool.affine_select(out=c.ident[:, :], in_=c.ident[:, :], compare_op=ALU.not_equal, fill=1.0,
                                   base=0, pattern=[[-1, P]], channel_multiplier=1).then_inc(made, 1)
                pool.affine_select(out=c.order_bias[:, :], in_=c.order_bias[:, :], compare_op=ALU.is_gt, fill=-2.0,
                                   base=0, pattern=[[1, P]], channel_multiplier=-1).then_inc(made, 1)
                pool.affine_select(out=c.before[:, :], in_=c.before[:, :], compare_op=ALU.is_gt, fill=0.0,
                                   base=0, pattern=[[1, P]], channel_multiplier=-1).then_inc(made, 1)

            @block.vector
            def _(dve):
                dve.wait_ge(made, 11)
                dve.tensor_copy(c.ident_b[:, :], c.ident[:, :]).then_inc(seen, 1)
                dve.tensor_copy(c.iota_b[:, :], c.iota_f[:, 0:P]).then_inc(seen, 1)
                dve.tensor_copy(c.iota_h[:, :], c.iota_f[:, :]).then_inc(seen, 1)


def build_neighbour_table(nc, c, g, key_in, val_in):
    with Mem(nc, f"ix{g.name}") as m:
        lo_c = m.sb("lo_c", [P, EU, EX, CHAINS], BF16)
        hi_c = m.sb("hi_c", [P, EU, EX, CHAINS], BF16)
        val_c = m.sb("val_c", [P, EU, EX, CHAINS])
        oh_lo = m.sb("oh_lo", [P, EU, EX * CHAINS, P], BF16)
        oh_hi = m.sb("oh_hi", [P, EU, EX * CHAINS, NT], BF16)
        zeros = m.sb("zeros", [P, WIN], BF16)
        place = m.sb("place", [P, EU, EX, CHAINS, 3])
        col = m.sb("col", [P, EU, EX, CHAINS])
        start = m.sb("start", [P, CHAINS, NT])
        lane_of = m.sb("lane_of", [P, NT])

        edges_in, parts, split, turned, evacuated = (m.sem(x) for x in ("edges_in", "parts", "split", "turned", "evac"))
        ohs, counted, padded = m.sem("ohs"), m.sem("counted"), m.sem("padded")

        full = EROWS - 1
        rest = N_EDGES - full * ROWE
        with Mem(nc, f"ixa{g.name}") as a:
            turn = [a.ps(f"turn{k}", [P, EX, P]) for k in range(3)]
            hist = a.ps("hist", [P, 512])
            with Mem(nc, f"ixr{g.name}") as r:
                key_i, val_i = r.sb("key_i", [EROWS, ROWE], I32), r.sb("val_i", [EROWS, ROWE], I32)
                lo_i, hi_i = r.sb("lo_i", [EROWS, ROWE], I32), r.sb("hi_i", [EROWS, ROWE], I32)
                part_f = r.sb("part_f", [EROWS, 3, ROWE])
                part_b = r.sb("part_b", [EROWS, 2, ROWE], BF16)
                above = r.sb("above", [EROWS, ROWE])
                with nc.Block() as block:
                    @block.sync
                    def _(sp):
                        sp.wait_ge(padded, 2)
                        for src, dst in ((key_in, key_i), (val_in, val_i)):
                            sp.dma_start(dst[0:full, :], src[0:full * ROWE].rearrange("(p e) -> p e", e=ROWE)).then_inc(edges_in, 16)
                            sp.dma_start(dst[full:EROWS, 0:rest], src[full * ROWE:N_EDGES].rearrange("(p e) -> p e", p=1)).then_inc(edges_in, 16)
                        sp.wait_ge(split, 1)
                        sp.dma_start(g.key_parts.rearrange("h (p e) -> p h e", e=ROWE), part_b[:, :, :]).then_inc(parts, 16)
                        sp.wait_ge(parts, 16)

                    @block.vector
                    def _(dve):
                        dve.memset(key_i[:, :], KEY_PAD).then_inc(padded, 1)
                        dve.memset(val_i[:, :], 0).then_inc(padded, 1)
                        dve.memset(zeros[:, :], 0.0).then_inc(padded, 1)
                        dve.wait_ge(edges_in, 64)
                        dve.tensor_single_scalar(lo_i[:, :], key_i[:, :], P - 1, ALU.bitwise_and).then_inc(counted, 1)
                        dve.tensor_single_scalar(hi_i[:, :], key_i[:, :], 7, ALU.logical_shift_right).then_inc(counted, 1)
                        dve.tensor_scalar(above[:, :], val_i[:, :], float(DUMMY), float(P), ALU.is_ge, ALU.mult).then_inc(counted, 1)
                        dve.wait_ge(counted, 3)
                        dve.tensor_copy(part_f[:, 0, :], lo_i[:, :]).then_inc(counted, 1)
                        dve.tensor_copy(part_f[:, 1, :], hi_i[:, :]).then_inc(counted, 1)
                        dve.scalar_tensor_tensor(part_f[:, 2, :], above[:, :], -float(DUMMY), val_i[:, :],
                                                 ALU.add, ALU.add).then_inc(counted, 1)
                        dve.wait_ge(counted, 6)
                        dve.scalar_tensor_tensor(part_f[:, 2, :], key_i[:, :], float(NPAD), part_f[:, 2, :],
                                                 ALU.is_lt, ALU.mult).then_inc(counted, 1)
                        dve.tensor_copy(part_b[:, :, :], part_f[:, 0:2, :]).then_inc(split, 1)
                        dve.wait_ge(turned, 1)
                        for k, out in enumerate((lo_c, hi_c, val_c)):
                            for x in range(EX):
                                dve.tensor_copy(out[:, :, x, :],
                                                turn[k][:, x, 0:EROWS].rearrange("p (q u) -> p u q", u=EU)).then_inc(evacuated, 1)
                        dve.wait_ge(evacuated, 3 * EX)
                        with dve.Fori(0, EU) as u:
                            dve.tensor_tensor(oh_lo[:, bass.ds(u, 1), :, :].rearrange("p a t l -> p (a t) l"),
                                              lo_c[:, bass.ds(u, 1), :, :].rearrange("p a x q -> p (a x q)").unsqueeze(2).to_broadcast([P, EX * CHAINS, P]),
                                              c.iota_b[:, :].unsqueeze(1).to_broadcast([P, EX * CHAINS, P]),
                                              ALU.is_equal).then_inc(ohs, 1)
                            dve.tensor_tensor(oh_hi[:, bass.ds(u, 1), :, :].rearrange("p a t l -> p (a t) l"),
                                              hi_c[:, bass.ds(u, 1), :, :].rearrange("p a x q -> p (a x q)").unsqueeze(2).to_broadcast([P, EX * CHAINS, NT]),
                                              c.iota_b[:, 0:NT].unsqueeze(1).to_broadcast([P, EX * CHAINS, NT]),
                                              ALU.is_equal).then_inc(ohs, 1)

                    @block.tensor
                    def _(pe):
                        pe.wait_ge(counted, 7)
                        for k in range(3):
                            for x in range(EX):
                                last = pe.transpose(turn[k][:, x, 0:EROWS], part_f[:, k, x * P:(x + 1) * P], c.ident[0:EROWS, 0:EROWS])
                        last.then_inc(turned, 1)
                        pe.wait_ge(padded, 3)
                        pe.matmul(hist[:, 0:CHAINS * NT], zeros[:, 0:P], zeros[:, 0:CHAINS * NT], start=True, stop=True)
                        with pe.Fori(0, EU) as u:
                            pe.wait_ge(ohs, u * 2 + 2)
                            for t in range(EX * CHAINS):
                                q = t % CHAINS
                                last = pe.matmul(hist[:, q * NT:(q + 1) * NT],
                                                 oh_lo[:, bass.ds(u, 1), t, :].rearrange("p a l -> p (a l)"),
                                                 oh_hi[:, bass.ds(u, 1), t, :].rearrange("p a l -> p (a l)"),
                                                 start=False, stop=True, skip_group_check=True)
                            last.then_inc(g.hist_done, 1)

            counts = a.sb("counts", [P, CHAINS, NT])
            deg = a.sb("deg", [P, NT])
            skey = a.sb("skey", [P, NT])
            keys_bc = a.sb("keys_bc", [P, NPAD])
            junk = [a.sb(f"junk{k}", [P, NPAD], BF16) for k in range(2)]
            above_v, sign_v = a.sb("above_v", [P, NT]), a.sb("sign_v", [P, NT])
            nskey = a.sb("nskey", [P, NT])
            node_f = a.sb("node_f", [P, NT])
            rank_i = a.sb("rank_i", [P, 3, NT], I32)
            rank_f = a.sb("rank_f", [P, 3, NT])
            oh_lane = a.sb("oh_lane", [P, NT, P])
            oh_tile = a.sb("oh_tile", [P, NT, NT])
            oh_val = a.sb("oh_val", [P, NT, 2, NT])
            sorted_ps = a.ps("sorted", [P, 2 * NT])
            sdeg, mdeg = a.sb("sdeg", [P, NT]), a.sb("mdeg", [P, NT])
            ch_i, ch_f = a.sb("ch_i", [P, NT], I32), a.sb("ch_f", [P, NT])
            cum = a.sb("cum", [P, NT + 1])
            pick = a.sb("pick", [P, NT, NT])
            base_of = a.sb("base_of", [P, NT])
            above_n = a.sb("above_n", [P, NT])
            CPL = MAX_CHUNKS // P
            chunk_f, tile_f, tile_i = a.sb("chunk_f", [P, CPL]), a.sb("tile_f", [P, CPL]), a.sb("tile_i", [P, CPL], I32)
            tile_past = a.sb("tile_past", [P, CPL, NT])
            tiled = a.sem("tiled")
            n_dve = NT // 2 + 1
            chain, keyed, key_out, key_bc, signs, ranked, sums, maxed = (
                a.sem(x) for x in ("chain", "keyed", "key_out", "key_bc", "signs", "ranked", "sums", "maxed"))
            with nc.Block() as block:
                @block.gpsimd
                def _(pool):
                    pool.iota(node_f[:, :], pattern=[[P, NT]], base=0, channel_multiplier=1,
                              allow_small_or_imprecise_dtypes=True).then_inc(keyed, 1)
                    pool.iota(chunk_f[:, :], pattern=[[1, CPL]], base=0, channel_multiplier=CPL,
                              allow_small_or_imprecise_dtypes=True).then_inc(keyed, 1)
                    pool.wait_ge(maxed, 1)
                    pool.partition_all_reduce(mdeg[:, :], sdeg[:, :], P, RMAX).then_inc(maxed, 1)

                @block.vector
                def _(dve):
                    n = [0]

                    def step(ins):
                        n[0] += 1
                        ins.then_inc(chain, 1)
                        dve.wait_ge(chain, n[0])

                    dve.wait_ge(g.hist_done, EU)
                    step(dve.tensor_copy(counts[:, :, :], hist[:, 0:CHAINS * NT].rearrange("p (q t) -> p q t", t=NT)))
                    step(dve.tensor_reduce(deg[:, :], counts[:, :, :].rearrange("p q t -> p t q"), AX.X, ALU.add))
                    dve.wait_ge(keyed, 2)
                    step(dve.tensor_scalar(skey[:, :], deg[:, :], 4000.0, 4096.0, ALU.min, ALU.mult))
                    step(dve.tensor_tensor(skey[:, :], skey[:, :], node_f[:, :], ALU.add))
                    dve.tensor_scalar(nskey[:, :], skey[:, :], -1.0, None, ALU.mult).then_inc(keyed, 1)
                    step(dve.memset(start[:, 0, :], 0.0))
                    for q in range(1, CHAINS):
                        step(dve.tensor_tensor(start[:, q, :], start[:, q - 1, :], counts[:, q - 1, :], ALU.add))
                    dve.wait_ge(key_bc, 16)
                    for t in range(n_dve):
                        if t >= 2:
                            dve.wait_ge(ranked, t - 1)
                        dve.tensor_scalar(junk[0][:, :], keys_bc[:, :], skey[:, t:t + 1], 0.0, ALU.is_gt, ALU.add,
                                          accum_out=above_v[:, t:t + 1]).then_inc(ranked, 1)
                        dve.wait_ge(ranked, t + 1)
                    dve.wait_ge(signs, NT - n_dve)
                    step(dve.tensor_scalar(above_v[:, n_dve:NT], sign_v[:, n_dve:NT], float(NPAD - 1), 0.5, ALU.add, ALU.mult))
                    step(dve.tensor_copy(rank_i[:, 0, :], above_v[:, :]))
                    step(dve.tensor_single_scalar(rank_i[:, 1, :], rank_i[:, 0, :], P - 1, ALU.bitwise_and))
                    step(dve.tensor_single_scalar(rank_i[:, 2, :], rank_i[:, 0, :], 7, ALU.logical_shift_right))
                    step(dve.tensor_copy(rank_f[:, :, :], rank_i[:, :, :]))
                    step(dve.tensor_copy(lane_of[:, :], rank_f[:, 1, :]))
                    step(dve.tensor_tensor(oh_lane[:, :, :], rank_f[:, 1, :].unsqueeze(2).to_broadcast([P, NT, P]),
                                           c.iota_f[:, 0:P].unsqueeze(1).to_broadcast([P, NT, P]), ALU.is_equal))
                    step(dve.tensor_tensor(oh_tile[:, :, :], rank_f[:, 2, :].unsqueeze(2).to_broadcast([P, NT, NT]),
                                           c.iota_f[:, 0:NT].unsqueeze(1).to_broadcast([P, NT, NT]), ALU.is_equal))
                    step(dve.tensor_scalar(above_n[:, :], node_f[:, :], float(DUMMY), float(P), ALU.is_ge, ALU.mult))
                    step(dve.tensor_tensor(above_n[:, :], above_n[:, :], node_f[:, :], ALU.add))
                    step(dve.tensor_tensor(oh_val[:, :, 0, :], oh_tile[:, :, :],
                                           above_n[:, :].unsqueeze(2).to_broadcast([P, NT, NT]), ALU.mult))
                    step(dve.tensor_tensor(oh_val[:, :, 1, :], oh_tile[:, :, :],
                                           deg[:, :].unsqueeze(2).to_broadcast([P, NT, NT]), ALU.mult))
                    dve.sem_inc(ranked, 1)
                    dve.wait_ge(sums, 1)
                    step(dve.tensor_copy(g.order[:, :], sorted_ps[:, 0:NT]))
                    dve.tensor_copy(sdeg[:, :], sorted_ps[:, NT:2 * NT]).then_inc(maxed, 1)
                    dve.wait_ge(maxed, 2)
                    step(dve.tensor_scalar(ch_f[:, :], mdeg[:, :], float(ROUNDS - 1), float(ROUNDS), ALU.add, ALU.max))
                    step(dve.tensor_copy(ch_i[:, :], ch_f[:, :]))
                    step(dve.tensor_single_scalar(ch_i[:, :], ch_i[:, :], 2, ALU.logical_shift_right))
                    step(dve.tensor_copy(ch_f[:, :], ch_i[:, :]))
                    step(dve.memset(cum[:, 0:1], 0.0))
                    step(dve.tensor_tensor_scan(cum[:, 1:NT + 1], c.ones[:, 0:NT], ch_f[:, :], 0.0, ALU.mult, ALU.add))
                    step(dve.tensor_copy(g.first_chunk[:, :], cum[:, :]))
                    step(dve.tensor_tensor(tile_past[:, :, :], chunk_f[:, :].unsqueeze(2).to_broadcast([P, CPL, NT]),
                                           cum[:, 1:NT + 1].unsqueeze(1).to_broadcast([P, CPL, NT]), ALU.is_ge))
                    step(dve.tensor_reduce(tile_f[:, :], tile_past[:, :, :], AX.X, ALU.add))
                    step(dve.tensor_scalar(tile_f[:, :], tile_f[:, :], float(NT - 1), None, ALU.min))
                    dve.tensor_copy(tile_i[:, :], tile_f[:, :]).then_inc(tiled, 1)
                    step(dve.tensor_scalar(cum[:, :], cum[:, :], float(ROUNDS), None, ALU.mult))
                    step(dve.tensor_tensor(pick[:, :, :], oh_tile[:, :, :],
                                           cum[:, 0:NT].unsqueeze(1).to_broadcast([P, NT, NT]), ALU.mult))
                    step(dve.tensor_reduce(base_of[:, :], pick[:, :, :], AX.X, ALU.add))
                    step(dve.tensor_tensor(start[:, :, :], start[:, :, :],
                                           base_of[:, :].unsqueeze(1).to_broadcast([P, CHAINS, NT]), ALU.add))

                @block.sync
                def _(sp):
                    sp.wait_ge(keyed, 3)
                    sp.dma_start(g.sort_keys.rearrange("(p t) -> p t", t=NT), skey[:, :]).then_inc(key_out, 16)
                    sp.wait_ge(key_out, 16)
                    sp.dma_start(keys_bc[:, :], g.sort_keys.rearrange("(a n) -> a n", a=1).to_broadcast([P, NPAD])).then_inc(key_bc, 16)
                    sp.wait_ge(tiled, 1)
                    sp.dma_start(g.tile_of.rearrange("(p n) -> p n", p=P), tile_i[:, :]).then_inc(key_out, 16)
                    sp.wait_ge(key_out, 32)

                @block.scalar
                def _(act):
                    act.wait_ge(keyed, 3)
                    act.wait_ge(key_bc, 16)
                    for k, t in enumerate(range(n_dve, NT)):
                        act.activation(junk[1][:, :], keys_bc[:, :], ACT.Sign, bias=nskey[:, t:t + 1],
                                       accum_out=sign_v[:, t:t + 1]).then_inc(signs, 1)
                        act.wait_ge(signs, k + 1)

                @block.tensor
                def _(pe):
                    pe.wait_ge(ranked, n_dve + 1)
                    for t in range(NT):
                        last = pe.matmul(sorted_ps[:, :], oh_lane[:, t, :], oh_val[:, t, :, :].rearrange("p a b -> p (a b)"),
                                         start=(t == 0), stop=(t == NT - 1))
                    last.then_inc(sums, 1)

        with Mem(nc, f"ixb{g.name}") as b:
            run = b.ps("run", [P, 512])
            same = b.ps("same", [P, CHAINS, P])
            found = b.ps("found", [P, 2, 2, 512])
            parts_bc = b.sb("parts_bc", [P, 2, CHAINS, ROWE], BF16)
            ohT_lo = b.sb("ohT_lo", [P, 2, CHAINS, ROWE], BF16)
            ohT_hi = b.sb("ohT_hi", [NT, 2, CHAINS, ROWE], BF16)
            snap = b.sb("snap", [P, 2, CHAINS, 3 * NT], BF16)
            earlier = b.sb("earlier", [P, 2, CHAINS, P], BF16)
            pick = b.sb("pick", [P, 2, CHAINS, 3, NT])
            bc_in = b.sem("bc_in")
            (begun, ohT_ready, snap_hi, snap_lo, same_ready, earlier_ready, found_ready,
             picked, reduced, advanced, filled) = (
                b.sem(x) for x in ("begun", "ohT_ready", "snap_hi", "snap_lo", "same_ready",
                                   "earlier_ready", "found_ready", "picked", "reduced", "advanced", "filled"))
            kp = g.key_parts.rearrange("h (q u e) -> h q u e", q=CHAINS, e=ROWE)
            last_u = EU - 1

            def row_loop(eng, row):
                row(0, True)
                with eng.Fori(1, EU) as u:
                    row(u, False)

            with nc.Block() as block:
                @block.sync
                def _(sp):
                    def load_row(r):
                        for h in range(2):
                            sp.dma_start(parts_bc[:, h, :, :],
                                         kp[h, :, bass.ds(r % EU, 1), :].rearrange("q a e -> (q a) e").unsqueeze(0).to_broadcast([P, CHAINS, ROWE])).then_inc(bc_in, 16)

                    load_row(0)
                    with sp.Fori(1, EU + 1) as r:
                        sp.wait_ge(ohT_ready, r * 2)
                        sp.sem_inc(g.passed, 1)
                        load_row(r)

                @block.scalar
                def _(act):
                    act.wait_ge(begun, 1)
                    act.sem_inc(earlier_ready, 1)
                    with act.Fori(0, EU) as u:
                        for x in range(EX):
                            s = u * EX + (x + 1)
                            k = x % 2
                            act.wait_ge(advanced, s)
                            act.activation(snap[:, k, :, 0:NT], run[:, 0:CHAINS * NT].rearrange("p (q t) -> p q t", t=NT),
                                           ACT.Copy).then_inc(snap_hi, 1)
                            act.wait_ge(same_ready, s)
                            act.activation(earlier[:, k, :, :], same[:, :, :], ACT.Relu, bias=c.minus1[:, 0:1]).then_inc(earlier_ready, 1)

                @block.vector
                def _(dve):
                    dve.memset(c.minus1[:, :], -1.0).then_inc(filled, 1)
                    for k in range(2):
                        dve.tensor_copy(snap[:, k, :, 2 * NT:3 * NT],
                                        lane_of[:, :].unsqueeze(1).to_broadcast([P, CHAINS, NT])).then_inc(filled, 1)
                    dve.wait_ge(filled, 3)
                    dve.sem_inc(begun, 1)
                    dve.sem_inc(picked, 6)

                    def low_one_hots(r, rk):
                        dve.wait_ge(bc_in, r * 32 + 32)
                        dve.tensor_scalar(ohT_lo[:, bass.ds(rk, 1), :, :].rearrange("p a q e -> p (a q) e"),
                                          parts_bc[:, 0, :, :], c.lane_f[:, 0:1], None, ALU.is_equal).then_inc(ohT_ready, 1)

                    def high_one_hots(r, rk):
                        dve.tensor_scalar(ohT_hi[:, bass.ds(rk, 1), :, :].rearrange("p a q e -> p (a q) e"),
                                          parts_bc[0:NT, 1, :, :], c.lane_f[0:NT, 0:1], None, ALU.is_equal).then_inc(ohT_ready, 1)

                    def pick_places(u, x, n):
                        k = x % 2
                        dve.wait_ge(found_ready, n)
                        for half in range(2):
                            oh = oh_hi[:, bass.ds(u, 1), x * CHAINS + 4 * half:x * CHAINS + 4 * half + 4, :]
                            oh = oh.rearrange("p a t l -> p (a t) l").unsqueeze(2).to_broadcast([P, 4, 3, NT])
                            dve.tensor_tensor(pick[:, k, 4 * half:4 * half + 4, :, :],
                                              found[:, k, half, 0:4 * 3 * NT].rearrange("p (q r t) -> p q r t", r=3, t=NT),
                                              oh, ALU.mult).then_inc(picked, 1)
                        dve.wait_ge(picked, n * 2 + 2)
                        dve.tensor_reduce(place[:, bass.ds(u, 1), x, :, :].rearrange("p a q r -> p (a q) r"),
                                          pick[:, k, :, :, :].rearrange("p q r t -> p (q r) t"), AX.X, ALU.add).then_inc(reduced, 1)

                    def row(u, first):
                        for x in range(EX):
                            s = u * EX + (x + 1)
                            k = x % 2
                            dve.wait_ge(snap_hi, s)
                            dve.tensor_tensor(snap[:, k, :, NT:2 * NT], run[:, 0:CHAINS * NT].rearrange("p (q t) -> p q t", t=NT),
                                              snap[:, k, :, 0:NT], ALU.subtract).then_inc(snap_lo, 1)
                            if x >= 2:
                                pick_places(u, x - 2, s)
                            elif not first:
                                pick_places(u - 1, x + 2, s)
                            if x == 1:
                                if first:
                                    dve.wait_ge(found_ready, 2)
                                low_one_hots(u + 1, (u + 1) % 2)
                            if x == 2:
                                high_one_hots(u + 1, (u + 1) % 2)

                    low_one_hots(0, 0)
                    high_one_hots(0, 0)
                    row_loop(dve, row)
                    for x in (2, 3):
                        pick_places(last_u, x, EU * EX + x - 1)

                @block.tensor
                def _(pe):
                    def mark_same(uk, x, n):
                        pe.wait_ge(earlier_ready, n)
                        for q in range(CHAINS):
                            tl = ohT_lo[:, bass.ds(uk, 1), q, x * P:(x + 1) * P].rearrange("p a e -> p (a e)")
                            th = ohT_hi[:, bass.ds(uk, 1), q, x * P:(x + 1) * P].rearrange("p a e -> p (a e)")
                            pe.matmul(same[:, q, :], tl, tl, start=True, stop=False, skip_group_check=True)
                            pe.matmul(same[:, q, :], th, th, start=False, stop=False, skip_group_check=True)
                            last = pe.matmul(same[:, q, :], c.ident_b[:, :], c.order_bias[:, :], start=False, stop=True, skip_group_check=True)
                        last.then_inc(same_ready, 1)

                    def find(uk, x, n):
                        k = x % 2
                        pe.wait_ge(picked, n * 2)
                        for q in range(CHAINS):
                            out = found[:, k, q // 4, (q % 4) * 3 * NT:(q % 4 + 1) * 3 * NT]
                            tl = ohT_lo[:, bass.ds(uk, 1), q, x * P:(x + 1) * P].rearrange("p a e -> p (a e)")
                            pe.matmul(out, tl, snap[:, k, q, :], start=True, stop=False, skip_group_check=True)
                            last = pe.matmul(out[:, NT:2 * NT], earlier[:, k, q, :], c.ones_b[:, 0:NT], start=False, stop=True, skip_group_check=True)
                        last.then_inc(found_ready, 1)

                    def advance(u, x, n):
                        pe.wait_ge(snap_lo, n)
                        for q in range(CHAINS):
                            last = pe.matmul(run[:, q * NT:(q + 1) * NT], oh_lo[:, bass.ds(u, 1), x * CHAINS + q, :].rearrange("p a l -> p (a l)"),
                                             oh_hi[:, bass.ds(u, 1), x * CHAINS + q, :].rearrange("p a l -> p (a l)"), start=False, stop=True, skip_group_check=True)
                        last.then_inc(advanced, 1)

                    def row(u, first):
                        for x in range(EX):
                            n = u * EX + (x + 1)
                            if x == 0:
                                pe.wait_ge(ohT_ready, u * 2 + 2)
                            mark_same(u % 2, x, n)
                            if x > 0:
                                pe.wait_ge(earlier_ready, n)
                                find(u % 2, x - 1, n)
                            elif not first:
                                find((u + 1) % 2, EX - 1, n)
                            advance(u, x, n)

                    pe.matmul(run[:, 0:CHAINS * NT], c.ident[:, :], start[:, :, :].rearrange("p q t -> p (q t)"),
                              start=True, stop=True).then_inc(advanced, 1)
                    pe.wait_ge(filled, 3)
                    pe.sem_inc(found_ready, 2)
                    row_loop(pe, row)
                    pe.wait_ge(earlier_ready, EU * EX + 1)
                    find(last_u % 2, EX - 1, EU * EX + 1)

        with Mem(nc, f"ixc{g.name}") as d:
            window = d.ps("window", [P, WIN])
            RING = 4
            BATCH = 16
            oh_p, off_p = d.sb("oh_p", [P, 2, BATCH, P], F16), d.sb("off_p", [P, 2, BATCH, P], F16)
            oh_c = [d.sb(f"oh_c{k}", [P, WIN], F16) for k in range(RING)]
            lane_e = d.sb("lane_e", [P, ETILES], F16)
            table_i = d.sb("table_i", [P, WIN], I32)
            n_win = d.sb("n_win", [P, 1], I32)
            seq, made, apart, squared, laned, summed, stored = (
                d.sem(x) for x in ("seq", "made", "apart", "squared", "laned", "summed", "stored"))
            flat = lambda t: t[:, :, :, :].rearrange("p u x q -> p (u x q)")
            max_w = MAX_WIN
            with nc.Block() as block:
                @block.vector
                def _(dve):
                    dve.tensor_tensor(col[:, :, :, :], place[:, :, :, :, 0], place[:, :, :, :, 1], ALU.add).then_inc(seq, 1)
                    dve.tensor_copy(lane_e[:, :].rearrange("p (u x q) -> p u x q", u=EU, x=EX), place[:, :, :, :, 2]).then_inc(seq, 1)
                    dve.tensor_single_scalar(n_win[:, :], g.first_chunk[:, NT:NT + 1], WIN // ROUNDS - 1, ALU.add).then_inc(seq, 1)
                    dve.wait_ge(seq, 3)
                    dve.tensor_single_scalar(n_win[:, :], n_win[:, :], 7, ALU.logical_shift_right).then_inc(seq, 1)
                    dve.wait_ge(seq, 4)
                    dve.sem_inc(g.windows_known, 1)
                    wins = dve.value_load(n_win[0:1, 0:1], min_val=1, max_val=max_w)
                    with dve.Fori(0, wins) as w:
                        dve.wait_ge(seq, w + 4)
                        dve.sem_inc(g.passed, 1)
                        with dve.Fori(0, ETILES // RING) as i:
                            for k in range(RING):
                                n = w * ETILES + i * RING + k
                                col_e = flat(col)[:, bass.ds(i * RING + k, 1)]
                                dve.wait_ge(summed, n + (BATCH + 2 - RING))
                                dve.tensor_scalar(oh_c[k][:, :], c.iota_h[:, :], col_e, flat(val_c)[:, bass.ds(i * RING + k, 1)],
                                                  ALU.is_equal, ALU.mult).then_inc(made, 1)
                        dve.wait_ge(summed, w * ETILES + (ETILES + BATCH + 1))
                        dve.wait_ge(stored, w * 16 + 16)
                        dve.tensor_scalar(table_i[:, :], window[:, :], float(DUMMY), None, ALU.add).then_inc(g.window_ready, 1)
                        dve.tensor_scalar(col[:, :, :, :], col[:, :, :, :], -float(WIN), None, ALU.add).then_inc(seq, 1)

                @block.tensor
                def _(pe):
                    pe.sem_inc(summed, BATCH + 1)
                    pe.wait_ge(g.windows_known, 1)
                    wins = pe.value_load(n_win[0:1, 0:1], min_val=1, max_val=max_w)
                    pe.sem_inc(g.window_ready, 1)
                    with pe.Fori(0, wins) as w:
                        pe.wait_ge(g.window_ready, w + 1)
                        pe.matmul(window[:, :], zeros[:, 0:P].bitcast(F16), zeros[:, :].bitcast(F16), start=True, stop=True)
                        with pe.Fori(0, ETILES // BATCH // 2) as i:
                            for b in range(2):
                                pe.wait_ge(laned, w * (ETILES // BATCH) + i * 2 + (b + 1))
                                pe.sem_inc(g.passed, 1)
                                for k in range(BATCH):
                                    n = w * ETILES + (i * 2 + b) * BATCH + k
                                    pe.wait_ge(made, n + 1)
                                    pe.matmul(window[:, :], oh_p[:, b, k, :], oh_c[k % RING][:, :], start=False, stop=True,
                                              skip_group_check=True).then_inc(summed, 1)

                @block.gpsimd
                def _(pool):
                    pool.wait_ge(g.windows_known, 1)
                    wins = pool.value_load(n_win[0:1, 0:1], min_val=1, max_val=max_w)
                    with pool.Fori(0, wins) as w:
                        with pool.Fori(0, ETILES // BATCH // 2) as i:
                            for b in range(2):
                                n = w * ETILES + (i * 2 + b) * BATCH
                                pool.wait_ge(summed, n + 1)
                                pool.sem_inc(g.passed, 1)
                                pool.tensor_tensor(off_p[:, b, :, :], lane_e[:, bass.ds((i * 2 + b) * BATCH, BATCH)].unsqueeze(2).to_broadcast([P, BATCH, P]),
                                                   c.iota_h[:, 0:P].unsqueeze(1).to_broadcast([P, BATCH, P]), ALU.subtract).then_inc(apart, 1)

                @block.scalar
                def _(act):
                    act.wait_ge(g.windows_known, 1)
                    wins = act.value_load(n_win[0:1, 0:1], min_val=1, max_val=max_w)
                    with act.Fori(0, wins) as w:
                        with act.Fori(0, ETILES // BATCH // 2) as i:
                            for b in range(2):
                                m = w * (ETILES // BATCH) + i * 2 + (b + 1)
                                act.wait_ge(apart, m)
                                act.activation(off_p[:, b, :, :], off_p[:, b, :, :], ACT.Square).then_inc(squared, 1)
                                act.wait_ge(squared, m)
                                act.activation(oh_p[:, b, :, :], off_p[:, b, :, :], ACT.Relu, scale=-1.0, bias=c.ones[:, 0:1]).then_inc(laned, 1)

                @block.sync
                def _(sp):
                    sp.sem_inc(stored, 16)
                    sp.wait_ge(g.windows_known, 1)
                    wins = sp.value_load(n_win[0:1, 0:1], min_val=1, max_val=max_w)
                    with sp.Fori(0, wins) as w:
                        sp.wait_ge(g.window_ready, w + 2)
                        sp.sem_inc(g.passed, 1)
                        sp.dma_start(g.neighbours[bass.ds(w, 1), :, :].rearrange("a p c -> (a p) c"), table_i[:, :]).then_inc(stored, 16)
                    sp.wait_ge(stored, 16 * wins + 16)
                    sp.sem_inc(g.passed, 1)


D = 256
KC = D // P
GROUP = 5
EPS = 1e-5


def each_tile(eng, body, peel=1):
    with eng.Fori(0, (NT - peel) // 2) as i:
        for s in range(2):
            body(i * 2 + s, s)
    for t in range(NT - peel, NT):
        body(t, t % 2)


def norm_stats(nc, c, name, x, mean, inv):
    with Mem(nc, name) as m:
        stats = m.sb("stats", [P, NT, 6])
        std = m.sb("std", [P, NT])
        stat_done, aggr_done, std_done, inv_done = (m.sem(s) for s in ("stat", "aggr", "std", "inv"))
        with nc.Block() as block:
            @block.vector
            def _(dve):
                for t in range(NT):
                    dve.bn_stats(stats[:, t, :], x[:, t, :]).then_inc(stat_done, 1)
                dve.wait_ge(stat_done, NT)
                for t in range(NT):
                    dve.bn_aggr(mean[:, t, :], stats[:, t, :]).then_inc(aggr_done, 1)
                dve.wait_ge(std_done, 1)
                dve.reciprocal(inv[:, :], std[:, :]).then_inc(inv_done, 1)
                dve.wait_ge(inv_done, 1)

            @block.scalar
            def _(act):
                act.wait_ge(aggr_done, NT)
                act.activation(std[:, :], mean[:, :, 1], ACT.Sqrt, bias=c.eps[:, 0:1]).then_inc(std_done, 1)


def normalise(dve, out, x, mean, inv, t):
    if isinstance(t, int):
        return dve.tensor_scalar(out, x[:, t, :], mean[:, t, 0:1], inv[:, t:t + 1], ALU.subtract, ALU.mult)
    return dve.tensor_scalar(out, x[:, bass.ds(t, 1), :].rearrange("p a f -> p (a f)"),
                             mean[:, bass.ds(t, 1), 0:1].rearrange("p a f -> p (a f)"), inv[:, bass.ds(t, 1)],
                             ALU.subtract, ALU.mult)


def layernorm(nc, c, name, x, out):
    with Mem(nc, name) as m:
        mean, inv = m.sb("mean", [P, NT, 2]), m.sb("inv", [P, NT])
        norm_stats(nc, c, name + "s", x, mean, inv)
        normed = m.sem("normed")
        with nc.Block() as block:
            @block.vector
            def _(dve):
                for t in range(NT):
                    normalise(dve, out[:, t, :], x, mean, inv, t).then_inc(normed, 1)
                dve.wait_ge(normed, NT)


def project(nc, c, name, weights, bias, n_out, banks, a=None, norm=None, take_act=None, take_dve=None, store=None, n_stores=0, load=None):
    with Mem(nc, name) as m:
        rows = m.sb("rows", [P, 2, D])
        a_t = m.sb("a_t", [P, 2, KC, P])
        turn = m.ps("turn", [P, 2, 512])
        prod = m.ps("prod", [P, 2, banks, 512])
        per = n_out // banks
        loaded = [m.sem(f"loaded{k}") for k in range(NT // GROUP)]
        tiles_in, staged, turned, copied, multiplied, out_dve, out_act, stored = (
            m.sem(s) for s in ("tiles_in", "staged", "turned", "copied", "mult", "out_dve", "out_act", "stored"))

        def stage(eng, t, s):
            eng.wait_ge(turned, t + 1)
            if norm is not None:
                normalise(eng, rows[:, s, :], *norm, t).then_inc(staged, 1)
                return
            if load is not None:
                eng.wait_ge(tiles_in, t + 1)
            eng.activation(rows[:, s, :], a[:, bass.ds(t, 1), :].rearrange("p a f -> p (a f)"), ACT.Copy).then_inc(staged, 1)

        with nc.Block() as block:
            @block.sync
            def _(sp):
                if load is not None:
                    for k in range(NT // GROUP):
                        load(sp, k).then_inc(loaded[k], 16)
                    for k in range(NT // GROUP):
                        sp.wait_ge(loaded[k], 16)
                        sp.sem_inc(tiles_in, GROUP)
                if store is not None:
                    for k in range(NT // GROUP):
                        if take_dve is not None:
                            sp.wait_ge(out_dve, GROUP * (k + 1) + 2)
                        if take_act is not None:
                            sp.wait_ge(out_act, GROUP * (k + 1) + 2)
                        for ins in store(sp, k):
                            ins.then_inc(stored, 16)
                    sp.wait_ge(stored, 16 * (NT // GROUP) * n_stores)

            @block.tensor
            def _(pe):
                pe.sem_inc(multiplied, 2)
                pe.sem_inc(turned, 2)

                def turn_tile(t, s):
                    pe.wait_ge(staged, t + 1)
                    pe.wait_ge(copied, t + 1)
                    for h in range(KC):
                        last = pe.transpose(turn[:, s, h * P:(h + 1) * P], rows[:, s, h * P:(h + 1) * P], c.ident[:, :])
                    last.then_inc(turned, 1)

                def multiply(t, s):
                    pe.wait_ge(copied, t + 3)
                    if take_dve is not None:
                        pe.wait_ge(out_dve, t + 1)
                    if take_act is not None:
                        pe.wait_ge(out_act, t + 1)
                    for b in range(banks):
                        out = prod[:, s, b, 0:per]
                        for h in range(KC):
                            last = pe.matmul(out, a_t[:, s, h, :], weights[:, h, b * per:(b + 1) * per],
                                             start=(h == 0), stop=(bias is None and h == KC - 1))
                        if bias is not None:
                            last = pe.matmul(out, c.ones[0:1, :], bias[0:1, b * per:(b + 1) * per], start=False, stop=True)
                    last.then_inc(multiplied, 1)

                def tile(t, s):
                    if not (isinstance(t, int) and t == NT - 1):
                        turn_tile(t + 1, 1 - s)
                    multiply(t, s)

                turn_tile(0, 0)
                each_tile(pe, tile)

            @block.scalar
            def _(act):
                act.sem_inc(copied, 2)
                act.sem_inc(out_act, 2)

                def tile(t, s):
                    act.wait_ge(turned, t + 3)
                    act.wait_ge(multiplied, t + 1)
                    act.activation(a_t[:, s, :, :].rearrange("p h n -> p (h n)"), turn[:, s, 0:D], ACT.Copy).then_inc(copied, 1)
                    if norm is None and not (isinstance(t, int) and t + 2 >= NT):
                        stage(act, t + 2, s)
                    if take_act is not None:
                        act.wait_ge(multiplied, t + 3)
                        take_act(act, t, prod[:, s, :, :]).then_inc(out_act, 1)

                if norm is None:
                    for t in range(2):
                        stage(act, t, t)
                each_tile(act, tile, peel=3)

            @block.vector
            def _(dve):
                dve.sem_inc(out_dve, 2)

                def tile(t, s):
                    if norm is not None and not (isinstance(t, int) and t + 2 >= NT):
                        stage(dve, t + 2, s)
                    if take_dve is not None:
                        dve.wait_ge(multiplied, t + 3)
                        take_dve(dve, t, prod[:, s, :, :]).then_inc(out_dve, 1)

                if norm is not None:
                    for t in range(2):
                        stage(dve, t, t)
                each_tile(dve, tile, peel=3)


SLOTS = 4


def attend(nc, c, g, name, heads, own_table, table, width, out_table, qk, bias_row=None):
    h, dh = heads, D // heads
    av = dh + 1
    own_w = D if qk else width
    groups = NT // GROUP
    with Mem(nc, name) as m:
        rows = m.sb("rows", [P, SLOTS, ROUNDS, width])
        own = m.sb("own", [P, NT, own_w])
        acc = m.sb("acc", [P, NT, h, av])
        peak = m.sb("peak", [P, NT, h])
        new_peak = m.sb("new_peak", [P, SLOTS, 1, h])
        idx = m.sb("idx", [P, SLOTS, ROUNDS], I32)
        tile_of = m.sb("tile_of", [1, MAX_CHUNKS], I32)
        score = m.sb("score", [P, SLOTS, ROUNDS + 1, h])
        wv = m.sb("wv", [P, SLOTS, ROUNDS + 1, h, av])
        recip = m.sb("recip", [P, 2, NT, h])
        part = m.ps("part", [P, SLOTS, 512])
        prod = m.sb("prod", [P, ROUNDS, D]) if qk else m.sb("prod", [P, ROUNDS, h])
        bias_bc = None if qk else m.sb("bias_bc", [P, D])
        idx_in = [m.sem(f"idx_in{k}") for k in range(SLOTS)]
        gathered = [m.sem(f"gathered{k}") for k in range(SLOTS)]
        (own_in, chunk_ready, multiplied, summed, scored, maxed, shifted, exped, weighted, peaked, kept, part_sum,
         rescaled, added, state_set, normed, scattered, passed, biased, gelued, bias_in, tiles_in, den) = (
            m.sem(s) for s in ("own_in", "chunk_ready", "multiplied", "summed", "scored", "maxed", "shifted",
                               "exped", "weighted", "peaked", "kept", "part_sum", "rescaled", "added", "state_set",
                               "normed", "scattered", "passed", "biased", "gelued", "bias_in", "tiles_in", "den"))

        def blocks_of(eng):
            total = eng.value_load(g.first_chunk[0:1, NT:NT + 1], min_val=NT, max_val=MAX_CHUNKS)
            return eng.snap((total + (SLOTS - 1)) // SLOTS)

        with nc.Block() as block:
            @block.sync
            def _(sp):
                def load_idx(j, k):
                    sp.dma_start(idx[:, k, :], g.neighbours[bass.ds(j // (WIN // ROUNDS), 1), :, bass.ds((j % (WIN // ROUNDS)) * ROUNDS, ROUNDS)]
                                 .rearrange("a p c -> (a p) c")).then_inc(idx_in[k], 16)

                for k in range(SLOTS):
                    load_idx(k, k)
                sp.dma_start(tile_of[:, :], g.tile_of.rearrange("(a n) -> a n", a=1)).then_inc(tiles_in, 16)
                if not qk:
                    sp.dma_start(bias_bc[:, :], bias_row.rearrange("(a n) -> a n", a=1).to_broadcast([P, D])).then_inc(bias_in, 16)
                blocks = blocks_of(sp)
                with sp.Fori(1, blocks) as i:
                    for k in range(SLOTS):
                        sp.wait_ge(gathered[k], i * (16 * ROUNDS))
                        sp.sem_inc(chunk_ready, 1)
                        load_idx(i * SLOTS + k, k)
                for k in range(SLOTS):
                    sp.wait_ge(gathered[k], blocks * (16 * ROUNDS))
                    sp.sem_inc(chunk_ready, 1)

            @block.gpsimd
            def _(pool):
                for t in range(NT):
                    pool.indirect_dma_start(out=own[:, t, :], out_offset=None, in_=own_table,
                                            in_offset=bass.IndirectOffsetOnAxis(ap=g.order[:, t:t + 1], axis=0)).then_inc(own_in, 16)
                with pool.Fori(0, blocks_of(pool)) as i:
                    for k in range(SLOTS):
                        pool.wait_ge(idx_in[k], i * 16 + 16)
                        pool.wait_ge(weighted, i * SLOTS + (k + 1))
                        pool.sem_inc(passed, 1)
                        for r in range(ROUNDS):
                            pool.indirect_dma_start(out=rows[:, k, r, :], out_offset=None, in_=table,
                                                    in_offset=bass.IndirectOffsetOnAxis(ap=idx[:, k, r:r + 1], axis=0)).then_inc(gathered[k], 16)
                for t in range(NT):
                    if t % GROUP == 0:
                        pool.wait_ge(normed if qk else gelued, t // GROUP + 1)
                    pool.indirect_dma_start(out=out_table, out_offset=bass.IndirectOffsetOnAxis(ap=g.order[:, t:t + 1], axis=0),
                                            in_=own[:, t, 0:D], in_offset=None).then_inc(scattered, 16)
                pool.wait_ge(scattered, 16 * NT)

            @block.vector
            def _(dve):
                if qk:
                    dve.memset(peak[:, :, :], -1.0e30).then_inc(state_set, 1)
                    dve.memset(acc[:, :, :, :], 0.0).then_inc(state_set, 1)
                    dve.wait_ge(state_set, 2)
                    dve.wait_ge(own_in, 16 * NT)
                else:
                    dve.wait_ge(own_in, 16 * NT)
                    dve.tensor_tensor(recip[:, 0, :, :], own[:, :, D:D + h], own[:, :, D + h:D + 2 * h], ALU.add).then_inc(state_set, 1)
                    dve.tensor_copy(acc[:, :, :, 0:dh], own[:, :, 0:D].rearrange("p t (h d) -> p t h d", d=dh)).then_inc(state_set, 1)
                    dve.memset(acc[:, :, :, dh], 1.0).then_inc(state_set, 1)
                    dve.wait_ge(state_set, 3)
                    dve.scalar_tensor_tensor(peak[:, :, :], recip[:, 0, :, :], 0.2, recip[:, 0, :, :], ALU.mult, ALU.max).then_inc(state_set, 1)
                    dve.wait_ge(state_set, 4)
                dve.wait_ge(tiles_in, 16)
                dve.sem_inc(weighted, SLOTS)
                dve.sem_inc(added, 3)
                dve.sem_inc(rescaled, 2)
                dve.sem_inc(kept, 1)
                blocks = blocks_of(dve)

                def tile_at(j):
                    return dve.value_load(tile_of[0:1, bass.ds(j, 1)], min_val=0, max_val=NT - 1)

                def begin_scores(k, n, t):
                    row = rows[:, k, :, :]
                    dve.wait_ge(kept, n)
                    dve.tensor_copy(score[:, k, ROUNDS:ROUNDS + 1, :], peak[:, bass.ds(t, 1), :]).then_inc(peaked, 1)
                    dve.wait_ge(chunk_ready, n)
                    if qk:
                        q = own[:, bass.ds(t, 1), :].to_broadcast([P, ROUNDS, D])
                        dve.tensor_tensor(prod[:, :, :], row[:, :, 0:D], q, ALU.mult).then_inc(multiplied, 1)
                    else:
                        dve.tensor_tensor(prod[:, :, :], row[:, :, D:D + h], own[:, bass.ds(t, 1), D + h:D + 2 * h].to_broadcast([P, ROUNDS, h]),
                                          ALU.add).then_inc(multiplied, 1)

                def sum_scores(k, n):
                    s = score[:, k, 0:ROUNDS, :]
                    dve.wait_ge(multiplied, n)
                    if qk:
                        dve.tensor_reduce(s, prod[:, :, :].rearrange("p r (h d) -> p r h d", d=dh), AX.X, ALU.add).then_inc(summed, 1)
                    else:
                        dve.scalar_tensor_tensor(s, prod[:, :, :], 0.2, prod[:, :, :], ALU.mult, ALU.max).then_inc(summed, 1)

                def bias_scores(k, n):
                    s = score[:, k, 0:ROUNDS, :]
                    dve.wait_ge(summed, n)
                    if qk:
                        dve.tensor_tensor(s, s, rows[:, k, :, 2 * D:2 * D + 1].to_broadcast([P, ROUNDS, h]), ALU.add).then_inc(scored, 1)

                def shift_scores(k, n, t):
                    s = score[:, k, :, :]
                    dve.wait_ge(peaked, n)
                    if qk:
                        dve.wait_ge(scored, n)
                    dve.tensor_reduce(new_peak[:, k, 0, :], s.rearrange("p r h -> p h r"), AX.X, ALU.max).then_inc(maxed, 1)
                    dve.wait_ge(maxed, n)
                    dve.tensor_tensor(s, s, new_peak[:, k, :, :].to_broadcast([P, ROUNDS + 1, h]), ALU.subtract).then_inc(shifted, 1)
                    dve.tensor_copy(peak[:, bass.ds(t, 1), :], new_peak[:, k, :, :]).then_inc(kept, 1)

                def weight_chunk(k, n):
                    row, w = rows[:, k, :, :], wv[:, k, :, :, :]
                    val = row[:, :, D:2 * D] if qk else row[:, :, 0:D]
                    dve.wait_ge(exped, n)
                    dve.tensor_tensor(w[:, 0:ROUNDS, :, 0:dh], val.rearrange("p r (h d) -> p r h d", d=dh),
                                      w[:, 0:ROUNDS, :, dh:dh + 1].to_broadcast([P, ROUNDS, h, dh]), ALU.mult).then_inc(weighted, 1)

                def rescale(k, n, t):
                    a = acc[:, bass.ds(t, 1), :, :].rearrange("p a h f -> p (a h) f")
                    dve.wait_ge(added, n)
                    dve.tensor_tensor(a, a, wv[:, k, ROUNDS, :, dh:dh + 1].to_broadcast([P, h, av]), ALU.mult).then_inc(rescaled, 1)

                def accumulate(k, n, t):
                    a = acc[:, bass.ds(t, 1), :, :].rearrange("p a h f -> p (a h f)")
                    dve.wait_ge(rescaled, n)
                    dve.wait_ge(part_sum, n)
                    dve.tensor_tensor(a, a, part[:, k, 0:h * av], ALU.add).then_inc(added, 1)

                def block_of(i, first):
                    n = [k + 1 if first else dve.snap(i * SLOTS + (k + 1)) for k in range(SLOTS)]
                    t = [tile_at(0 if first else i * SLOTS)]
                    for k in range(SLOTS):
                        one, two = (k - 1) % SLOTS, (k - 2) % SLOTS
                        begin_scores(k, n[k], t[k])
                        if not (first and k < 1):
                            weight_chunk(one, n[k] - 1)
                        if k < SLOTS - 1:
                            t.append(tile_at(k + 1 if first else i * SLOTS + (k + 1)))
                        sum_scores(k, n[k])
                        if not (first and k < 2):
                            t_two = t[k - 2] if k >= 2 else tile_at(i * SLOTS + (k - 2))
                            rescale(two, n[k], t_two)
                        bias_scores(k, n[k])
                        if not (first and k < 2):
                            accumulate(two, n[k], t_two)
                        shift_scores(k, n[k], t[k])

                block_of(0, True)
                with dve.Fori(1, blocks) as i:
                    block_of(i, False)
                last = dve.snap(blocks * SLOTS)
                weight_chunk(SLOTS - 1, last)
                for back in (1, 0):
                    t_back = tile_at(last - (back + 1))
                    rescale(SLOTS - 1 - back, last + (2 - back), t_back)
                    accumulate(SLOTS - 1 - back, last + (2 - back), t_back)
                dve.wait_ge(added, last + 3)
                dve.tensor_scalar(recip[:, 0, :, :], acc[:, :, :, dh], 1.0e-30, None, ALU.max).then_inc(den, 1)
                dve.wait_ge(den, 1)
                dve.reciprocal(recip[:, 1, :, :], recip[:, 0, :, :]).then_inc(den, 1)
                dve.wait_ge(den, 2)
                if not qk:
                    dve.wait_ge(bias_in, 16)
                for k in range(groups):
                    part_t = slice(GROUP * k, GROUP * (k + 1))
                    dve.tensor_tensor(own[:, part_t, 0:D].rearrange("p t (h d) -> p t h d", d=dh), acc[:, part_t, :, 0:dh],
                                      recip[:, 1, part_t, :].unsqueeze(3).to_broadcast([P, GROUP, h, dh]), ALU.mult).then_inc(normed, 1)
                    if not qk:
                        dve.wait_ge(normed, k + 1)
                        dve.tensor_tensor(own[:, part_t, 0:D], own[:, part_t, 0:D], bias_bc[:, :].unsqueeze(1).to_broadcast([P, GROUP, D]),
                                          ALU.add).then_inc(biased, 1)

            @block.scalar
            def _(act):
                with act.Fori(0, blocks_of(act)) as i:
                    for k in range(SLOTS):
                        act.wait_ge(shifted, i * SLOTS + (k + 1))
                        act.activation(wv[:, k, :, :, dh], score[:, k, :, :], ACT.Exp).then_inc(exped, 1)
                if not qk:
                    for k in range(groups):
                        act.wait_ge(biased, k + 1)
                        out = own[:, GROUP * k:GROUP * (k + 1), 0:D]
                        act.activation(out, out, ACT.Gelu).then_inc(gelued, 1)

            @block.tensor
            def _(pe):
                pe.sem_inc(part_sum, 2)
                with pe.Fori(0, blocks_of(pe)) as i:
                    for k in range(SLOTS):
                        pe.wait_ge(weighted, i * SLOTS + (k + 1 + SLOTS))
                        for r in range(ROUNDS):
                            last = pe.matmul(part[:, k, 0:h * av], c.ident[:, :], wv[:, k, r, :, :].rearrange("p h f -> p (h f)"),
                                             start=(r == 0), stop=(r == ROUNDS - 1))
                        last.then_inc(part_sum, 1)


def load_weights(nc, name, loads):
    with Mem(nc, name) as m:
        loaded = m.sem("loaded")
        with nc.Block() as block:
            @block.sync
            def _(sp):
                for dst, src in loads:
                    sp.dma_start(dst, src).then_inc(loaded, 16)
                sp.wait_ge(loaded, 16 * len(loads))


def tiles(table, w):
    return table.rearrange("(t p) w -> p t w", p=P)


def table_tiles(k):
    t = GROUP * k
    s = t + (1 if t >= DUMMY // P else 0)
    return slice(s, s + GROUP)


def load_nodes(nc, c, x_in, x):
    full = N_NODES // P
    rest = N_NODES - full * P
    with Mem(nc, "ldx") as m:
        cleared, loaded = m.sem("cleared"), m.sem("loaded")
        with nc.Block() as block:
            @block.vector
            def _(dve):
                dve.memset(x[:, full, :], 0.0).then_inc(cleared, 1)
                dve.memset(c.eps[:, :], EPS).then_inc(cleared, 1)
                dve.wait_ge(cleared, 2)

            @block.sync
            def _(sp):
                sp.dma_start(x[:, 0:full, :], x_in[0:full * P, :].rearrange("(t p) f -> p t f", p=P)).then_inc(loaded, 16)
                sp.wait_ge(cleared, 2)
                sp.dma_start(x[0:rest, full, :], x_in[full * P:N_NODES, :]).then_inc(loaded, 16)
                sp.wait_ge(loaded, 32)


def fill_rows(nc, name, rows, width, low_cols=None):
    with Mem(nc, name) as m:
        fill = m.sb("fill", [P, width])
        filled, stored = m.sem("filled"), m.sem("stored")
        with nc.Block() as block:
            @block.vector
            def _(dve):
                dve.memset(fill[:, :], 0.0).then_inc(filled, 1)
                if low_cols is not None:
                    dve.wait_ge(filled, 1)
                    dve.memset(fill[:, low_cols], -3.0e38).then_inc(filled, 1)

            @block.sync
            def _(sp):
                sp.wait_ge(filled, 1 if low_cols is None else 2)
                n = rows.shape[0] // P
                for t in range(n):
                    sp.dma_start(rows[t * P:(t + 1) * P, :], fill[:, :]).then_inc(stored, 16)
                sp.wait_ge(stored, 16 * n)


NE, HID = 8, 1024
HC = HID // P
A_ROWS = 2 * NPAD
MAX_SLOT_TILES = 57
SLOT_COLS = 60


def top_two(nc, c, name, logits, n_exp, padded, top, idx_f):
    with Mem(nc, name) as m:
        top8, idx8 = m.sb("top8", [P, NT, 8]), m.sb("idx8", [P, NT, 8], mybir.dt.uint32)
        maxed, found, copied = m.sem("maxed"), m.sem("found"), m.sem("copied")
        with nc.Block() as block:
            @block.vector
            def _(dve):
                for t in range(NT):
                    dve.max(top8[:, t, :], logits[:, t, :]).then_inc(maxed, 1)
                dve.wait_ge(maxed, NT)
                for t in range(NT):
                    dve.max_index(idx8[:, t, :], top8[:, t, :], logits[:, t, :]).then_inc(found, 1)
                dve.wait_ge(found, NT)
                dve.tensor_copy(idx_f[:, :, :], idx8[:, :, 0:2]).then_inc(copied, 1)
                dve.tensor_copy(top[:, :, :], top8[:, :, 0:2]).then_inc(copied, 1)
                dve.wait_ge(copied, 2)


def route(nc, c, r, logits):
    with Mem(nc, "rt") as m:
        top, idx_f = m.sb("top", [P, NT, 2]), m.sb("idx_f", [P, NT, 2])
        top_two(nc, c, "rt2", logits, NE, NE, top, idx_f)
        diff, e2, den = m.sb("diff", [P, NT]), m.sb("e2", [P, NT]), m.sb("den", [P, NT])
        chosen = m.sb("chosen", [P, 3, NT, NE])
        node_f = m.sb("node_f", [P, NT])
        counts_ps, before_ps = m.ps("counts", [P, 512]), m.ps("before", [P, 512])
        cum = m.sb("cum", [P, NE, NT + 1])
        last_of = m.sb("last_of", [P, NE + 1])
        n_i, n_f = m.sb("n_i", [P, NE], I32), m.sb("n_f", [P, NE])
        slot_all = m.sb("slot_all", [P, NT, NE])
        pick = m.sb("pick", [P, 2, NT, NE])
        slot_f = m.sb("slot_f", [P, 2, NT])
        sl_i = m.sb("sl_i", [P, 2, 2, NT], I32)
        sl_f = m.sb("sl_f", [P, 2, 2, NT])
        oh_lane, oh_tile = m.sb("oh_lane", [P, 2, P]), m.sb("oh_tile", [P, 2, SLOT_COLS])
        slots_ps = m.ps("slots", [P, SLOT_COLS])
        past = m.sb("past", [P, SLOT_COLS, NE])
        exp_f = m.sb("exp_f", [P, SLOT_COLS])
        chain, ready, expd, summed, made, placed = (m.sem(x) for x in ("chain", "ready", "expd", "summed", "made", "placed"))
        with nc.Block() as block:
            @block.gpsimd
            def _(pool):
                pool.iota(node_f[:, :], pattern=[[P, NT]], base=0, channel_multiplier=1,
                          allow_small_or_imprecise_dtypes=True).then_inc(ready, 1)

            @block.scalar
            def _(act):
                act.wait_ge(ready, 2)
                act.activation(e2[:, :], diff[:, :], ACT.Exp).then_inc(expd, 1)

            @block.vector
            def _(dve):
                n = [0]

                def step(ins):
                    n[0] += 1
                    ins.then_inc(chain, 1)
                    dve.wait_ge(chain, n[0])

                dve.wait_ge(ready, 1)
                dve.tensor_tensor(diff[:, :], top[:, :, 1], top[:, :, 0], ALU.subtract).then_inc(ready, 1)
                for k in range(2):
                    step(dve.tensor_tensor(chosen[:, k, :, :], idx_f[:, :, k:k + 1].to_broadcast([P, NT, NE]),
                                           c.iota_f[:, 0:NE].unsqueeze(1).to_broadcast([P, NT, NE]), ALU.is_equal))
                step(dve.tensor_tensor(chosen[:, 2, :, :], chosen[:, 0, :, :], chosen[:, 1, :, :], ALU.add))
                dve.sem_inc(ready, 1)
                dve.wait_ge(expd, 1)
                step(dve.tensor_scalar(den[:, :], e2[:, :], 1.0, None, ALU.add))
                step(dve.reciprocal(r.weight[:, 0, :], den[:, :]))
                step(dve.tensor_tensor(r.weight[:, 1, :], r.weight[:, 0, :], e2[:, :], ALU.mult))
                dve.wait_ge(summed, 1)
                step(dve.memset(cum[:, :, 0:1], 0.0))
                for e in range(NE):
                    step(dve.tensor_tensor_scan(cum[:, e, 1:NT + 1], c.ones[:, 0:NT],
                                                counts_ps[:, 0:NT * NE].rearrange("p (t e) -> p e t", e=NE)[:, e, :], 0.0, ALU.mult, ALU.add))
                step(dve.tensor_scalar(n_f[:, :], cum[:, :, NT], float(P - 1), float(P), ALU.add, ALU.max))
                step(dve.tensor_copy(n_i[:, :], n_f[:, :]))
                step(dve.tensor_single_scalar(n_i[:, :], n_i[:, :], 7, ALU.logical_shift_right))
                step(dve.tensor_copy(n_f[:, :], n_i[:, :]))
                step(dve.memset(last_of[:, 0:1], 0.0))
                step(dve.tensor_tensor_scan(last_of[:, 1:NE + 1], c.ones[:, 0:NE], n_f[:, :], 0.0, ALU.mult, ALU.add))
                step(dve.tensor_copy(r.first_tile[:, :], last_of[:, :]))
                step(dve.tensor_scalar(n_f[:, :], last_of[:, 0:NE], float(P), None, ALU.mult))
                step(dve.tensor_tensor(slot_all[:, :, :], cum[:, :, 0:NT].rearrange("p e t -> p t e"),
                                       n_f[:, :].unsqueeze(1).to_broadcast([P, NT, NE]), ALU.add))
                step(dve.tensor_tensor(slot_all[:, :, :], slot_all[:, :, :],
                                       before_ps[:, 0:NT * NE].rearrange("p (t e) -> p t e", e=NE), ALU.add))
                for k in range(2):
                    step(dve.tensor_tensor(pick[:, k, :, :], chosen[:, k, :, :], slot_all[:, :, :], ALU.mult))
                    step(dve.tensor_reduce(slot_f[:, k, :], pick[:, k, :, :], AX.X, ALU.add))
                step(dve.tensor_copy(r.slot[:, :, :], slot_f[:, :, :]))
                step(dve.tensor_single_scalar(sl_i[:, :, 0, :], r.slot[:, :, :], P - 1, ALU.bitwise_and))
                step(dve.tensor_single_scalar(sl_i[:, :, 1, :], r.slot[:, :, :], 7, ALU.logical_shift_right))
                step(dve.tensor_copy(sl_f[:, :, :, :], sl_i[:, :, :, :]))
                step(dve.tensor_tensor(past[:, :, :], c.iota_f[:, 0:SLOT_COLS].unsqueeze(2).to_broadcast([P, SLOT_COLS, NE]),
                                       last_of[:, 1:NE + 1].unsqueeze(1).to_broadcast([P, SLOT_COLS, NE]), ALU.is_ge))
                step(dve.tensor_reduce(exp_f[:, :], past[:, :, :], AX.X, ALU.add))
                step(dve.tensor_scalar(exp_f[:, :], exp_f[:, :], float(NE - 1), None, ALU.min))
                step(dve.tensor_copy(r.expert[:, :], exp_f[:, :]))
                with dve.Fori(0, NT) as t:
                    for k in range(2):
                        dve.wait_ge(placed, t * 2 + (k + 1))
                        dve.tensor_scalar(oh_lane[:, k, :], c.iota_f[:, 0:P], sl_f[:, k, 0, bass.ds(t, 1)], None, ALU.is_equal).then_inc(made, 1)
                        dve.tensor_scalar(oh_tile[:, k, :], c.iota_f[:, 0:SLOT_COLS], sl_f[:, k, 1, bass.ds(t, 1)], node_f[:, bass.ds(t, 1)],
                                          ALU.is_equal, ALU.mult).then_inc(made, 1)
                dve.wait_ge(placed, 2 * NT + 2)
                step(dve.tensor_copy(r.node[:, :], slots_ps[:, :]))

            @block.tensor
            def _(pe):
                pe.wait_ge(ready, 3)
                flat = chosen[:, 2, :, :].rearrange("p t e -> p (t e)")
                pe.matmul(counts_ps[:, 0:NT * NE], c.ones[:, :], flat, start=True, stop=True)
                pe.matmul(before_ps[:, 0:NT * NE], c.before[:, :], flat, start=True, stop=True).then_inc(summed, 1)
                pe.matmul(slots_ps[:, :], c.zeros[:, 0:P], c.zeros[:, 0:SLOT_COLS], start=True, stop=True).then_inc(placed, 2)
                with pe.Fori(0, NT) as t:
                    for k in range(2):
                        pe.wait_ge(made, t * 4 + 2 * (k + 1))
                        pe.matmul(slots_ps[:, :], oh_lane[:, k, :], oh_tile[:, k, :], start=False, stop=True,
                                  skip_group_check=True).then_inc(placed, 1)


def experts(nc, c, r, xn_rows, y_rows, w):
    with Mem(nc, "ex") as m:
        w1, w2 = m.sb("w1", [P, 2, KC, HID]), m.sb("w2", [P, 2, HC, D])
        b1, b2 = m.sb("b1", [P, NE, HC]), m.sb("b2", [P, NE, D])
        ln_g, ln_b = m.sb("ln_g", [P, NE, KC]), m.sb("ln_b", [P, NE, KC])
        node_at = m.sb("node_at", [P, 1], I32)
        x_in = m.sb("x_in", [P, D])
        xe = m.sb("xe", [P, KC, P])
        hid = m.sb("hid", [P, HC, P])
        y = m.sb("y", [P, 2, D])
        turn, up, down = m.ps("turn", [P, 512]), m.ps("up", [P, HC // 2, 512]), m.ps("down", [P, 2, 512])
        w_in = [m.sem(f"w_in{k}") for k in range(2)]
        (arrived, node_set, turned, scaled, up_done, act_done, down_done, y_ready, y_stored, bias_in, passed) = (
            m.sem(s) for s in ("arrived", "node_set", "turned", "scaled", "up_done", "act_done", "down_done",
                               "y_ready", "y_stored", "bias_in", "passed"))

        def first_tile(eng, e):
            return eng.value_load(r.first_tile[0:1, bass.ds(e, 1)], min_val=0, max_val=MAX_SLOT_TILES)

        with nc.Block() as block:
            @block.sync
            def _(sp):
                def load_expert(e, k):
                    sp.dma_start(w1[:, k, :, :], w.w1[bass.ds(e, 1), :, :].rearrange("a (k p) n -> p (a k) n", p=P)).then_inc(w_in[k], 16)
                    sp.dma_start(w2[:, k, :, :], w.w2[bass.ds(e, 1), :, :].rearrange("a (k p) n -> p (a k) n", p=P)).then_inc(w_in[k], 16)

                load_expert(0, 0)
                with nc.allow_non_contiguous_dma(reason="per-partition biases, a few thousand numbers"):
                    sp.dma_start(b1[:, :, :], w.b1.rearrange("e (c p) -> p e c", p=P)).then_inc(bias_in, 16)
                    sp.dma_start(ln_g[:, :, :], w.ln_g.rearrange("e (c p) -> p e c", p=P)).then_inc(bias_in, 16)
                    sp.dma_start(ln_b[:, :, :], w.ln_b.rearrange("e (c p) -> p e c", p=P)).then_inc(bias_in, 16)
                sp.dma_start(b2[:, :, :], w.b2.rearrange("(a e) f -> a e f", a=1).to_broadcast([P, NE, D])).then_inc(bias_in, 16)
                load_expert(1, 1)
                with sp.Fori(1, NE // 2) as i:
                    for k in range(2):
                        sp.wait_ge(down_done, first_tile(sp, i * 2 + k - 1))
                        sp.sem_inc(passed, 1)
                        load_expert(i * 2 + k, k)

            @block.gpsimd
            def _(pool):
                with pool.Fori(0, pool.snap(first_tile(pool, NE) + 1)) as n:
                    pool.wait_ge(turned, n + 1)
                    pool.tensor_copy(node_at[:, :], r.node[:, bass.ds(n, 1)]).then_inc(node_set, 1)
                    pool.wait_ge(node_set, n + 1)
                    pool.sem_inc(passed, 1)
                    pool.indirect_dma_start(out=x_in[:, :], out_offset=None, in_=xn_rows,
                                            in_offset=bass.IndirectOffsetOnAxis(ap=node_at[:, :], axis=0)).then_inc(arrived, 16)

            @block.vector
            def _(dve):
                total = first_tile(dve, NE)
                dve.wait_ge(bias_in, 64)

                def scale(n):
                    e = dve.value_load(r.expert[0:1, bass.ds(n, 1)], min_val=0, max_val=NE - 1)
                    dve.wait_ge(turned, n + 2)
                    for h in range(KC):
                        dve.tensor_scalar(xe[:, h, :], turn[:, h * P:(h + 1) * P],
                                          ln_g[:, bass.ds(e, 1), h], ln_b[:, bass.ds(e, 1), h], ALU.mult, ALU.add).then_inc(scaled, 1)

                dve.sem_inc(y_ready, 2)
                scale(0)
                with dve.Fori(0, total) as n:
                    scale(n + 1)
                    e = dve.value_load(r.expert[0:1, bass.ds(n, 1)], min_val=0, max_val=NE - 1)
                    dve.wait_ge(down_done, n + 1)
                    dve.wait_ge(y_stored, n * 16 + 16)
                    dve.tensor_tensor(y[:, bass.ds(n % 2, 1), :].rearrange("p a f -> p (a f)"),
                                      down[:, bass.ds(n % 2, 1), 0:D].rearrange("p a f -> p (a f)"),
                                      b2[:, bass.ds(e, 1), :].rearrange("p a f -> p (a f)"), ALU.add).then_inc(y_ready, 1)

            @block.tensor
            def _(pe):
                def turn_tile(n):
                    pe.wait_ge(arrived, n * 16 + 16)
                    for h in range(KC):
                        last = pe.transpose(turn[:, h * P:(h + 1) * P], x_in[:, h * P:(h + 1) * P], c.ident[:, :])
                    last.then_inc(turned, 1)

                pe.sem_inc(turned, 1)
                turn_tile(0)
                pe.wait_ge(bias_in, 64)
                with pe.Fori(0, NE // 2) as i:
                    for k in range(2):
                        e = i * 2 + k
                        pe.wait_ge(w_in[k], i * 32 + 32)
                        pe.sem_inc(passed, 1)
                        with pe.Fori(first_tile(pe, e), first_tile(pe, e + 1)) as n:
                            pe.wait_ge(scaled, n * KC + KC)
                            for q in range(HC):
                                for h in range(KC):
                                    last = pe.matmul(up[:, q // 2, (q % 2) * P:(q % 2 + 1) * P], w1[:, k, h, q * P:(q + 1) * P], xe[:, h, :], start=(h == 0), stop=(h == KC - 1))
                                if q % 2:
                                    last.then_inc(up_done, 1)
                            turn_tile(n + 1)
                            pe.wait_ge(y_ready, n + 1)
                            out = down[:, bass.ds(n % 2, 1), 0:D].rearrange("p a f -> p (a f)")
                            for q in range(HC):
                                pe.wait_ge(act_done, n * HC + (q + 1))
                                last = pe.matmul(out, hid[:, q, :], w2[:, k, q, :], start=(q == 0), stop=(q == HC - 1))
                            last.then_inc(down_done, 1)

            @block.scalar
            def _(act):
                total = first_tile(act, NE)
                act.sem_inc(y_stored, 32)
                act.wait_ge(bias_in, 64)
                with act.Fori(0, total) as n:
                    e = act.value_load(r.expert[0:1, bass.ds(n, 1)], min_val=0, max_val=NE - 1)
                    for q in range(HC):
                        if q % 2 == 0:
                            act.wait_ge(up_done, n * (HC // 2) + (q // 2 + 1))
                        act.activation(hid[:, q, :], up[:, q // 2, (q % 2) * P:(q % 2 + 1) * P], ACT.Gelu, bias=b1[:, bass.ds(e, 1), q]).then_inc(act_done, 1)
                    act.wait_ge(y_ready, n + 3)
                    act.wait_ge(y_stored, n * 16 + 32)
                    act.dma_start(y_rows[bass.ds(n, 1), :, :].rearrange("a p f -> (a p) f"),
                                  y[:, bass.ds(n % 2, 1), :].rearrange("p a f -> p (a f)")).then_inc(y_stored, 16)
                act.wait_ge(y_stored, total * 16 + 32)
                act.sem_inc(passed, 1)


def combine(nc, c, r, y_rows, x):
    with Mem(nc, "cb") as m:
        ys = m.sb("ys", [P, 2, NT, D])
        arrived = [m.sem(f"arrived{k}") for k in range(NT // GROUP)]
        added = m.sem("added")
        with nc.Block() as block:
            @block.gpsimd
            def _(pool):
                for t in range(NT):
                    for k in range(2):
                        pool.indirect_dma_start(out=ys[:, k, t, :], out_offset=None, in_=y_rows,
                                                in_offset=bass.IndirectOffsetOnAxis(ap=r.slot[:, k, t:t + 1], axis=0)).then_inc(arrived[t // GROUP], 16)

            @block.vector
            def _(dve):
                for j in range(NT // GROUP):
                    dve.wait_ge(arrived[j], 32 * GROUP)
                    for k in range(2):
                        for t in range(GROUP * j, GROUP * (j + 1)):
                            dve.scalar_tensor_tensor(x[:, t, :], ys[:, k, t, :], r.weight[:, k, t:t + 1], x[:, t, :],
                                                     ALU.mult, ALU.add).then_inc(added, 1)
                        dve.wait_ge(added, GROUP * (2 * j + k + 1))


GH, GC = 4, 64
GW = D + 2 * GH
QH = 8
KVW = 2 * D + 4
E2, SH2, EH1, EH2 = 4, 128, 128, 64


def gat_weights(nc, c, name, w_ext, w_in, a_src, a_dst):
    with Mem(nc, name) as m:
        att = m.sb("att", [P, KC, 2 * GH])
        w_t = m.sb("w_t", [P, KC, KC, P])
        turn, prod = m.ps("turn", [P, KC, KC, P]), m.ps("prod", [P, KC, 2 * GH])
        cleared, loaded, turned, copied, mult, done = (m.sem(s) for s in ("cleared", "loaded", "turned", "copied", "mult", "done"))
        with nc.Block() as block:
            @block.sync
            def _(sp):
                sp.dma_start(w_ext[:, :, 0:D], w_in.rearrange("(k p) n -> p k n", p=P)).then_inc(loaded, 16)
                sp.wait_ge(cleared, 1)
                for k, a in enumerate((a_src, a_dst)):
                    for h in range(GH):
                        sp.dma_start(att[(h % 2) * GC:(h % 2 + 1) * GC, h // 2, k * GH + h:k * GH + h + 1],
                                     a[h, :].rearrange("(c o) -> c o", o=1)).then_inc(loaded, 16)

            @block.vector
            def _(dve):
                dve.memset(att[:, :, :], 0.0).then_inc(cleared, 1)
                dve.wait_ge(turned, 1)
                dve.tensor_copy(w_t[:, :, :, :], turn[:, :, :, :]).then_inc(copied, 1)
                dve.wait_ge(mult, 1)
                dve.tensor_copy(w_ext[:, :, D:GW], prod[:, :, :]).then_inc(done, 1)
                dve.wait_ge(done, 1)

            @block.tensor
            def _(pe):
                pe.wait_ge(loaded, 16 * (1 + 2 * GH))
                for k in range(KC):
                    for f in range(KC):
                        last = pe.transpose(turn[:, f, k, :], w_ext[:, k, f * P:(f + 1) * P], c.ident[:, :])
                last.then_inc(turned, 1)
                pe.wait_ge(copied, 1)
                for k in range(KC):
                    for f in range(KC):
                        last = pe.matmul(prod[:, k, :], w_t[:, f, k, :], att[:, f, :], start=(f == 0), stop=(f == KC - 1))
                last.then_inc(mult, 1)


def gates_to_weights(nc, c, raw, w5):
    with Mem(nc, "gw") as m:
        gates = m.sb("gates", [P, NT, 8])
        peak, total = m.sb("peak", [P, NT]), m.sb("total", [P, NT])
        top, idx_f = m.sb("top", [P, NT, 2]), m.sb("idx_f", [P, NT, 2])
        wt = m.sb("wt", [P, 3, NT])
        chosen = m.sb("chosen", [P, 2, NT, E2])
        chain, ready, expd = m.sem("chain"), m.sem("ready"), m.sem("expd")
        with nc.Block() as block:
            @block.vector
            def _(dve):
                n = [0]

                def step(ins):
                    n[0] += 1
                    ins.then_inc(chain, 1)
                    dve.wait_ge(chain, n[0])

                step(dve.memset(gates[:, :, :], -1.0))
                step(dve.tensor_reduce(peak[:, :], raw[:, :, :], AX.X, ALU.max))
                dve.tensor_tensor(raw[:, :, :], raw[:, :, :], peak[:, :].unsqueeze(2).to_broadcast([P, NT, E2]), ALU.subtract).then_inc(ready, 1)
                dve.wait_ge(expd, 1)
                step(dve.tensor_reduce(total[:, :], gates[:, :, 0:E2], AX.X, ALU.add))
                step(dve.reciprocal(total[:, :], total[:, :]))
                step(dve.tensor_tensor(gates[:, :, 0:E2], gates[:, :, 0:E2], total[:, :].unsqueeze(2).to_broadcast([P, NT, E2]), ALU.mult))

            @block.scalar
            def _(act):
                act.wait_ge(ready, 1)
                act.activation(gates[:, :, 0:E2], raw[:, :, :], ACT.Exp).then_inc(expd, 1)

        top_two(nc, c, "gt2", gates, E2, 8, top, idx_f)
        chain2, ready2, expd2 = m.sem("chain2"), m.sem("ready2"), m.sem("expd2")
        with nc.Block() as block:
            @block.vector
            def _(dve):
                n = [0]

                def step(ins):
                    n[0] += 1
                    ins.then_inc(chain2, 1)
                    dve.wait_ge(chain2, n[0])

                dve.tensor_tensor(wt[:, 0, :], top[:, :, 1], top[:, :, 0], ALU.subtract).then_inc(ready2, 1)
                for k in range(2):
                    step(dve.tensor_tensor(chosen[:, k, :, :], idx_f[:, :, k:k + 1].to_broadcast([P, NT, E2]),
                                           c.iota_f[:, 0:E2].unsqueeze(1).to_broadcast([P, NT, E2]), ALU.is_equal))
                dve.wait_ge(expd2, 1)
                step(dve.tensor_scalar(wt[:, 2, :], wt[:, 1, :], 1.0, None, ALU.add))
                step(dve.reciprocal(wt[:, 0, :], wt[:, 2, :]))
                step(dve.tensor_tensor(wt[:, 1, :], wt[:, 0, :], wt[:, 1, :], ALU.mult))
                for k in range(2):
                    step(dve.tensor_tensor(chosen[:, k, :, :], chosen[:, k, :, :], wt[:, k, :].unsqueeze(2).to_broadcast([P, NT, E2]), ALU.mult))
                step(dve.memset(w5[:, :, E2:E2 + 1], 1.0))
                step(dve.tensor_tensor(w5[:, :, 0:E2], chosen[:, 0, :, :], chosen[:, 1, :, :], ALU.add))

            @block.scalar
            def _(act):
                act.wait_ge(ready2, 1)
                act.activation(wt[:, 1, :], wt[:, 0, :], ACT.Exp).then_inc(expd2, 1)


def shared_and_experts(nc, c, norm, x, w5, w, out):
    with Mem(nc, "f2") as m:
        sw1, sw2, sw3 = m.sb("sw1", [P, KC, D]), m.sb("sw2", [P, KC, SH2]), m.sb("sw3", [P, D])
        ew1, ew2 = m.sb("ew1", [P, E2, KC, EH1]), m.sb("ew2", [P, E2, EH2])
        ew3 = m.sb("ew3", [P, E2 // 2, D])
        bias1 = m.sb("bias1", [P, KC + E2])
        bias2 = m.sb("bias2", [P, 1 + E2 // 2])
        bias3 = m.sb("bias3", [E2 + 1, D])
        pair = m.sb("pair", [E2, E2 // 2, P])
        rows = m.sb("rows", [P, 2, D + E2 + 1])
        x_t = m.sb("x_t", [P, 2, KC, P])
        w_t = m.sb("w_t", [E2 + 1, 2, P])
        h1 = m.sb("h1", [P, 2, KC + E2, P])
        h2 = m.sb("h2", [P, 2, 1 + E2 // 2, P])
        turn = m.ps("turn", [P, 512])
        p1 = m.ps("p1", [P, (KC + E2) // 2, 512])
        p2 = m.ps("p2", [P, 4, P])
        pw = m.ps("pw", [P, 4, P])
        p3 = m.ps("p3", [P, 2, 512])
        loads = m.sem("loads")
        outd = [m.sem(f"outd{k}") for k in range(NT // GROUP)]
        (built, staged, turned, x_copied, w_copied, up1, act1, up2, act2, scaled, down, added) = (
            m.sem(s) for s in ("built", "staged", "turned", "x_copied", "w_copied", "up1", "act1", "up2", "act2", "scaled", "down", "added"))
        with nc.Block() as block:
            @block.sync
            def _(sp):
                with nc.allow_non_contiguous_dma(reason="per-partition biases, about a thousand numbers"):
                    sp.dma_start(sw1[:, :, :], w.sW1.rearrange("(k p) n -> p k n", p=P)).then_inc(loads, 16)
                    sp.dma_start(sw2[:, :, :], w.sW2.rearrange("(k p) n -> p k n", p=P)).then_inc(loads, 16)
                    sp.dma_start(sw3[:, :], w.sW3).then_inc(loads, 16)
                    sp.dma_start(ew2[:, :, :], w.eW2.rearrange("e p n -> p e n")).then_inc(loads, 16)
                    for t in range(2):
                        sp.dma_start(ew3[t * EH2:(t + 1) * EH2, :, :], w.eW3.rearrange("(j t) p n -> t p j n", t=2)[t]).then_inc(loads, 16)
                        sp.dma_start(bias2[t * EH2:(t + 1) * EH2, 1:1 + E2 // 2], w.eb2.rearrange("(j t) p -> t p j", t=2)[t]).then_inc(loads, 16)
                    sp.dma_start(bias1[:, 0:KC], w.sb1.rearrange("(k p) -> p k", p=P)).then_inc(loads, 16)
                    sp.dma_start(bias1[:, KC:KC + E2], w.eb1.rearrange("e p -> p e")).then_inc(loads, 16)
                    sp.dma_start(bias2[:, 0:1], w.sb2.rearrange("(p o) -> p o", o=1)).then_inc(loads, 16)
                    sp.dma_start(bias3[0:E2, :], w.eb3).then_inc(loads, 16)
                    sp.dma_start(bias3[E2:E2 + 1, :], w.sb3.rearrange("(o n) -> o n", o=1)).then_inc(loads, 16)
                    for e in range(E2):
                        sp.dma_start(ew1[:, e, :, :], w.eW1[e].rearrange("(k p) n -> p k n", p=P)).then_inc(loads, 16)
                for k in range(NT // GROUP):
                    sp.wait_ge(added, GROUP * (k + 1) + 2)
                    full = min(GROUP * (k + 1), N_NODES // P)
                    sp.dma_start(out[GROUP * k * P:full * P, :].rearrange("(t p) f -> p t f", p=P), x[:, GROUP * k:full, :]).then_inc(outd[k], 16)
                rest = N_NODES - (N_NODES // P) * P
                sp.dma_start(out[N_NODES - rest:N_NODES, :], x[0:rest, NT - 1, :]).then_inc(outd[0], 16)
                sp.wait_ge(outd[0], 32)
                for k in range(1, NT // GROUP):
                    sp.wait_ge(outd[k], 16)

            @block.gpsimd
            def _(pool):
                pool.memset(pair[:, :, :], 1.0).then_inc(built, 1)
                pool.wait_ge(built, 1)
                pool.affine_select(out=pair[:, :, :], in_=pair[:, :, :], compare_op=ALU.is_ge, fill=0.0, base=0,
                                   pattern=[[P, E2 // 2], [1, P]], channel_multiplier=-EH2).then_inc(built, 1)
                pool.wait_ge(built, 2)
                pool.affine_select(out=pair[:, :, :], in_=pair[:, :, :], compare_op=ALU.is_ge, fill=0.0, base=EH2 - 1,
                                   pattern=[[-P, E2 // 2], [-1, P]], channel_multiplier=EH2).then_inc(built, 1)

            @block.tensor
            def _(pe):
                pe.sem_inc(down, 2)
                pe.wait_ge(built, 3)
                pe.wait_ge(loads, 16 * N_LOADS)

                def tile(t, s):
                    pe.wait_ge(staged, (t + 1) * 2)
                    pe.wait_ge(x_copied, t + 1)
                    pe.wait_ge(w_copied, t + 1)
                    for h in range(KC):
                        pe.transpose(turn[:, h * P:(h + 1) * P], rows[:, s, h * P:(h + 1) * P], c.ident[:, :])
                    pe.wait_ge(scaled, (t + 1) * (E2 // 2))
                    pe.transpose(pw[0:E2 + 1, 3, :], rows[:, s, D:], c.ident[:, :]).then_inc(turned, 1)
                    pe.wait_ge(x_copied, t + 2)
                    pe.wait_ge(act1, (t + 1) * (KC + E2))
                    xt = [x_t[:, s, h, :] for h in range(KC)]
                    for q in range(KC + E2):
                        for h in range(KC):
                            lhs = sw1[:, h, q * P:(q + 1) * P] if q < KC else ew1[:, q - KC, h, :]
                            last = pe.matmul(p1[:, q // 2, (q % 2) * P:(q % 2 + 1) * P], lhs, xt[h], start=(h == 0), stop=(h == KC - 1))
                        if q % 2:
                            last.then_inc(up1, 1)
                    pe.wait_ge(w_copied, t + 2)
                    for j in range(E2 // 2):
                        last = pe.matmul(pw[:, j, :], pair[:, j, :], w_t[0:E2, s, :], start=True, stop=True)
                    hh = lambda q: h1[:, s, q, :]
                    pe.wait_ge(act2, (t + 1) * (1 + E2 // 2))
                    for k in range(KC):
                        pe.wait_ge(act1, (t + 1) * (KC + E2) + (k + 1))
                        last = pe.matmul(p2[:, 0, :], sw2[:, k, :], hh(k), start=(k == 0), stop=(k == KC - 1))
                    for e in range(E2):
                        pe.wait_ge(act1, (t + 1) * (KC + E2) + (KC + e + 1))
                        r0 = (e % 2) * EH2
                        last = pe.matmul(p2[r0:r0 + EH2, 1 + e // 2, :], ew2[:, e, :], hh(KC + e), start=True, stop=True)
                    last.then_inc(up2, 1)
                    o = p3[:, s, 0:D]
                    pe.wait_ge(down, t + 1)
                    pe.wait_ge(added, t + 1)
                    pe.matmul(o, w_t[:, s, :], bias3[:, :], start=True, stop=False)
                    pe.wait_ge(act2, (t + 1) * (1 + E2 // 2) + 1)
                    pe.matmul(o, h2[:, s, 0, :], sw3[:, :], start=False, stop=False)
                    for j in range(E2 // 2):
                        pe.wait_ge(scaled, (t + 1) * (E2 // 2) + (j + 1))
                        last = pe.matmul(o, h2[:, s, 1 + j, :], ew3[:, j, :], start=False, stop=(j == E2 // 2 - 1))
                    last.then_inc(down, 1)

                each_tile(pe, tile)

            @block.scalar
            def _(act):
                act.sem_inc(x_copied, 1)
                act.sem_inc(act1, KC + E2)
                act.sem_inc(act2, 1 + E2 // 2)
                act.wait_ge(loads, 16 * N_LOADS)

                def tile(t, s):
                    act.wait_ge(turned, t + 1)
                    act.activation(x_t[:, s, :, :].rearrange("p k n -> p (k n)"), turn[:, 0:D], ACT.Copy).then_inc(x_copied, 1)
                    for q in range(KC + E2):
                        if q % 2 == 0:
                            act.wait_ge(up1, t * ((KC + E2) // 2) + (q // 2 + 1))
                        act.activation(h1[:, s, q, :], p1[:, q // 2, (q % 2) * P:(q % 2 + 1) * P], ACT.Relu,
                                       bias=bias1[:, q:q + 1]).then_inc(act1, 1)
                    act.wait_ge(up2, t + 1)
                    for j in range(1 + E2 // 2):
                        act.activation(h2[:, s, j, :], p2[:, j, :], ACT.Relu,
                                       bias=bias2[:, j:j + 1]).then_inc(act2, 1)

                each_tile(act, tile)

            @block.vector
            def _(dve):
                dve.sem_inc(w_copied, 1)
                dve.sem_inc(scaled, E2 // 2)
                dve.sem_inc(added, 2)

                def stage(t, s):
                    normalise(dve, rows[:, s, 0:D], *norm, t).then_inc(staged, 1)
                    dve.tensor_copy(rows[:, s, D:], w5[:, bass.ds(t, 1), :].rearrange("p a n -> p (a n)")).then_inc(staged, 1)

                def tile(t, s):
                    dve.wait_ge(turned, t + 1)
                    dve.tensor_copy(w_t[:, s, :], pw[0:E2 + 1, 3, :]).then_inc(w_copied, 1)
                    if not (isinstance(t, int) and t == NT - 1):
                        stage(t + 1, 1 - s)
                    for j in range(E2 // 2):
                        dve.wait_ge(act2, (t + 1) * (1 + E2 // 2) + (j + 2))
                        h = h2[:, s, 1 + j, :]
                        dve.tensor_tensor(h, h, pw[:, j, :], ALU.mult).then_inc(scaled, 1)
                    dve.wait_ge(down, t + 3)
                    xt = x[:, bass.ds(t, 1), :].rearrange("p a f -> p (a f)")
                    dve.tensor_tensor(xt, xt, p3[:, s, 0:D], ALU.add).then_inc(added, 1)

                stage(0, 0)
                each_tile(dve, tile)


N_LOADS = 4 + 4 + 5 + E2


class Names:
    pass


def program(nc, a, out):
    Mem.past.clear()
    dram = lambda name, shape, dt=F32: nc.dram_tensor(name, shape, dt, kind="Internal").ap()
    with Mem(nc, "all") as m:
        c = Names()
        c.lane_f, c.iota_f = m.sb("lane_f", [P, 1]), m.sb("iota_f", [P, WIN])
        c.ident, c.before, c.ones, c.zeros = (m.sb(x, [P, P]) for x in ("ident", "before", "ones", "zeros"))
        c.order_bias, c.ones_b, c.ident_b, c.iota_b = (m.sb(x, [P, P], BF16) for x in ("order_bias", "ones_b", "ident_b", "iota_b"))
        c.iota_h = m.sb("iota_h", [P, WIN], F16)
        c.minus1, c.eps = m.sb("minus1", [P, 1]), m.sb("eps", [P, 1])
        build_constants(nc, c)

        graphs = []
        for name, key, val in (("s", a.src, a.dst), ("d", a.dst, a.src)):
            g = Names()
            g.name = name
            g.order, g.first_chunk = m.sb(f"order_{name}", [P, NT], I32), m.sb(f"first_chunk_{name}", [P, NT + 1], I32)
            g.key_parts, g.sort_keys = dram(f"key_parts_{name}", (2, EROWS * ROWE), BF16), dram(f"sort_keys_{name}", (NPAD,))
            g.tile_of = dram(f"tile_of_{name}", (MAX_CHUNKS,), I32)
            g.neighbours = dram(f"neighbours_{name}", (MAX_WIN, P, WIN), I32)
            g.hist_done, g.windows_known, g.window_ready, g.passed = (
                m.sem(f"{x}_{name}") for x in ("hist_done", "windows_known", "window_ready", "passed"))
            build_neighbour_table(nc, c, g, key, val)
            graphs.append(g)

        x = m.sb("x", [P, NT, D])
        load_nodes(nc, c, a.x, x)

        q_rows, kv_rows, att_rows = dram("q_rows", (TABLE_ROWS, D)), dram("kv_rows", (TABLE_ROWS, KVW)), dram("attended_rows", (TABLE_ROWS, D))
        project_qkv(nc, c, a, x, q_rows, kv_rows)
        with Mem(nc, "at") as p:
            fill_rows(nc, "fdk", kv_rows[DUMMY:DUMMY + P, :], KVW, slice(2 * D, 2 * D + 1))
            fill_rows(nc, "fdq", q_rows[DUMMY:DUMMY + P, :], D)
            attend(nc, c, graphs[0], "att", QH, q_rows, kv_rows, KVW, att_rows, True)
        with Mem(nc, "wo") as p:
            att, wt, bias = p.sb("att", [P, NT, D]), p.sb("w", [P, KC, D]), p.sb("bias", [1, D])
            load_weights(nc, "wol", [(wt[:, :, :], a.Wo.rearrange("(k p) n -> p k n", p=P)), (bias[:, :], a.bo.rearrange("(o n) -> o n", o=1))])
            add_product(nc, c, "wop", att, att_rows, wt, bias, x)

        xn_rows, y_rows = dram("xn_rows", (NPAD, D)), dram("y_rows", (MAX_SLOT_TILES + 1, P, D))
        r = Names()
        r.weight, r.slot = m.sb("r_weight", [P, 2, NT]), m.sb("r_slot", [P, 2, NT], I32)
        r.node, r.expert, r.first_tile = m.sb("r_node", [P, SLOT_COLS], I32), m.sb("r_expert", [P, SLOT_COLS], I32), m.sb("r_first_tile", [P, NE + 1], I32)
        with Mem(nc, "ro") as p:
            xt, xn, wr, br = p.sb("xt", [P, NT, D]), p.sb("xn", [P, NT, D]), p.sb("wr", [P, KC, NE]), p.sb("br", [1, NE])
            logits = p.sb("logits", [P, NT, NE])
            load_weights(nc, "rol", [(wr[:, :, :], a.Wr.rearrange("(k p) n -> p k n", p=P)), (br[:, :], a.br.rearrange("(o n) -> o n", o=1))])
            layernorm(nc, c, "ln1", x, xt)
            layernorm(nc, c, "ln1i", xt, xn)
            project(nc, c, "rop", wr, br, NE, 1, a=xt,
                    take_dve=lambda dve, t, prod: dve.tensor_copy(logits[:, bass.ds(t, 1), :], prod[:, :, 0:NE]),
                    store=lambda sp, k: [sp.dma_start(xn_rows[GROUP * k * P:GROUP * (k + 1) * P, :].rearrange("(t p) f -> p t f", p=P),
                                                      xn[:, GROUP * k:GROUP * (k + 1), :])], n_stores=1)
            route(nc, c, r, logits)
        w = Names()
        w.w1, w.w2, w.b1, w.b2, w.ln_g, w.ln_b = a.W1, a.W2, a.b1, a.b2, a.ln_g, a.ln_b
        fill_rows(nc, "fdy", y_rows.rearrange("t p f -> (t p) f")[A_ROWS:(MAX_SLOT_TILES + 1) * P, :], D)
        experts(nc, c, r, xn_rows, y_rows, w)
        combine(nc, c, r, y_rows.rearrange("t p f -> (t p) f"), x)

        h_rows = [dram(f"h_rows{i}", (TABLE_ROWS, GW)) for i in range(2)]
        g_rows = [dram(f"g_rows{i}", (TABLE_ROWS, D)) for i in range(2)]
        for i, (w_in, a_src, a_dst, b) in enumerate(((a.gW0, a.a_src0, a.a_dst0, a.gb0), (a.gW1, a.a_src1, a.a_dst1, a.gb1))):
            with Mem(nc, f"gat{i}") as p:
                wt, h_in, h_out = p.sb("w", [P, KC, GW]), p.sb("h_in", [P, NT, D]), p.sb("h_out", [P, NT, GW])
                gat_weights(nc, c, f"gaw{i}", wt, w_in, a_src, a_dst)
                fill_rows(nc, f"fdg{i}", h_rows[i][DUMMY:DUMMY + P, :], GW, slice(D, D + GH))
                mean, inv = p.sb("mean", [P, NT, 2]), p.sb("inv", [P, NT])
                if i == 0:
                    norm_stats(nc, c, "ln2", x, mean, inv)
                project(nc, c, f"gap{i}", wt, None, GW, 1, a=h_in, norm=(x, mean, inv) if i == 0 else None,
                        take_dve=lambda dve, t, prod: dve.tensor_copy(h_out[:, bass.ds(t, 1), :], prod[:, :, 0:GW]),
                        store=lambda sp, k: [sp.dma_start(tiles(h_rows[i], GW)[:, table_tiles(k), :], h_out[:, GROUP * k:GROUP * (k + 1), :])], n_stores=1,
                        load=None if i == 0 else (lambda sp, k: sp.dma_start(h_in[:, GROUP * k:GROUP * (k + 1), :], tiles(g_rows[0], D)[:, table_tiles(k), :])))
            attend(nc, c, graphs[1], f"gt{i}", GH, h_rows[i], h_rows[i], GW, g_rows[i], False, bias_row=b)

        with Mem(nc, "last") as p:
            mean, inv = p.sb("mean", [P, NT, 2]), p.sb("inv", [P, NT])
            gw, gb = p.sb("gw", [P, KC, E2]), p.sb("gb", [1, E2])
            raw, w5 = p.sb("raw", [P, NT, E2]), p.sb("w5", [P, NT, E2 + 1])
            load_weights(nc, "lal", [(gw[:, :, :], a.gW.rearrange("(k p) n -> p k n", p=P)), (gb[:, :], a.gb.rearrange("(o n) -> o n", o=1))])
            add_rows(nc, c, "addg", x, g_rows[1])
            norm_stats(nc, c, "ln3", x, mean, inv)
            project(nc, c, "gap", gw, gb, E2, 1, norm=(x, mean, inv),
                    take_dve=lambda dve, t, prod: dve.tensor_copy(raw[:, bass.ds(t, 1), :], prod[:, :, 0:E2]))
            gates_to_weights(nc, c, raw, w5)
            shared_and_experts(nc, c, (x, mean, inv), x, w5, a, out)


def project_qkv(nc, c, a, x, q_rows, kv_rows):
    with Mem(nc, "qkv") as p:
        mean, inv = p.sb("mean", [P, NT, 2]), p.sb("inv", [P, NT])
        wt, bias = p.sb("w", [P, KC, 3 * D]), p.sb("bias", [P, 3 * D])
        q_all, kv_all = p.sb("q_all", [P, NT, D]), p.sb("kv_all", [P, NT, KVW])
        load_weights(nc, "qkvl", [(wt[:, :, i * D:(i + 1) * D], w.rearrange("(k p) n -> p k n", p=P)) for i, w in enumerate((a.Wq, a.Wk, a.Wv))]
                     + [(bias[:, i * D:(i + 1) * D], b.rearrange("(o n) -> o n", o=1).to_broadcast([P, D])) for i, b in enumerate((a.bq, a.bk, a.bv))])
        q_scale = float((D // QH) ** -0.5)
        norm_stats(nc, c, "ln0", x, mean, inv)
        cleared = p.sem("cleared")
        with nc.Block() as block:
            @block.vector
            def _(dve):
                dve.memset(kv_all[:, :, 2 * D:KVW], 0.0).then_inc(cleared, 1)
                dve.tensor_scalar(bias[:, 0:D], bias[:, 0:D], q_scale, None, ALU.mult).then_inc(cleared, 1)
                dve.wait_ge(cleared, 2)
        half = 3 * D // 2

        def take_dve(dve, t, prod):
            dve.scalar_tensor_tensor(q_all[:, bass.ds(t, 1), :].rearrange("p a n -> p (a n)"), prod[:, 0, 0:D], q_scale,
                                     bias[:, 0:D], ALU.mult, ALU.add)
            dve.tensor_tensor(kv_all[:, bass.ds(t, 1), 0:half - D].rearrange("p a n -> p (a n)"), prod[:, 0, D:half],
                              bias[:, D:half], ALU.add)
            return dve.tensor_tensor(kv_all[:, bass.ds(t, 1), half - D:2 * D].rearrange("p a n -> p (a n)"), prod[:, 1, 0:half],
                                     bias[:, half:3 * D], ALU.add)

        project(nc, c, "qkp", wt, None, 3 * D, 2, norm=(x, mean, inv), take_dve=take_dve,
                store=lambda sp, k: [sp.dma_start(tiles(q_rows, D)[:, table_tiles(k), :], q_all[:, GROUP * k:GROUP * (k + 1), :]),
                                     sp.dma_start(tiles(kv_rows, KVW)[:, table_tiles(k), :], kv_all[:, GROUP * k:GROUP * (k + 1), :])], n_stores=2)


def add_product(nc, c, name, att, att_rows, wt, bias, x):
    def take_dve(dve, t, prod):
        xt = x[:, bass.ds(t, 1), :].rearrange("p a n -> p (a n)")
        return dve.tensor_tensor(xt, xt, prod[:, 0, 0:D], ALU.add)

    project(nc, c, name, wt, bias, D, 1, a=att, take_dve=take_dve,
            load=lambda sp, k: sp.dma_start(att[:, GROUP * k:GROUP * (k + 1), :], tiles(att_rows, D)[:, table_tiles(k), :]))


def add_rows(nc, c, name, x, rows):
    with Mem(nc, name) as m:
        buf = m.sb("buf", [P, NT, D])
        loaded = [m.sem(f"loaded{k}") for k in range(NT // GROUP)]
        added = m.sem("added")
        with nc.Block() as block:
            @block.sync
            def _(sp):
                for k in range(NT // GROUP):
                    sp.dma_start(buf[:, GROUP * k:GROUP * (k + 1), :], tiles(rows, D)[:, table_tiles(k), :]).then_inc(loaded[k], 16)

            @block.vector
            def _(dve):
                for k in range(NT // GROUP):
                    dve.wait_ge(loaded[k], 16)
                    part = x[:, GROUP * k:GROUP * (k + 1), :]
                    dve.tensor_tensor(part, part, buf[:, GROUP * k:GROUP * (k + 1), :], ALU.add).then_inc(added, 1)
                dve.wait_ge(added, NT // GROUP)


ARRAYS = {
    "x": "x", "src": "src", "dst": "dst",
    "Wq": "L0_gnn_Wq", "bq": "L0_gnn_bq", "Wk": "L0_gnn_Wk", "bk": "L0_gnn_bk", "Wv": "L0_gnn_Wv", "bv": "L0_gnn_bv",
    "Wo": "L0_gnn_Wo", "bo": "L0_gnn_bo",
    "Wr": "L0_ffn_Wr", "br": "L0_ffn_br", "ln_g": "L0_ffn_ln_g", "ln_b": "L0_ffn_ln_b",
    "W1": "L0_ffn_W1", "b1": "L0_ffn_b1", "W2": "L0_ffn_W2", "b2": "L0_ffn_b2",
    "gW0": "L1_gnn_W0", "a_src0": "L1_gnn_a_src0", "a_dst0": "L1_gnn_a_dst0", "gb0": "L1_gnn_b0",
    "gW1": "L1_gnn_W1", "a_src1": "L1_gnn_a_src1", "a_dst1": "L1_gnn_a_dst1", "gb1": "L1_gnn_b1",
    "sW1": "L1_ffn_sW1", "sb1": "L1_ffn_sb1", "sW2": "L1_ffn_sW2", "sb2": "L1_ffn_sb2", "sW3": "L1_ffn_sW3", "sb3": "L1_ffn_sb3",
    "eW1": "L1_ffn_eW1", "eb1": "L1_ffn_eb1", "eW2": "L1_ffn_eW2", "eb2": "L1_ffn_eb2", "eW3": "L1_ffn_eW3", "eb3": "L1_ffn_eb3",
    "gW": "L1_ffn_gW", "gb": "L1_ffn_gb",
}


def head_major(v, axis):
    v = np.moveaxis(v, axis, -1)
    v = v.reshape(v.shape[:-1] + (D // QH, QH)).swapaxes(-1, -2).reshape(v.shape)
    return np.ascontiguousarray(np.moveaxis(v, -1, axis))


def kernel(**inputs):
    import concourse.bacc as bacc
    from concourse.bass_utils import run_bass_kernel_spmd

    nc = bacc.Bacc("TRN2", target_bir_lowering=False, num_devices=1)
    arrays, a = {}, Names()
    for name, full in ARRAYS.items():
        v = np.ascontiguousarray(inputs[full])
        if name in ("Wq", "Wk", "Wv", "bq", "bk", "bv"):
            v = head_major(v, v.ndim - 1)
        if name == "Wo":
            v = head_major(v, 0)
        arrays[f"in_{name}"] = v
        vars(a)[name] = nc.dram_tensor(f"in_{name}", v.shape, mybir.dt.from_np(v.dtype), kind="ExternalInput").ap()
    out = nc.dram_tensor("out", (N_NODES, D), F32, kind="ExternalOutput").ap()
    program(nc, a, out)
    r = run_bass_kernel_spmd(nc, [arrays], core_ids=[0])
    return r.results[0]["out"]
```

```python
import concourse.bass as bass
from concourse import mybir
from contextlib import ExitStack
import numpy as np

F32, BF16, F16, I32 = mybir.dt.float32, mybir.dt.bfloat16, mybir.dt.float16, mybir.dt.int32
ALU, ACT, AX = mybir.AluOpType, mybir.ActivationFunctionType, mybir.AxisListType

P = 128
N_NODES, N_EDGES = 3125, 53125
NT = -(-N_NODES // P)
NPAD = NT * P
DUMMY = 15 * P
TABLE_ROWS = NPAD + P
ROUNDS = 4
ROWE = 512
EROWS = -(-N_EDGES // ROWE)
EX = ROWE // P
CHAINS = 8
EU = EROWS // CHAINS
ETILES = EROWS * EX
WIN = 512
MAX_CHUNKS = (N_EDGES + 3 * NT + 4 * NT) // ROUNDS + 1
MAX_WIN = -(-MAX_CHUNKS * ROUNDS // WIN)
MAX_CHUNKS = MAX_WIN * WIN // ROUNDS
KEY_PAD = 4095
RMAX = bass.bass_isa.ReduceOp.max


def table_row(t):
    return (t + (1 if t >= DUMMY // P else 0)) * P


MANY_SEMS = 100


class Mem:

    past = []

    def __init__(self, nc, name):
        self.nc, self.name, self.stack, self.sems = nc, name, ExitStack(), []

    def __enter__(self):
        self.stack.__enter__()
        return self

    def __exit__(self, *a):
        self.past.extend(self.sems)
        if len(self.past) > MANY_SEMS:
            self.nc.clear_and_free_semaphores(self.past)
            self.nc.all_engine_barrier()
            self.past.clear()
        return self.stack.__exit__(*a)

    def sb(self, name, shape, dt=F32):
        return self.stack.enter_context(self.nc.sbuf_tensor(f"{self.name}_{name}", shape, dt))

    def ps(self, name, shape, dt=F32):
        return self.stack.enter_context(self.nc.psum_tensor(f"{self.name}_{name}", shape, dt))

    def sem(self, name):
        self.sems.append(self.nc.alloc_semaphore(name=f"{self.name}_{name}"))
        return self.sems[-1]


def build_constants(nc, c):
    with Mem(nc, "cst") as m:
        made, seen = m.sem("made"), m.sem("seen")
        with nc.Block() as block:
            @block.gpsimd
            def _(pool):
                pool.iota(c.lane_f[:, :], pattern=[[0, 1]], base=0, channel_multiplier=1,
                          allow_small_or_imprecise_dtypes=True).then_inc(made, 1)
                pool.iota(c.iota_f[:, :], pattern=[[1, WIN]], base=0, channel_multiplier=0,
                          allow_small_or_imprecise_dtypes=True).then_inc(made, 1)
                pool.memset(c.ident[:, :], 0.0).then_inc(made, 1)
                pool.memset(c.order_bias[:, :], 0.0).then_inc(made, 1)
                pool.memset(c.ones[:, :], 1.0).then_inc(made, 1)
                pool.memset(c.ones_b[:, :], 1.0).then_inc(made, 1)
                pool.memset(c.before[:, :], 1.0).then_inc(made, 1)
                pool.memset(c.zeros[:, :], 0.0).then_inc(made, 1)
                pool.wait_ge(made, 8)
                pool.affine_select(out=c.ident[:, :], in_=c.ident[:, :], compare_op=ALU.not_equal, fill=1.0,
                                   base=0, pattern=[[-1, P]], channel_multiplier=1).then_inc(made, 1)
                pool.affine_select(out=c.order_bias[:, :], in_=c.order_bias[:, :], compare_op=ALU.is_gt, fill=-2.0,
                                   base=0, pattern=[[1, P]], channel_multiplier=-1).then_inc(made, 1)
                pool.affine_select(out=c.before[:, :], in_=c.before[:, :], compare_op=ALU.is_gt, fill=0.0,
                                   base=0, pattern=[[1, P]], channel_multiplier=-1).then_inc(made, 1)

            @block.vector
            def _(dve):
                dve.wait_ge(made, 11)
                dve.tensor_copy(c.ident_b[:, :], c.ident[:, :]).then_inc(seen, 1)
                dve.tensor_copy(c.iota_b[:, :], c.iota_f[:, 0:P]).then_inc(seen, 1)
                dve.tensor_copy(c.iota_h[:, :], c.iota_f[:, :]).then_inc(seen, 1)


def build_neighbour_table(nc, c, g, key_in, val_in):
    with Mem(nc, f"ix{g.name}") as m:
        lo_c = m.sb("lo_c", [P, EU, EX, CHAINS], BF16)
        hi_c = m.sb("hi_c", [P, EU, EX, CHAINS], BF16)
        val_c = m.sb("val_c", [P, EU, EX, CHAINS])
        oh_lo = m.sb("oh_lo", [P, EU, EX * CHAINS, P], BF16)
        oh_hi = m.sb("oh_hi", [P, EU, EX * CHAINS, NT], BF16)
        zeros = m.sb("zeros", [P, WIN], BF16)
        place = m.sb("place", [P, EU, EX, CHAINS, 3])
        col = m.sb("col", [P, EU, EX, CHAINS])
        start = m.sb("start", [P, CHAINS, NT])
        lane_of = m.sb("lane_of", [P, NT])

        edges_in, parts, split, turned, evacuated = (m.sem(x) for x in ("edges_in", "parts", "split", "turned", "evac"))
        ohs, counted, padded = m.sem("ohs"), m.sem("counted"), m.sem("padded")

        full = EROWS - 1
        rest = N_EDGES - full * ROWE
        with Mem(nc, f"ixa{g.name}") as a:
            turn = [a.ps(f"turn{k}", [P, EX, P]) for k in range(3)]
            hist = a.ps("hist", [P, 512])
            with Mem(nc, f"ixr{g.name}") as r:
                key_i, val_i = r.sb("key_i", [EROWS, ROWE], I32), r.sb("val_i", [EROWS, ROWE], I32)
                lo_i, hi_i = r.sb("lo_i", [EROWS, ROWE], I32), r.sb("hi_i", [EROWS, ROWE], I32)
                part_f = r.sb("part_f", [EROWS, 3, ROWE])
                part_b = r.sb("part_b", [EROWS, 2, ROWE], BF16)
                above = r.sb("above", [EROWS, ROWE])
                with nc.Block() as block:
                    @block.sync
                    def _(sp):
                        sp.wait_ge(padded, 2)
                        for src, dst in ((key_in, key_i), (val_in, val_i)):
                            sp.dma_start(dst[0:full, :], src[0:full * ROWE].rearrange("(p e) -> p e", e=ROWE)).then_inc(edges_in, 16)
                            sp.dma_start(dst[full:EROWS, 0:rest], src[full * ROWE:N_EDGES].rearrange("(p e) -> p e", p=1)).then_inc(edges_in, 16)
                        sp.wait_ge(split, 1)
                        sp.dma_start(g.key_parts.rearrange("h (p e) -> p h e", e=ROWE), part_b[:, :, :]).then_inc(parts, 16)
                        sp.wait_ge(parts, 16)

                    @block.vector
                    def _(dve):
                        dve.memset(key_i[:, :], KEY_PAD).then_inc(padded, 1)
                        dve.memset(val_i[:, :], 0).then_inc(padded, 1)
                        dve.memset(zeros[:, :], 0.0).then_inc(padded, 1)
                        dve.wait_ge(edges_in, 64)
                        dve.tensor_single_scalar(lo_i[:, :], key_i[:, :], P - 1, ALU.bitwise_and).then_inc(counted, 1)
                        dve.tensor_single_scalar(hi_i[:, :], key_i[:, :], 7, ALU.logical_shift_right).then_inc(counted, 1)
                        dve.tensor_scalar(above[:, :], val_i[:, :], float(DUMMY), float(P), ALU.is_ge, ALU.mult).then_inc(counted, 1)
                        dve.wait_ge(counted, 3)
                        dve.tensor_copy(part_f[:, 0, :], lo_i[:, :]).then_inc(counted, 1)
                        dve.tensor_copy(part_f[:, 1, :], hi_i[:, :]).then_inc(counted, 1)
                        dve.scalar_tensor_tensor(part_f[:, 2, :], above[:, :], -float(DUMMY), val_i[:, :],
                                                 ALU.add, ALU.add).then_inc(counted, 1)
                        dve.wait_ge(counted, 6)
                        dve.scalar_tensor_tensor(part_f[:, 2, :], key_i[:, :], float(NPAD), part_f[:, 2, :],
                                                 ALU.is_lt, ALU.mult).then_inc(counted, 1)
                        dve.tensor_copy(part_b[:, :, :], part_f[:, 0:2, :]).then_inc(split, 1)
                        dve.wait_ge(turned, 1)
                        for k, out in enumerate((lo_c, hi_c, val_c)):
                            for x in range(EX):
                                dve.tensor_copy(out[:, :, x, :],
                                                turn[k][:, x, 0:EROWS].rearrange("p (q u) -> p u q", u=EU)).then_inc(evacuated, 1)
                        dve.wait_ge(evacuated, 3 * EX)
                        with dve.Fori(0, EU) as u:
                            dve.tensor_tensor(oh_lo[:, bass.ds(u, 1), :, :].rearrange("p a t l -> p (a t) l"),
                                              lo_c[:, bass.ds(u, 1), :, :].rearrange("p a x q -> p (a x q)").unsqueeze(2).to_broadcast([P, EX * CHAINS, P]),
                                              c.iota_b[:, :].unsqueeze(1).to_broadcast([P, EX * CHAINS, P]),
                                              ALU.is_equal).then_inc(ohs, 1)
                            dve.tensor_tensor(oh_hi[:, bass.ds(u, 1), :, :].rearrange("p a t l -> p (a t) l"),
                                              hi_c[:, bass.ds(u, 1), :, :].rearrange("p a x q -> p (a x q)").unsqueeze(2).to_broadcast([P, EX * CHAINS, NT]),
                                              c.iota_b[:, 0:NT].unsqueeze(1).to_broadcast([P, EX * CHAINS, NT]),
                                              ALU.is_equal).then_inc(ohs, 1)

                    @block.tensor
                    def _(pe):
                        pe.wait_ge(counted, 7)
                        for k in range(3):
                            for x in range(EX):
                                last = pe.transpose(turn[k][:, x, 0:EROWS], part_f[:, k, x * P:(x + 1) * P], c.ident[0:EROWS, 0:EROWS])
                        last.then_inc(turned, 1)
                        pe.wait_ge(padded, 3)
                        pe.matmul(hist[:, 0:CHAINS * NT], zeros[:, 0:P], zeros[:, 0:CHAINS * NT], start=True, stop=True)
                        with pe.Fori(0, EU) as u:
                            pe.wait_ge(ohs, u * 2 + 2)
                            for t in range(EX * CHAINS):
                                q = t % CHAINS
                                last = pe.matmul(hist[:, q * NT:(q + 1) * NT],
                                                 oh_lo[:, bass.ds(u, 1), t, :].rearrange("p a l -> p (a l)"),
                                                 oh_hi[:, bass.ds(u, 1), t, :].rearrange("p a l -> p (a l)"),
                                                 start=False, stop=True, skip_group_check=True)
                            last.then_inc(g.hist_done, 1)

            counts = a.sb("counts", [P, CHAINS, NT])
            deg = a.sb("deg", [P, NT])
            skey = a.sb("skey", [P, NT])
            keys_bc = a.sb("keys_bc", [P, NPAD])
            junk = [a.sb(f"junk{k}", [P, NPAD], BF16) for k in range(2)]
            above_v, sign_v = a.sb("above_v", [P, NT]), a.sb("sign_v", [P, NT])
            nskey = a.sb("nskey", [P, NT])
            node_f = a.sb("node_f", [P, NT])
            rank_i = a.sb("rank_i", [P, 3, NT], I32)
            rank_f = a.sb("rank_f", [P, 3, NT])
            oh_lane = a.sb("oh_lane", [P, NT, P])
            oh_tile = a.sb("oh_tile", [P, NT, NT])
            oh_val = a.sb("oh_val", [P, NT, 2, NT])
            sorted_ps = a.ps("sorted", [P, 2 * NT])
            sdeg, mdeg = a.sb("sdeg", [P, NT]), a.sb("mdeg", [P, NT])
            ch_i, ch_f = a.sb("ch_i", [P, NT], I32), a.sb("ch_f", [P, NT])
            cum = a.sb("cum", [P, NT + 1])
            pick = a.sb("pick", [P, NT, NT])
            base_of = a.sb("base_of", [P, NT])
            above_n = a.sb("above_n", [P, NT])
            CPL = MAX_CHUNKS // P
            chunk_f, tile_f, tile_i = a.sb("chunk_f", [P, CPL]), a.sb("tile_f", [P, CPL]), a.sb("tile_i", [P, CPL], I32)
            tile_past = a.sb("tile_past", [P, CPL, NT])
            tiled = a.sem("tiled")
            n_dve = NT // 2
            chain, keyed, key_out, key_bc, signs, ranked, sums, maxed = (
                a.sem(x) for x in ("chain", "keyed", "key_out", "key_bc", "signs", "ranked", "sums", "maxed"))
            with nc.Block() as block:
                @block.gpsimd
                def _(pool):
                    pool.iota(node_f[:, :], pattern=[[P, NT]], base=0, channel_multiplier=1,
                              allow_small_or_imprecise_dtypes=True).then_inc(keyed, 1)
                    pool.iota(chunk_f[:, :], pattern=[[1, CPL]], base=0, channel_multiplier=CPL,
                              allow_small_or_imprecise_dtypes=True).then_inc(keyed, 1)
                    pool.wait_ge(maxed, 1)
                    pool.partition_all_reduce(mdeg[:, :], sdeg[:, :], P, RMAX).then_inc(maxed, 1)

                @block.vector
                def _(dve):
                    n = [0]

                    def step(ins):
                        n[0] += 1
                        ins.then_inc(chain, 1)
                        dve.wait_ge(chain, n[0])

                    dve.wait_ge(g.hist_done, EU)
                    step(dve.tensor_copy(counts[:, :, :], hist[:, 0:CHAINS * NT].rearrange("p (q t) -> p q t", t=NT)))
                    step(dve.tensor_reduce(deg[:, :], counts[:, :, :].rearrange("p q t -> p t q"), AX.X, ALU.add))
                    dve.wait_ge(keyed, 2)
                    step(dve.tensor_scalar(skey[:, :], deg[:, :], 4000.0, 4096.0, ALU.min, ALU.mult))
                    step(dve.tensor_tensor(skey[:, :], skey[:, :], node_f[:, :], ALU.add))
                    dve.tensor_scalar(nskey[:, :], skey[:, :], -1.0, None, ALU.mult).then_inc(keyed, 1)
                    step(dve.memset(start[:, 0, :], 0.0))
                    for q in range(1, CHAINS):
                        step(dve.tensor_tensor(start[:, q, :], start[:, q - 1, :], counts[:, q - 1, :], ALU.add))
                    dve.wait_ge(key_bc, 16)
                    for t in range(n_dve):
                        if t >= 2:
                            dve.wait_ge(ranked, t - 1)
                        dve.tensor_scalar(junk[0][:, :], keys_bc[:, :], skey[:, t:t + 1], 0.0, ALU.is_gt, ALU.add,
                                          accum_out=above_v[:, t:t + 1]).then_inc(ranked, 1)
                        dve.wait_ge(ranked, t + 1)
                    dve.wait_ge(signs, NT - n_dve)
                    step(dve.tensor_scalar(above_v[:, n_dve:NT], sign_v[:, n_dve:NT], float(NPAD - 1), 0.5, ALU.add, ALU.mult))
                    step(dve.tensor_copy(rank_i[:, 0, :], above_v[:, :]))
                    step(dve.tensor_single_scalar(rank_i[:, 1, :], rank_i[:, 0, :], P - 1, ALU.bitwise_and))
                    step(dve.tensor_single_scalar(rank_i[:, 2, :], rank_i[:, 0, :], 7, ALU.logical_shift_right))
                    step(dve.tensor_copy(rank_f[:, :, :], rank_i[:, :, :]))
                    step(dve.tensor_copy(lane_of[:, :], rank_f[:, 1, :]))
                    step(dve.tensor_tensor(oh_lane[:, :, :], rank_f[:, 1, :].unsqueeze(2).to_broadcast([P, NT, P]),
                                           c.iota_f[:, 0:P].unsqueeze(1).to_broadcast([P, NT, P]), ALU.is_equal))
                    step(dve.tensor_tensor(oh_tile[:, :, :], rank_f[:, 2, :].unsqueeze(2).to_broadcast([P, NT, NT]),
                                           c.iota_f[:, 0:NT].unsqueeze(1).to_broadcast([P, NT, NT]), ALU.is_equal))
                    step(dve.tensor_scalar(above_n[:, :], node_f[:, :], float(DUMMY), float(P), ALU.is_ge, ALU.mult))
                    step(dve.tensor_tensor(above_n[:, :], above_n[:, :], node_f[:, :], ALU.add))
                    step(dve.tensor_tensor(oh_val[:, :, 0, :], oh_tile[:, :, :],
                                           above_n[:, :].unsqueeze(2).to_broadcast([P, NT, NT]), ALU.mult))
                    step(dve.tensor_tensor(oh_val[:, :, 1, :], oh_tile[:, :, :],
                                           deg[:, :].unsqueeze(2).to_broadcast([P, NT, NT]), ALU.mult))
                    dve.sem_inc(ranked, 1)
                    dve.wait_ge(sums, 1)
                    step(dve.tensor_copy(g.order[:, :], sorted_ps[:, 0:NT]))
                    dve.tensor_copy(sdeg[:, :], sorted_ps[:, NT:2 * NT]).then_inc(maxed, 1)
                    dve.wait_ge(maxed, 2)
                    step(dve.tensor_scalar(ch_f[:, :], mdeg[:, :], float(ROUNDS - 1), float(ROUNDS), ALU.add, ALU.max))
                    step(dve.tensor_copy(ch_i[:, :], ch_f[:, :]))
                    step(dve.tensor_single_scalar(ch_i[:, :], ch_i[:, :], 2, ALU.logical_shift_right))
                    step(dve.tensor_copy(ch_f[:, :], ch_i[:, :]))
                    step(dve.memset(cum[:, 0:1], 0.0))
                    step(dve.tensor_tensor_scan(cum[:, 1:NT + 1], c.ones[:, 0:NT], ch_f[:, :], 0.0, ALU.mult, ALU.add))
                    step(dve.tensor_copy(g.first_chunk[:, :], cum[:, :]))
                    step(dve.tensor_tensor(tile_past[:, :, :], chunk_f[:, :].unsqueeze(2).to_broadcast([P, CPL, NT]),
                                           cum[:, 1:NT + 1].unsqueeze(1).to_broadcast([P, CPL, NT]), ALU.is_ge))
                    step(dve.tensor_reduce(tile_f[:, :], tile_past[:, :, :], AX.X, ALU.add))
                    step(dve.tensor_scalar(tile_f[:, :], tile_f[:, :], float(NT - 1), None, ALU.min))
                    dve.tensor_copy(tile_i[:, :], tile_f[:, :]).then_inc(tiled, 1)
                    step(dve.tensor_scalar(cum[:, :], cum[:, :], float(ROUNDS), None, ALU.mult))
                    step(dve.tensor_tensor(pick[:, :, :], oh_tile[:, :, :],
                                           cum[:, 0:NT].unsqueeze(1).to_broadcast([P, NT, NT]), ALU.mult))
                    step(dve.tensor_reduce(base_of[:, :], pick[:, :, :], AX.X, ALU.add))
                    step(dve.tensor_tensor(start[:, :, :], start[:, :, :],
                                           base_of[:, :].unsqueeze(1).to_broadcast([P, CHAINS, NT]), ALU.add))

                @block.sync
                def _(sp):
                    sp.wait_ge(keyed, 3)
                    sp.dma_start(g.sort_keys.rearrange("(p t) -> p t", t=NT), skey[:, :]).then_inc(key_out, 16)
                    sp.wait_ge(key_out, 16)
                    sp.dma_start(keys_bc[:, :], g.sort_keys.rearrange("(a n) -> a n", a=1).to_broadcast([P, NPAD])).then_inc(key_bc, 16)
                    sp.wait_ge(tiled, 1)
                    sp.dma_start(g.tile_of.rearrange("(p n) -> p n", p=P), tile_i[:, :]).then_inc(key_out, 16)
                    sp.wait_ge(key_out, 32)

                @block.scalar
                def _(act):
                    act.wait_ge(keyed, 3)
                    act.wait_ge(key_bc, 16)
                    for k, t in enumerate(range(n_dve, NT)):
                        act.activation(junk[1][:, :], keys_bc[:, :], ACT.Sign, bias=nskey[:, t:t + 1],
                                       accum_out=sign_v[:, t:t + 1]).then_inc(signs, 1)
                        act.wait_ge(signs, k + 1)

                @block.tensor
                def _(pe):
                    pe.wait_ge(ranked, n_dve + 1)
                    for t in range(NT):
                        last = pe.matmul(sorted_ps[:, :], oh_lane[:, t, :], oh_val[:, t, :, :].rearrange("p a b -> p (a b)"),
                                         start=(t == 0), stop=(t == NT - 1))
                    last.then_inc(sums, 1)

        with Mem(nc, f"ixb{g.name}") as b:
            run = b.ps("run", [P, 512])
            same = b.ps("same", [P, 2, CHAINS, P])
            found = b.ps("found", [P, 2, 512])
            parts_bc = b.sb("parts_bc", [P, 2, CHAINS, ROWE], BF16)
            ohT_lo = b.sb("ohT_lo", [P, 2, CHAINS, ROWE], BF16)
            ohT_hi = b.sb("ohT_hi", [NT, 2, CHAINS, ROWE], BF16)
            snap = b.sb("snap", [P, 2, CHAINS, 3 * NT], BF16)
            earlier = b.sb("earlier", [P, 2, CHAINS, P], BF16)
            pick = b.sb("pick", [P, 2, CHAINS, 3, NT])
            bc_in = b.sem("bc_in")
            (begun, ohT_ready, snap_hi, snap_lo, same_ready, earlier_ready, found_ready, late_ready,
             picked, reduced, advanced, filled) = (
                b.sem(x) for x in ("begun", "ohT_ready", "snap_hi", "snap_lo", "same_ready",
                                   "earlier_ready", "found_ready", "late_ready", "picked", "reduced", "advanced", "filled"))
            kp = g.key_parts.rearrange("h (q u e) -> h q u e", q=CHAINS, e=ROWE)
            last_u = EU - 1
            HALF = CHAINS // 2

            def row_loop(eng, row):
                row(0, 0, True)
                with eng.Fori(0, EU // 2) as i:
                    for k in (1, 2):
                        row(i * 2 + k, k % 2, False)

            with nc.Block() as block:
                @block.sync
                def _(sp):
                    def load_row(r):
                        for h in range(2):
                            sp.dma_start(parts_bc[:, h, :, :],
                                         kp[h, :, bass.ds(r % EU, 1), :].rearrange("q a e -> (q a) e").unsqueeze(0).to_broadcast([P, CHAINS, ROWE])).then_inc(bc_in, 16)

                    load_row(0)
                    with sp.Fori(1, EU + 1) as r:
                        sp.wait_ge(ohT_ready, r * 2)
                        sp.sem_inc(g.passed, 1)
                        load_row(r)

                @block.scalar
                def _(act):
                    act.wait_ge(begun, 1)
                    act.sem_inc(late_ready, 2)
                    with act.Fori(0, EU) as u:
                        for x in range(EX):
                            s = u * EX + (x + 1)
                            k = x % 2
                            act.wait_ge(advanced, s)
                            act.activation(snap[:, k, :, 0:NT], run[:, 0:CHAINS * NT].rearrange("p (q t) -> p q t", t=NT),
                                           ACT.Copy).then_inc(snap_hi, 1)
                            act.wait_ge(same_ready, s)
                            act.activation(earlier[:, k, HALF:, :], same[:, k, HALF:, :], ACT.Relu, bias=c.minus1[:, 0:1]).then_inc(late_ready, 1)

                @block.vector
                def _(dve):
                    dve.memset(c.minus1[:, :], -1.0).then_inc(filled, 1)
                    for k in range(2):
                        dve.tensor_copy(snap[:, k, :, 2 * NT:3 * NT],
                                        lane_of[:, :].unsqueeze(1).to_broadcast([P, CHAINS, NT])).then_inc(filled, 1)
                    dve.wait_ge(filled, 3)
                    dve.sem_inc(begun, 1)
                    dve.sem_inc(picked, 6)
                    dve.sem_inc(earlier_ready, 2)

                    def low_one_hots(r, rk):
                        dve.wait_ge(bc_in, r * 32 + 32)
                        dve.tensor_scalar(ohT_lo[:, rk, :, :],
                                          parts_bc[:, 0, :, :], c.lane_f[:, 0:1], None, ALU.is_equal).then_inc(ohT_ready, 1)

                    def high_one_hots(r, rk):
                        dve.tensor_scalar(ohT_hi[:, rk, :, :],
                                          parts_bc[0:NT, 1, :, :], c.lane_f[0:NT, 0:1], None, ALU.is_equal).then_inc(ohT_ready, 1)

                    def pick_places(u, x, n):
                        k = x % 2
                        dve.wait_ge(found_ready, n)
                        for half in range(2):
                            oh = oh_hi[:, bass.ds(u, 1), x * CHAINS + 4 * half:x * CHAINS + 4 * half + 4, :]
                            oh = oh.rearrange("p a t l -> p (a t) l").unsqueeze(2).to_broadcast([P, 4, 3, NT])
                            dve.tensor_tensor(pick[:, k, 4 * half:4 * half + 4, :, :],
                                              found[:, half, 0:4 * 3 * NT].rearrange("p (q r t) -> p q r t", r=3, t=NT),
                                              oh, ALU.mult).then_inc(picked, 1)

                    def sum_places(u, x, n):
                        k = x % 2
                        dve.wait_ge(picked, n * 2 + 2)
                        dve.tensor_reduce(place[:, bass.ds(u, 1), x, :, :].rearrange("p a q r -> p (a q) r"),
                                          pick[:, k, :, :, :].rearrange("p q r t -> p (q r) t"), AX.X, ALU.add).then_inc(reduced, 1)

                    def row(u, uk, first):
                        for x in range(EX):
                            s = u * EX + (x + 1)
                            k = x % 2
                            dve.wait_ge(snap_hi, s)
                            dve.tensor_tensor(snap[:, k, :, NT:2 * NT], run[:, 0:CHAINS * NT].rearrange("p (q t) -> p q t", t=NT),
                                              snap[:, k, :, 0:NT], ALU.subtract).then_inc(snap_lo, 1)
                            back = (u, x - 2) if x >= 2 else (u - 1, x + 2)
                            if x >= 2 or not first:
                                pick_places(*back, s)
                            dve.wait_ge(same_ready, s)
                            dve.scalar_tensor_tensor(earlier[:, k, 0:HALF, :], same[:, k, 0:HALF, :], 1.5,
                                                     c.before[:, :].unsqueeze(1).to_broadcast([P, HALF, P]), ALU.is_ge, ALU.mult).then_inc(earlier_ready, 1)
                            if x >= 2 or not first:
                                sum_places(*back, s)
                            if x == 1:
                                if first:
                                    dve.wait_ge(found_ready, 2)
                                low_one_hots(u + 1, 1 - uk)
                            if x == 2:
                                high_one_hots(u + 1, 1 - uk)

                    low_one_hots(0, 0)
                    high_one_hots(0, 0)
                    row_loop(dve, row)
                    for x in (2, 3):
                        pick_places(last_u, x, EU * EX + x - 1)
                        sum_places(last_u, x, EU * EX + x - 1)

                @block.tensor
                def _(pe):
                    def mark_same(uk, x, n):
                        pe.wait_ge(earlier_ready, n)
                        pe.wait_ge(late_ready, n)
                        for q in range(CHAINS):
                            tl = ohT_lo[:, uk, q, x * P:(x + 1) * P]
                            th = ohT_hi[:, uk, q, x * P:(x + 1) * P]
                            pe.matmul(same[:, x % 2, q, :], tl, tl, start=True, stop=False, skip_group_check=True)
                            last = pe.matmul(same[:, x % 2, q, :], th, th, start=False, stop=(q < HALF), skip_group_check=True)
                            if q >= HALF:
                                last = pe.matmul(same[:, x % 2, q, :], c.ident_b[:, :], c.order_bias[:, :], start=False, stop=True, skip_group_check=True)
                        last.then_inc(same_ready, 1)

                    def find(uk, x, n):
                        k = x % 2
                        pe.wait_ge(earlier_ready, n + 1)
                        pe.wait_ge(late_ready, n + 1)
                        pe.wait_ge(picked, n * 2 + 2)
                        for q in range(CHAINS):
                            out = found[:, q // 4, (q % 4) * 3 * NT:(q % 4 + 1) * 3 * NT]
                            tl = ohT_lo[:, uk, q, x * P:(x + 1) * P]
                            pe.matmul(out, tl, snap[:, k, q, :], start=True, stop=False, skip_group_check=True)
                            last = pe.matmul(out[:, NT:2 * NT], earlier[:, k, q, :], c.ones_b[:, 0:NT], start=False, stop=True, skip_group_check=True)
                        last.then_inc(found_ready, 1)

                    def advance(u, x, n):
                        pe.wait_ge(snap_lo, n)
                        for q in range(CHAINS):
                            last = pe.matmul(run[:, q * NT:(q + 1) * NT], oh_lo[:, bass.ds(u, 1), x * CHAINS + q, :].rearrange("p a l -> p (a l)"),
                                             oh_hi[:, bass.ds(u, 1), x * CHAINS + q, :].rearrange("p a l -> p (a l)"), start=False, stop=True, skip_group_check=True)
                        last.then_inc(advanced, 1)

                    def row(u, uk, first):
                        for x in range(EX):
                            n = u * EX + (x + 1)
                            if x == 0:
                                pe.wait_ge(ohT_ready, u * 2 + 2)
                            mark_same(uk, x, n)
                            if x > 0:
                                find(uk, x - 1, n)
                            elif not first:
                                find(1 - uk, EX - 1, n)
                            advance(u, x, n)

                    pe.matmul(run[:, 0:CHAINS * NT], c.ident[:, :], start[:, :, :].rearrange("p q t -> p (q t)"),
                              start=True, stop=True).then_inc(advanced, 1)
                    pe.wait_ge(filled, 3)
                    pe.sem_inc(found_ready, 2)
                    row_loop(pe, row)
                    find(last_u % 2, EX - 1, EU * EX + 1)

        with Mem(nc, f"ixc{g.name}") as d:
            window = d.ps("window", [P, WIN])
            RING = 8
            BATCH = 16
            oh_p, off_p = d.sb("oh_p", [P, 2, BATCH, P], F16), d.sb("off_p", [P, 2, BATCH, P], F16)
            oh_c = [d.sb(f"oh_c{k}", [P, WIN], F16) for k in range(RING)]
            lane_e = d.sb("lane_e", [P, ETILES], F16)
            table_i = d.sb("table_i", [P, WIN], I32)
            n_win = d.sb("n_win", [P, 1], I32)
            seq, made, apart, squared, laned, summed, stored = (
                d.sem(x) for x in ("seq", "made", "apart", "squared", "laned", "summed", "stored"))
            flat = lambda t: t[:, :, :, :].rearrange("p u x q -> p (u x q)")
            max_w = MAX_WIN
            with nc.Block() as block:
                @block.vector
                def _(dve):
                    dve.tensor_tensor(col[:, :, :, :], place[:, :, :, :, 0], place[:, :, :, :, 1], ALU.add).then_inc(seq, 1)
                    dve.tensor_copy(lane_e[:, :].rearrange("p (u x q) -> p u x q", u=EU, x=EX), place[:, :, :, :, 2]).then_inc(seq, 1)
                    dve.tensor_single_scalar(n_win[:, :], g.first_chunk[:, NT:NT + 1], WIN // ROUNDS - 1, ALU.add).then_inc(seq, 1)
                    dve.wait_ge(seq, 3)
                    dve.tensor_single_scalar(n_win[:, :], n_win[:, :], 7, ALU.logical_shift_right).then_inc(seq, 1)
                    dve.wait_ge(seq, 4)
                    dve.sem_inc(g.windows_known, 1)
                    wins = dve.value_load(n_win[0:1, 0:1], min_val=1, max_val=max_w)
                    with dve.Fori(0, wins) as w:
                        dve.wait_ge(seq, w + 4)
                        dve.sem_inc(g.passed, 1)
                        with dve.Fori(0, ETILES // BATCH) as i:
                            for k in range(BATCH):
                                n = w * ETILES + i * BATCH + k
                                col_e = flat(col)[:, bass.ds(i * BATCH + k, 1)]
                                dve.wait_ge(summed, n + (BATCH + 2 - RING))
                                dve.tensor_scalar(oh_c[k % RING][:, :], c.iota_h[:, :], col_e, flat(val_c)[:, bass.ds(i * BATCH + k, 1)],
                                                  ALU.is_equal, ALU.mult).then_inc(made, 1)
                        dve.wait_ge(summed, w * ETILES + (ETILES + BATCH + 1))
                        dve.wait_ge(stored, w * 16 + 16)
                        dve.tensor_scalar(table_i[:, :], window[:, :], float(DUMMY), None, ALU.add).then_inc(g.window_ready, 1)
                        dve.tensor_scalar(col[:, :, :, :], col[:, :, :, :], -float(WIN), None, ALU.add).then_inc(seq, 1)

                @block.tensor
                def _(pe):
                    pe.sem_inc(summed, BATCH + 1)
                    pe.wait_ge(g.windows_known, 1)
                    wins = pe.value_load(n_win[0:1, 0:1], min_val=1, max_val=max_w)
                    pe.sem_inc(g.window_ready, 1)
                    with pe.Fori(0, wins) as w:
                        pe.wait_ge(g.window_ready, w + 1)
                        pe.matmul(window[:, :], zeros[:, 0:P].bitcast(F16), zeros[:, :].bitcast(F16), start=True, stop=True)
                        with pe.Fori(0, ETILES // BATCH // 2) as i:
                            for b in range(2):
                                pe.wait_ge(laned, w * (ETILES // BATCH) + i * 2 + (b + 3))
                                pe.sem_inc(g.passed, 1)
                                for k in range(BATCH):
                                    n = w * ETILES + (i * 2 + b) * BATCH + k
                                    pe.wait_ge(made, n + 1)
                                    pe.matmul(window[:, :], oh_p[:, b, k, :], oh_c[k % RING][:, :], start=False, stop=True,
                                              skip_group_check=True).then_inc(summed, 1)

                @block.gpsimd
                def _(pool):
                    pool.wait_ge(g.windows_known, 1)
                    wins = pool.value_load(n_win[0:1, 0:1], min_val=1, max_val=max_w)
                    with pool.Fori(0, wins) as w:
                        with pool.Fori(0, ETILES // BATCH // 2) as i:
                            for b in range(2):
                                pool.wait_ge(laned, w * (ETILES // BATCH) + i * 2 + (b + 1))
                                pool.sem_inc(g.passed, 1)
                                pool.tensor_tensor(off_p[:, b, :, :], lane_e[:, bass.ds((i * 2 + b) * BATCH, BATCH)].unsqueeze(2).to_broadcast([P, BATCH, P]),
                                                   c.iota_h[:, 0:P].unsqueeze(1).to_broadcast([P, BATCH, P]), ALU.subtract).then_inc(apart, 1)

                @block.scalar
                def _(act):
                    act.wait_ge(g.windows_known, 1)
                    wins = act.value_load(n_win[0:1, 0:1], min_val=1, max_val=max_w)
                    act.sem_inc(laned, 2)
                    with act.Fori(0, wins) as w:
                        with act.Fori(0, ETILES // BATCH // 2) as i:
                            for b in range(2):
                                m = w * (ETILES // BATCH) + i * 2 + (b + 1)
                                act.wait_ge(apart, m)
                                act.activation(off_p[:, b, :, :], off_p[:, b, :, :], ACT.Square).then_inc(squared, 1)
                                act.wait_ge(squared, m)
                                act.wait_ge(summed, w * ETILES + (i * 2 + b) * BATCH + 1)
                                act.activation(oh_p[:, b, :, :], off_p[:, b, :, :], ACT.Relu, scale=-1.0, bias=c.ones[:, 0:1]).then_inc(laned, 1)

                @block.sync
                def _(sp):
                    sp.sem_inc(stored, 16)
                    sp.wait_ge(g.windows_known, 1)
                    wins = sp.value_load(n_win[0:1, 0:1], min_val=1, max_val=max_w)
                    with sp.Fori(0, wins) as w:
                        sp.wait_ge(g.window_ready, w + 2)
                        sp.sem_inc(g.passed, 1)
                        sp.dma_start(g.neighbours[bass.ds(w, 1), :, :].rearrange("a p c -> (a p) c"), table_i[:, :]).then_inc(stored, 16)
                    sp.wait_ge(stored, 16 * wins + 16)
                    sp.sem_inc(g.passed, 1)


D = 256
KC = D // P
GROUP = 5
EPS = 1e-5


def each_tile(eng, body, peel=1):
    with eng.Fori(0, (NT - peel) // 2) as i:
        for s in range(2):
            body(i * 2 + s, s)
    for t in range(NT - peel, NT):
        body(t, t % 2)


def norm_stats(nc, c, name, x, mean, inv):
    with Mem(nc, name) as m:
        stats = m.sb("stats", [P, NT, 6])
        std = m.sb("std", [P, NT])
        stat_done, aggr_done, std_done, inv_done = (m.sem(s) for s in ("stat", "aggr", "std", "inv"))
        with nc.Block() as block:
            @block.vector
            def _(dve):
                for t in range(NT):
                    dve.bn_stats(stats[:, t, :], x[:, t, :]).then_inc(stat_done, 1)
                dve.wait_ge(stat_done, NT)
                for t in range(NT):
                    dve.bn_aggr(mean[:, t, :], stats[:, t, :]).then_inc(aggr_done, 1)
                dve.wait_ge(std_done, 1)
                dve.reciprocal(inv[:, :], std[:, :]).then_inc(inv_done, 1)
                dve.wait_ge(inv_done, 1)

            @block.scalar
            def _(act):
                act.wait_ge(aggr_done, NT)
                act.activation(std[:, :], mean[:, :, 1], ACT.Sqrt, bias=c.eps[:, 0:1]).then_inc(std_done, 1)


def normalise(dve, out, x, mean, inv, t):
    if isinstance(t, int):
        return dve.tensor_scalar(out, x[:, t, :], mean[:, t, 0:1], inv[:, t:t + 1], ALU.subtract, ALU.mult)
    return dve.tensor_scalar(out, x[:, bass.ds(t, 1), :].rearrange("p a f -> p (a f)"),
                             mean[:, bass.ds(t, 1), 0:1].rearrange("p a f -> p (a f)"), inv[:, bass.ds(t, 1)],
                             ALU.subtract, ALU.mult)


def layernorm(nc, c, name, x, out):
    with Mem(nc, name) as m:
        mean, inv = m.sb("mean", [P, NT, 2]), m.sb("inv", [P, NT])
        norm_stats(nc, c, name + "s", x, mean, inv)
        normed = m.sem("normed")
        with nc.Block() as block:
            @block.vector
            def _(dve):
                for t in range(NT):
                    normalise(dve, out[:, t, :], x, mean, inv, t).then_inc(normed, 1)
                dve.wait_ge(normed, NT)


def project(nc, c, name, weights, bias, n_out, banks, a=None, norm=None, take_dve=None, store=None, n_stores=0, load=None,
            scatter=None):
    with Mem(nc, name) as m:
        rows = m.sb("rows", [P, 2, D])
        a_t = m.sb("a_t", [P, 2, KC, P])
        turn = m.ps("turn", [P, 2, 512])
        prod = m.ps("prod", [P, 2, banks, 512])
        per = n_out // banks
        loaded = [m.sem(f"loaded{k}") for k in range(NT // GROUP)]
        tiles_in, staged, turned, copied, multiplied, taken, stored = (
            m.sem(s) for s in ("tiles_in", "staged", "turned", "copied", "mult", "taken", "stored"))
        scattered = m.sem("scattered")

        def stage(eng, t, s):
            eng.wait_ge(turned, t + 1)
            if norm is not None:
                normalise(eng, rows[:, s, :], *norm, t).then_inc(staged, 1)
                return
            if load is not None:
                eng.wait_ge(tiles_in, t + 1)
            eng.activation(rows[:, s, :], a[:, bass.ds(t, 1), :].rearrange("p a f -> p (a f)"), ACT.Copy).then_inc(staged, 1)

        with nc.Block() as block:
            @block.sync
            def _(sp):
                if load is not None:
                    for k in range(NT // GROUP):
                        load(sp, k).then_inc(loaded[k], 16)
                    for k in range(NT // GROUP):
                        sp.wait_ge(loaded[k], 16)
                        sp.sem_inc(tiles_in, GROUP)
                if store is not None:
                    for k in range(NT // GROUP):
                        sp.wait_ge(taken, GROUP * (k + 1) + 2)
                        for ins in store(sp, k):
                            ins.then_inc(stored, 16)
                    sp.wait_ge(stored, 16 * (NT // GROUP) * n_stores)

            @block.gpsimd
            def _(pool):
                if scatter is not None:
                    for t in range(NT):
                        pool.wait_ge(taken, t + 3)
                        scatter(pool, t).then_inc(scattered, 16)
                    pool.wait_ge(scattered, 16 * NT)

            @block.tensor
            def _(pe):
                pe.sem_inc(multiplied, 2)
                pe.sem_inc(turned, 2)

                def turn_tile(t, s):
                    pe.wait_ge(staged, t + 1)
                    pe.wait_ge(copied, t + 1)
                    for h in range(KC):
                        last = pe.transpose(turn[:, s, h * P:(h + 1) * P], rows[:, s, h * P:(h + 1) * P], c.ident[:, :])
                    last.then_inc(turned, 1)

                def multiply(t, s):
                    pe.wait_ge(copied, t + 3)
                    pe.wait_ge(taken, t + 1)
                    for b in range(banks):
                        out = prod[:, s, b, 0:per]
                        for h in range(KC):
                            last = pe.matmul(out, a_t[:, s, h, :], weights[:, h, b * per:(b + 1) * per],
                                             start=(h == 0), stop=(bias is None and h == KC - 1))
                        if bias is not None:
                            last = pe.matmul(out, c.ones[0:1, :], bias[0:1, b * per:(b + 1) * per], start=False, stop=True)
                    last.then_inc(multiplied, 1)

                def tile(t, s):
                    if not (isinstance(t, int) and t == NT - 1):
                        turn_tile(t + 1, 1 - s)
                    multiply(t, s)

                turn_tile(0, 0)
                each_tile(pe, tile)

            @block.scalar
            def _(act):
                act.sem_inc(copied, 2)

                def tile(t, s):
                    act.wait_ge(turned, t + 3)
                    act.wait_ge(multiplied, t + 1)
                    act.activation(a_t[:, s, :, :].rearrange("p h n -> p (h n)"), turn[:, s, 0:D], ACT.Copy).then_inc(copied, 1)
                    if norm is None and not (isinstance(t, int) and t + 2 >= NT):
                        stage(act, t + 2, s)

                if norm is None:
                    for t in range(2):
                        stage(act, t, t)
                each_tile(act, tile, peel=3)

            @block.vector
            def _(dve):
                dve.sem_inc(taken, 2)

                def tile(t, s):
                    if norm is not None and not (isinstance(t, int) and t + 2 >= NT):
                        stage(dve, t + 2, s)
                    dve.wait_ge(multiplied, t + 3)
                    take_dve(dve, t, prod[:, s, :, :]).then_inc(taken, 1)

                if norm is not None:
                    for t in range(2):
                        stage(dve, t, t)
                each_tile(dve, tile, peel=3)


SLOTS = 4


def attend(nc, c, g, name, heads, own, own_table, table, width, out_table, qk, bias_row=None):
    h, dh = heads, D // heads
    av = dh + 1
    v0 = D + h if qk else 0
    act_rounds = ROUNDS // 2 if qk else 0
    dve_rounds = ROUNDS - act_rounds
    early = GROUP if qk else NT
    groups = NT // GROUP
    with Mem(nc, name) as m:
        rows = m.sb("rows", [P, SLOTS, ROUNDS, width])
        acc = m.sb("acc", [P, NT, h, av])
        peak = m.sb("peak", [P, NT, h])
        new_peak = m.sb("new_peak", [P, SLOTS, 1, h])
        idx = m.sb("idx", [P, SLOTS, ROUNDS], I32)
        tile_of = m.sb("tile_of", [1, MAX_CHUNKS], I32)
        score = m.sb("score", [P, SLOTS, ROUNDS + 1, h])
        wv = m.sb("wv", [P, SLOTS, ROUNDS + 1, h, av])
        recip = m.sb("recip", [P, 2, NT, h])
        part = m.ps("part", [P, SLOTS, 512])
        prod = m.sb("prod", [P, ROUNDS, D + h]) if qk else m.sb("prod", [P, ROUNDS, h])
        bias_bc = None if qk else m.sb("bias_bc", [P, D])
        idx_in = [m.sem(f"idx_in{k}") for k in range(SLOTS)]
        gathered = [m.sem(f"gathered{k}") for k in range(SLOTS)]
        (own_in, own_rest, chunk_ready, multiplied, summed, maxed, shifted, exped, weighted, act_weighted, peaked, kept, part_sum,
         rescaled, added, state_set, normed, scattered, passed, biased, gelued, bias_in, tiles_in, den) = (
            m.sem(s) for s in ("own_in", "own_rest", "chunk_ready", "multiplied", "summed", "maxed", "shifted",
                               "exped", "weighted", "act_weighted", "peaked", "kept", "part_sum", "rescaled", "added", "state_set",
                               "normed", "scattered", "passed", "biased", "gelued", "bias_in", "tiles_in", "den"))

        def blocks_of(eng):
            total = eng.value_load(g.first_chunk[0:1, NT:NT + 1], min_val=NT, max_val=MAX_CHUNKS)
            return eng.snap((total + (SLOTS - 1)) // SLOTS)

        with nc.Block() as block:
            @block.sync
            def _(sp):
                def load_idx(j, k):
                    sp.dma_start(idx[:, k, :], g.neighbours[bass.ds(j // (WIN // ROUNDS), 1), :, bass.ds((j % (WIN // ROUNDS)) * ROUNDS, ROUNDS)]
                                 .rearrange("a p c -> (a p) c")).then_inc(idx_in[k], 16)

                for k in range(SLOTS):
                    load_idx(k, k)
                sp.dma_start(tile_of[:, :], g.tile_of.rearrange("(a n) -> a n", a=1)).then_inc(tiles_in, 16)
                if not qk:
                    sp.dma_start(bias_bc[:, :], bias_row.rearrange("(a n) -> a n", a=1).to_broadcast([P, D])).then_inc(bias_in, 16)
                blocks = blocks_of(sp)
                with sp.Fori(1, blocks) as i:
                    for k in range(SLOTS):
                        sp.wait_ge(gathered[k], i * (16 * ROUNDS))
                        sp.sem_inc(chunk_ready, 1)
                        load_idx(i * SLOTS + k, k)
                for k in range(SLOTS):
                    sp.wait_ge(gathered[k], blocks * (16 * ROUNDS))
                    sp.sem_inc(chunk_ready, 1)

            @block.gpsimd
            def _(pool):
                def gather_own(ts, sem):
                    for t in ts:
                        pool.indirect_dma_start(out=own[:, t, :], out_offset=None, in_=own_table,
                                                in_offset=bass.IndirectOffsetOnAxis(ap=g.order[:, t:t + 1], axis=0)).then_inc(sem, 16)

                def gather_block(i):
                    for k in range(SLOTS):
                        pool.wait_ge(idx_in[k], i * 16 + 16)
                        pool.wait_ge(weighted, i * SLOTS + (k + 1))
                        if act_rounds:
                            pool.wait_ge(act_weighted, i * SLOTS + (k + 1))
                        pool.sem_inc(passed, 1)
                        for r in range(ROUNDS):
                            pool.indirect_dma_start(out=rows[:, k, r, :], out_offset=None, in_=table,
                                                    in_offset=bass.IndirectOffsetOnAxis(ap=idx[:, k, r:r + 1], axis=0)).then_inc(gathered[k], 16)

                if own_table is not None:
                    gather_own(range(early), own_in)
                gather_block(0)
                if own_table is not None:
                    gather_own(range(early, NT), own_rest)
                with pool.Fori(1, blocks_of(pool)) as i:
                    gather_block(i)
                for t in range(NT if out_table is not None else 0):
                    if t % GROUP == 0:
                        pool.wait_ge(normed if qk else gelued, t // GROUP + 1)
                    pool.indirect_dma_start(out=out_table, out_offset=bass.IndirectOffsetOnAxis(ap=g.order[:, t:t + 1], axis=0),
                                            in_=own[:, t, 0:D], in_offset=None).then_inc(scattered, 16)
                if out_table is not None:
                    pool.wait_ge(scattered, 16 * NT)

            @block.vector
            def _(dve):
                if qk:
                    dve.memset(peak[:, :, :], -1.0e30).then_inc(state_set, 1)
                    dve.memset(acc[:, :, :, :], 0.0).then_inc(state_set, 1)
                    dve.wait_ge(state_set, 2)
                    dve.wait_ge(own_in, 16 * early)
                else:
                    if own_table is not None:
                        dve.wait_ge(own_in, 16 * NT)
                    dve.tensor_tensor(recip[:, 0, :, :], own[:, :, D:D + h], own[:, :, D + h:D + 2 * h], ALU.add).then_inc(state_set, 1)
                    dve.tensor_copy(acc[:, :, :, 0:dh], own[:, :, 0:D].rearrange("p t (h d) -> p t h d", d=dh)).then_inc(state_set, 1)
                    dve.memset(acc[:, :, :, dh], 1.0).then_inc(state_set, 1)
                    dve.wait_ge(state_set, 3)
                    dve.scalar_tensor_tensor(peak[:, :, :], recip[:, 0, :, :], 0.2, recip[:, 0, :, :], ALU.mult, ALU.max).then_inc(state_set, 1)
                    dve.wait_ge(state_set, 4)
                dve.wait_ge(tiles_in, 16)
                dve.sem_inc(weighted, SLOTS)
                dve.sem_inc(added, 3)
                dve.sem_inc(rescaled, 2)
                dve.sem_inc(kept, 1)
                blocks = blocks_of(dve)

                def tile_at(j):
                    return dve.value_load(tile_of[0:1, bass.ds(j, 1)], min_val=0, max_val=NT - 1)

                def begin_scores(k, n, t):
                    row = rows[:, k, :, :]
                    dve.wait_ge(kept, n)
                    dve.tensor_copy(score[:, k, ROUNDS:ROUNDS + 1, :], peak[:, bass.ds(t, 1), :]).then_inc(peaked, 1)
                    dve.wait_ge(chunk_ready, n)
                    if qk:
                        q = own[:, bass.ds(t, 1), :].to_broadcast([P, ROUNDS, D + h])
                        dve.tensor_tensor(prod[:, :, :], row[:, :, 0:D + h], q, ALU.mult).then_inc(multiplied, 1)
                    else:
                        dve.tensor_tensor(prod[:, :, :], row[:, :, D:D + h], own[:, bass.ds(t, 1), D + h:D + 2 * h].to_broadcast([P, ROUNDS, h]),
                                          ALU.add).then_inc(multiplied, 1)

                def sum_scores(k, n):
                    s = score[:, k, 0:ROUNDS, :]
                    dve.wait_ge(multiplied, n)
                    if qk:
                        dve.tensor_reduce(s, prod[:, :, :].rearrange("p r (h d) -> p r h d", d=av), AX.X, ALU.add).then_inc(summed, 1)
                    else:
                        dve.scalar_tensor_tensor(s, prod[:, :, :], 0.2, prod[:, :, :], ALU.mult, ALU.max).then_inc(summed, 1)

                def raise_peak(k, n):
                    s = score[:, k, :, :]
                    dve.wait_ge(peaked, n)
                    dve.wait_ge(summed, n)
                    dve.tensor_reduce(new_peak[:, k, 0, :], s.rearrange("p r h -> p h r"), AX.X, ALU.max).then_inc(maxed, 1)

                def shift_scores(k, n, t):
                    s = score[:, k, :, :]
                    dve.wait_ge(maxed, n)
                    dve.tensor_tensor(s, s, new_peak[:, k, :, :].to_broadcast([P, ROUNDS + 1, h]), ALU.subtract).then_inc(shifted, 1)
                    dve.tensor_copy(peak[:, bass.ds(t, 1), :], new_peak[:, k, :, :]).then_inc(kept, 1)

                def weight_chunk(k, n):
                    row, w = rows[:, k, :, :], wv[:, k, :, :, :]
                    dve.wait_ge(exped, n)
                    dve.tensor_tensor(w[:, 0:dve_rounds, :, 0:dh], row[:, 0:dve_rounds, v0:v0 + D].rearrange("p r (h d) -> p r h d", d=dh),
                                      w[:, 0:dve_rounds, :, dh:dh + 1].to_broadcast([P, dve_rounds, h, dh]), ALU.mult).then_inc(weighted, 1)

                def rescale(k, n, t):
                    a = acc[:, bass.ds(t, 1), :, :].rearrange("p a h f -> p (a h) f")
                    dve.wait_ge(added, n)
                    dve.tensor_tensor(a, a, wv[:, k, ROUNDS, :, dh:dh + 1].to_broadcast([P, h, av]), ALU.mult).then_inc(rescaled, 1)

                def accumulate(k, n, t):
                    a = acc[:, bass.ds(t, 1), :, :].rearrange("p a h f -> p (a h f)")
                    dve.wait_ge(rescaled, n)
                    dve.wait_ge(part_sum, n)
                    dve.tensor_tensor(a, a, part[:, k, 0:h * av], ALU.add).then_inc(added, 1)

                def block_of(i, first):
                    n = [k + 1 if first else dve.snap(i * SLOTS + (k + 1)) for k in range(SLOTS)]
                    t = [tile_at(0 if first else i * SLOTS)]
                    for k in range(SLOTS):
                        one, two = (k - 1) % SLOTS, (k - 2) % SLOTS
                        begin_scores(k, n[k], t[k])
                        if not (first and k < 1):
                            weight_chunk(one, n[k] - 1)
                        if k < SLOTS - 1:
                            t.append(tile_at(k + 1 if first else i * SLOTS + (k + 1)))
                        sum_scores(k, n[k])
                        if not (first and k < 2):
                            t_two = t[k - 2] if k >= 2 else tile_at(i * SLOTS + (k - 2))
                            rescale(two, n[k], t_two)
                        raise_peak(k, n[k])
                        if not (first and k < 2):
                            accumulate(two, n[k], t_two)
                        shift_scores(k, n[k], t[k])

                block_of(0, True)
                if early < NT:
                    dve.wait_ge(own_rest, 16 * (NT - early))
                with dve.Fori(1, blocks) as i:
                    block_of(i, False)
                last = dve.snap(blocks * SLOTS)
                weight_chunk(SLOTS - 1, last)
                for back in (1, 0):
                    t_back = tile_at(last - (back + 1))
                    rescale(SLOTS - 1 - back, last + (2 - back), t_back)
                    accumulate(SLOTS - 1 - back, last + (2 - back), t_back)
                dve.wait_ge(added, last + 3)
                dve.tensor_scalar(recip[:, 0, :, :], acc[:, :, :, dh], 1.0e-30, None, ALU.max).then_inc(den, 1)
                dve.wait_ge(den, 1)
                dve.reciprocal(recip[:, 1, :, :], recip[:, 0, :, :]).then_inc(den, 1)
                dve.wait_ge(den, 2)
                if not qk:
                    dve.wait_ge(bias_in, 16)
                for k in range(groups):
                    part_t = slice(GROUP * k, GROUP * (k + 1))
                    dve.tensor_tensor(own[:, part_t, 0:D].rearrange("p t (h d) -> p t h d", d=dh), acc[:, part_t, :, 0:dh],
                                      recip[:, 1, part_t, :].unsqueeze(3).to_broadcast([P, GROUP, h, dh]), ALU.mult).then_inc(normed, 1)
                    if not qk:
                        dve.wait_ge(normed, k + 1)
                        dve.tensor_tensor(own[:, part_t, 0:D], own[:, part_t, 0:D], bias_bc[:, :].unsqueeze(1).to_broadcast([P, GROUP, D]),
                                          ALU.add).then_inc(biased, 1)

            @block.scalar
            def _(act):
                act.sem_inc(act_weighted, SLOTS)
                with act.Fori(0, blocks_of(act)) as i:
                    for k in range(SLOTS):
                        n = act.snap(i * SLOTS + (k + 1))
                        act.wait_ge(shifted, n)
                        act.activation(wv[:, k, :, :, dh], score[:, k, :, :], ACT.Exp).then_inc(exped, 1)
                        if act_rounds:
                            act.wait_ge(exped, n)
                            for r in range(dve_rounds, ROUNDS):
                                for e in range(h):
                                    last = act.activation(wv[:, k, r, e, 0:dh], rows[:, k, r, v0 + e * dh:v0 + (e + 1) * dh], ACT.Copy,
                                                          scale=wv[:, k, r, e, dh:dh + 1])
                            last.then_inc(act_weighted, 1)
                if not qk:
                    for k in range(groups):
                        act.wait_ge(biased, k + 1)
                        out = own[:, GROUP * k:GROUP * (k + 1), 0:D]
                        act.activation(out, out, ACT.Gelu).then_inc(gelued, 1)

            @block.tensor
            def _(pe):
                pe.sem_inc(part_sum, 2)
                with pe.Fori(0, blocks_of(pe)) as i:
                    for k in range(SLOTS):
                        pe.wait_ge(weighted, i * SLOTS + (k + 1 + SLOTS))
                        if act_rounds:
                            pe.wait_ge(act_weighted, i * SLOTS + (k + 1 + SLOTS))
                        for r in range(ROUNDS):
                            last = pe.matmul(part[:, k, 0:h * av], c.ident[:, :], wv[:, k, r, :, :].rearrange("p h f -> p (h f)"),
                                             start=(r == 0), stop=(r == ROUNDS - 1))
                        last.then_inc(part_sum, 1)


def tiles(table, w):
    return table.rearrange("(t p) w -> p t w", p=P)


def table_tiles(k):
    t = GROUP * k
    s = t + (1 if t >= DUMMY // P else 0)
    return slice(s, s + GROUP)


def prepare(nc, c, x_in, x, loads, late, cleared_first, fills):
    full = N_NODES // P
    rest = N_NODES - full * P
    with Mem(nc, "prep") as m:
        fill = {}
        for _, width, low in fills:
            if (width, str(low)) not in fill:
                fill[width, str(low)] = m.sb(f"fill{len(fill)}", [P, width]), low
        loaded, cleared, lowered = m.sem("loaded"), m.sem("cleared"), m.sem("lowered")
        stored = m.sem("stored")
        n_clear = 2 + len(cleared_first) + len(fill)
        n_low = sum(low is not None for _, low in fill.values())
        with nc.Block() as block:
            @block.vector
            def _(dve):
                dve.memset(x[:, full, :], 0.0).then_inc(cleared, 1)
                dve.memset(c.eps[:, :], EPS).then_inc(cleared, 1)
                for buf in cleared_first:
                    dve.memset(buf[:, :, :], 0.0).then_inc(cleared, 1)
                for buf, _ in fill.values():
                    dve.memset(buf[:, :], 0.0).then_inc(cleared, 1)
                dve.wait_ge(cleared, n_clear)
                for buf, low in fill.values():
                    if low is not None:
                        dve.memset(buf[:, low], -3.0e38).then_inc(lowered, 1)

            @block.sync
            def _(sp):
                sp.dma_start(x[:, 0:full, :], x_in[0:full * P, :].rearrange("(t p) f -> p t f", p=P)).then_inc(loaded, 16)
                for dst, src in loads:
                    sp.dma_start(dst, src).then_inc(loaded, 16)
                sp.wait_ge(cleared, n_clear)
                sp.dma_start(x[0:rest, full, :], x_in[full * P:N_NODES, :]).then_inc(loaded, 16)
                for dst, src in late:
                    sp.dma_start(dst, src).then_inc(loaded, 16)
                sp.wait_ge(loaded, 16 * (2 + len(loads) + len(late)))

            @block.scalar
            def _(act):
                act.wait_ge(lowered, n_low)
                for rows, width, low in fills:
                    act.dma_start(rows, fill[width, str(low)][0][:, :]).then_inc(stored, 16)
                act.wait_ge(stored, 16 * len(fills))


NE, HID = 8, 1024
HC = HID // P
A_ROWS = 2 * NPAD
MAX_SLOT_TILES = 57
SLOT_COLS = 60


def top_two(nc, c, name, logits, top, idx_f):
    with Mem(nc, name) as m:
        top8, idx8 = m.sb("top8", [P, NT, 8]), m.sb("idx8", [P, NT, 8], mybir.dt.uint32)
        maxed, found, copied = m.sem("maxed"), m.sem("found"), m.sem("copied")
        with nc.Block() as block:
            @block.vector
            def _(dve):
                for t in range(NT):
                    dve.max(top8[:, t, :], logits[:, t, :]).then_inc(maxed, 1)
                dve.wait_ge(maxed, NT)
                for t in range(NT):
                    dve.max_index(idx8[:, t, :], top8[:, t, :], logits[:, t, :]).then_inc(found, 1)
                dve.wait_ge(found, NT)
                dve.tensor_copy(idx_f[:, :, :], idx8[:, :, 0:2]).then_inc(copied, 1)
                dve.tensor_copy(top[:, :, :], top8[:, :, 0:2]).then_inc(copied, 1)
                dve.wait_ge(copied, 2)


def route(nc, c, r, logits):
    with Mem(nc, "rt") as m:
        top, idx_f = m.sb("top", [P, NT, 2]), m.sb("idx_f", [P, NT, 2])
        top_two(nc, c, "rt2", logits, top, idx_f)
        diff, e2, den = m.sb("diff", [P, NT]), m.sb("e2", [P, NT]), m.sb("den", [P, NT])
        chosen = m.sb("chosen", [P, 3, NT, NE])
        node_f = m.sb("node_f", [P, NT])
        counts_ps, before_ps = m.ps("counts", [P, 512]), m.ps("before", [P, 512])
        cum = m.sb("cum", [P, NE, NT + 1])
        last_of = m.sb("last_of", [P, NE + 1])
        n_i, n_f = m.sb("n_i", [P, NE], I32), m.sb("n_f", [P, NE])
        slot_all = m.sb("slot_all", [P, NT, NE])
        pick = m.sb("pick", [P, 2, NT, NE])
        slot_f = m.sb("slot_f", [P, 2, NT])
        sl_i = m.sb("sl_i", [P, 2, 2, NT], I32)
        sl_f = m.sb("sl_f", [P, 2, 2, NT])
        oh_lane, oh_tile = m.sb("oh_lane", [P, 2, P]), m.sb("oh_tile", [P, 2, SLOT_COLS])
        slots_ps = m.ps("slots", [P, SLOT_COLS])
        past = m.sb("past", [P, SLOT_COLS, NE])
        exp_f = m.sb("exp_f", [P, SLOT_COLS])
        chain, ready, expd, summed, made, placed = (m.sem(x) for x in ("chain", "ready", "expd", "summed", "made", "placed"))
        with nc.Block() as block:
            @block.gpsimd
            def _(pool):
                pool.iota(node_f[:, :], pattern=[[P, NT]], base=0, channel_multiplier=1,
                          allow_small_or_imprecise_dtypes=True).then_inc(ready, 1)

            @block.scalar
            def _(act):
                act.wait_ge(ready, 2)
                act.activation(e2[:, :], diff[:, :], ACT.Exp).then_inc(expd, 1)

            @block.vector
            def _(dve):
                n = [0]

                def step(ins):
                    n[0] += 1
                    ins.then_inc(chain, 1)
                    dve.wait_ge(chain, n[0])

                dve.wait_ge(ready, 1)
                dve.tensor_tensor(diff[:, :], top[:, :, 1], top[:, :, 0], ALU.subtract).then_inc(ready, 1)
                for k in range(2):
                    step(dve.tensor_tensor(chosen[:, k, :, :], idx_f[:, :, k:k + 1].to_broadcast([P, NT, NE]),
                                           c.iota_f[:, 0:NE].unsqueeze(1).to_broadcast([P, NT, NE]), ALU.is_equal))
                step(dve.tensor_tensor(chosen[:, 2, :, :], chosen[:, 0, :, :], chosen[:, 1, :, :], ALU.add))
                dve.sem_inc(ready, 1)
                dve.wait_ge(expd, 1)
                step(dve.tensor_scalar(den[:, :], e2[:, :], 1.0, None, ALU.add))
                step(dve.reciprocal(r.weight[:, 0, :], den[:, :]))
                step(dve.tensor_tensor(r.weight[:, 1, :], r.weight[:, 0, :], e2[:, :], ALU.mult))
                dve.wait_ge(summed, 1)
                step(dve.memset(cum[:, :, 0:1], 0.0))
                for e in range(NE):
                    step(dve.tensor_tensor_scan(cum[:, e, 1:NT + 1], c.ones[:, 0:NT],
                                                counts_ps[:, 0:NT * NE].rearrange("p (t e) -> p e t", e=NE)[:, e, :], 0.0, ALU.mult, ALU.add))
                step(dve.tensor_scalar(n_f[:, :], cum[:, :, NT], float(P - 1), float(P), ALU.add, ALU.max))
                step(dve.tensor_copy(n_i[:, :], n_f[:, :]))
                step(dve.tensor_single_scalar(n_i[:, :], n_i[:, :], 7, ALU.logical_shift_right))
                step(dve.tensor_copy(n_f[:, :], n_i[:, :]))
                step(dve.memset(last_of[:, 0:1], 0.0))
                step(dve.tensor_tensor_scan(last_of[:, 1:NE + 1], c.ones[:, 0:NE], n_f[:, :], 0.0, ALU.mult, ALU.add))
                step(dve.tensor_copy(r.first_tile[:, :], last_of[:, :]))
                step(dve.tensor_scalar(n_f[:, :], last_of[:, 0:NE], float(P), None, ALU.mult))
                step(dve.tensor_tensor(slot_all[:, :, :], cum[:, :, 0:NT].rearrange("p e t -> p t e"),
                                       n_f[:, :].unsqueeze(1).to_broadcast([P, NT, NE]), ALU.add))
                step(dve.tensor_tensor(slot_all[:, :, :], slot_all[:, :, :],
                                       before_ps[:, 0:NT * NE].rearrange("p (t e) -> p t e", e=NE), ALU.add))
                for k in range(2):
                    step(dve.tensor_tensor(pick[:, k, :, :], chosen[:, k, :, :], slot_all[:, :, :], ALU.mult))
                    step(dve.tensor_reduce(slot_f[:, k, :], pick[:, k, :, :], AX.X, ALU.add))
                step(dve.tensor_copy(r.slot[:, :, :], slot_f[:, :, :]))
                step(dve.tensor_single_scalar(sl_i[:, :, 0, :], r.slot[:, :, :], P - 1, ALU.bitwise_and))
                step(dve.tensor_single_scalar(sl_i[:, :, 1, :], r.slot[:, :, :], 7, ALU.logical_shift_right))
                step(dve.tensor_copy(sl_f[:, :, :, :], sl_i[:, :, :, :]))
                step(dve.tensor_tensor(past[:, :, :], c.iota_f[:, 0:SLOT_COLS].unsqueeze(2).to_broadcast([P, SLOT_COLS, NE]),
                                       last_of[:, 1:NE + 1].unsqueeze(1).to_broadcast([P, SLOT_COLS, NE]), ALU.is_ge))
                step(dve.tensor_reduce(exp_f[:, :], past[:, :, :], AX.X, ALU.add))
                step(dve.tensor_scalar(exp_f[:, :], exp_f[:, :], float(NE - 1), None, ALU.min))
                step(dve.tensor_copy(r.expert[:, :], exp_f[:, :]))
                with dve.Fori(0, NT) as t:
                    for k in range(2):
                        dve.wait_ge(placed, t * 2 + (k + 1))
                        dve.tensor_scalar(oh_lane[:, k, :], c.iota_f[:, 0:P], sl_f[:, k, 0, bass.ds(t, 1)], None, ALU.is_equal).then_inc(made, 1)
                        dve.tensor_scalar(oh_tile[:, k, :], c.iota_f[:, 0:SLOT_COLS], sl_f[:, k, 1, bass.ds(t, 1)], node_f[:, bass.ds(t, 1)],
                                          ALU.is_equal, ALU.mult).then_inc(made, 1)
                dve.wait_ge(placed, 2 * NT + 2)
                step(dve.tensor_copy(r.node[:, :], slots_ps[:, :]))

            @block.tensor
            def _(pe):
                pe.wait_ge(ready, 3)
                flat = chosen[:, 2, :, :].rearrange("p t e -> p (t e)")
                pe.matmul(counts_ps[:, 0:NT * NE], c.ones[:, :], flat, start=True, stop=True)
                pe.matmul(before_ps[:, 0:NT * NE], c.before[:, :], flat, start=True, stop=True).then_inc(summed, 1)
                pe.matmul(slots_ps[:, :], c.zeros[:, 0:P], c.zeros[:, 0:SLOT_COLS], start=True, stop=True).then_inc(placed, 2)
                with pe.Fori(0, NT) as t:
                    for k in range(2):
                        pe.wait_ge(made, t * 4 + 2 * (k + 1))
                        pe.matmul(slots_ps[:, :], oh_lane[:, k, :], oh_tile[:, k, :], start=False, stop=True,
                                  skip_group_check=True).then_inc(placed, 1)


def experts(nc, c, r, xn_rows, y_rows, w):
    with Mem(nc, "ex") as m:
        w1, w2 = m.sb("w1", [P, 2, KC, HID]), m.sb("w2", [P, 2, HC, D])
        b1, b2 = m.sb("b1", [P, NE, HC]), m.sb("b2", [P, NE, D])
        ln_g, ln_b = m.sb("ln_g", [P, NE, KC]), m.sb("ln_b", [P, NE, KC])
        node_at = m.sb("node_at", [P, 1], I32)
        x_in = m.sb("x_in", [P, D])
        xe = m.sb("xe", [P, KC, P])
        hid = m.sb("hid", [P, HC, P])
        y = m.sb("y", [P, 2, D])
        turn, up, down = m.ps("turn", [P, 512]), m.ps("up", [P, HC // 2, 512]), m.ps("down", [P, 2, 512])
        w_in = [m.sem(f"w_in{k}") for k in range(2)]
        (arrived, node_set, turned, scaled, up_done, act_done, down_done, y_ready, y_free, y_stored, bias_in, passed) = (
            m.sem(s) for s in ("arrived", "node_set", "turned", "scaled", "up_done", "act_done", "down_done",
                               "y_ready", "y_free", "y_stored", "bias_in", "passed"))

        def first_tile(eng, e, least=0):
            return eng.value_load(r.first_tile[0:1, bass.ds(e, 1)], min_val=least, max_val=MAX_SLOT_TILES)

        with nc.Block() as block:
            @block.sync
            def _(sp):
                def load_expert(e, k):
                    sp.dma_start(w1[:, k, :, :], w.w1[bass.ds(e, 1), :, :].rearrange("a (k p) n -> p (a k) n", p=P)).then_inc(w_in[k], 16)
                    sp.dma_start(w2[:, k, :, :], w.w2[bass.ds(e, 1), :, :].rearrange("a (k p) n -> p (a k) n", p=P)).then_inc(w_in[k], 16)

                load_expert(0, 0)
                with nc.allow_non_contiguous_dma(reason="per-partition biases, a few thousand numbers"):
                    sp.dma_start(b1[:, :, :], w.b1.rearrange("e (c p) -> p e c", p=P)).then_inc(bias_in, 16)
                    sp.dma_start(ln_g[:, :, :], w.ln_g.rearrange("e (c p) -> p e c", p=P)).then_inc(bias_in, 16)
                    sp.dma_start(ln_b[:, :, :], w.ln_b.rearrange("e (c p) -> p e c", p=P)).then_inc(bias_in, 16)
                sp.dma_start(b2[:, :, :], w.b2.rearrange("(a e) f -> a e f", a=1).to_broadcast([P, NE, D])).then_inc(bias_in, 16)
                load_expert(1, 1)
                with sp.Fori(1, NE // 2) as i:
                    for k in range(2):
                        sp.wait_ge(down_done, first_tile(sp, i * 2 + k - 1))
                        sp.sem_inc(passed, 1)
                        load_expert(i * 2 + k, k)

            @block.gpsimd
            def _(pool):
                total = first_tile(pool, NE, NE)

                def gather(n):
                    pool.wait_ge(turned, n + 1)
                    pool.tensor_copy(node_at[:, :], r.node[:, bass.ds(n, 1)]).then_inc(node_set, 1)
                    pool.wait_ge(node_set, n + 1)
                    pool.sem_inc(passed, 1)
                    pool.indirect_dma_start(out=x_in[:, :], out_offset=None, in_=xn_rows,
                                            in_offset=bass.IndirectOffsetOnAxis(ap=node_at[:, :], axis=0)).then_inc(arrived, 16)

                def store(n, first=False):
                    pool.wait_ge(y_ready, n + 3)
                    if not first:
                        pool.wait_ge(y_stored, n * 16)
                    pool.sem_inc(y_free, 1)
                    pool.dma_start(y_rows[bass.ds(n, 1), :, :].rearrange("a p f -> (a p) f"),
                                   y[:, bass.ds(n % 2, 1), :].rearrange("p a f -> p (a f)")).then_inc(y_stored, 16)

                for n in range(3):
                    gather(n)
                store(0, first=True)
                with pool.Fori(1, total) as n:
                    gather(n + 2)
                    store(n)
                pool.wait_ge(arrived, total * 16 + 32)
                pool.wait_ge(y_stored, total * 16)
                pool.sem_inc(passed, 1)

            @block.vector
            def _(dve):
                total = first_tile(dve, NE)
                dve.wait_ge(bias_in, 64)

                def scale(n):
                    e = dve.value_load(r.expert[0:1, bass.ds(n, 1)], min_val=0, max_val=NE - 1)
                    dve.wait_ge(turned, n + 2)
                    for h in range(KC):
                        dve.tensor_scalar(xe[:, h, :], turn[:, h * P:(h + 1) * P],
                                          ln_g[:, bass.ds(e, 1), h], ln_b[:, bass.ds(e, 1), h], ALU.mult, ALU.add).then_inc(scaled, 1)

                dve.sem_inc(y_ready, 2)
                dve.sem_inc(y_free, 1)
                scale(0)
                with dve.Fori(0, total) as n:
                    scale(n + 1)
                    e = dve.value_load(r.expert[0:1, bass.ds(n, 1)], min_val=0, max_val=NE - 1)
                    dve.wait_ge(down_done, n + 1)
                    dve.wait_ge(y_free, n + 1)
                    dve.tensor_tensor(y[:, bass.ds(n % 2, 1), :].rearrange("p a f -> p (a f)"),
                                      down[:, bass.ds(n % 2, 1), 0:D].rearrange("p a f -> p (a f)"),
                                      b2[:, bass.ds(e, 1), :].rearrange("p a f -> p (a f)"), ALU.add).then_inc(y_ready, 1)

            @block.tensor
            def _(pe):
                def turn_tile(n):
                    pe.wait_ge(arrived, n * 16 + 16)
                    for h in range(KC):
                        last = pe.transpose(turn[:, h * P:(h + 1) * P], x_in[:, h * P:(h + 1) * P], c.ident[:, :])
                    last.then_inc(turned, 1)

                pe.sem_inc(turned, 1)
                turn_tile(0)
                pe.wait_ge(bias_in, 64)
                with pe.Fori(0, NE // 2) as i:
                    for k in range(2):
                        e = i * 2 + k
                        pe.wait_ge(w_in[k], i * 32 + 32)
                        pe.sem_inc(passed, 1)
                        with pe.Fori(first_tile(pe, e), first_tile(pe, e + 1)) as n:
                            pe.wait_ge(scaled, n * KC + KC)
                            for q in range(HC):
                                for h in range(KC):
                                    last = pe.matmul(up[:, q // 2, (q % 2) * P:(q % 2 + 1) * P], w1[:, k, h, q * P:(q + 1) * P], xe[:, h, :], start=(h == 0), stop=(h == KC - 1))
                                if q % 2:
                                    last.then_inc(up_done, 1)
                            turn_tile(n + 1)
                            pe.wait_ge(y_ready, n + 1)
                            out = down[:, bass.ds(n % 2, 1), 0:D].rearrange("p a f -> p (a f)")
                            for q in range(HC):
                                pe.wait_ge(act_done, n * HC + (q + 1))
                                last = pe.matmul(out, hid[:, q, :], w2[:, k, q, :], start=(q == 0), stop=(q == HC - 1))
                            last.then_inc(down_done, 1)

            @block.scalar
            def _(act):
                total = first_tile(act, NE)
                act.wait_ge(bias_in, 64)
                with act.Fori(0, total) as n:
                    e = act.value_load(r.expert[0:1, bass.ds(n, 1)], min_val=0, max_val=NE - 1)
                    for q in range(HC):
                        if q % 2 == 0:
                            act.wait_ge(up_done, n * (HC // 2) + (q // 2 + 1))
                        act.activation(hid[:, q, :], up[:, q // 2, (q % 2) * P:(q % 2 + 1) * P], ACT.Gelu, bias=b1[:, bass.ds(e, 1), q]).then_inc(act_done, 1)


def combine(nc, c, r, y_rows, x):
    with Mem(nc, "cb") as m:
        ys = m.sb("ys", [P, 2, NT, D])
        arrived = [m.sem(f"arrived{k}") for k in range(NT // GROUP)]
        added = m.sem("added")
        with nc.Block() as block:
            @block.gpsimd
            def _(pool):
                for t in range(NT):
                    for k in range(2):
                        pool.indirect_dma_start(out=ys[:, k, t, :], out_offset=None, in_=y_rows,
                                                in_offset=bass.IndirectOffsetOnAxis(ap=r.slot[:, k, t:t + 1], axis=0)).then_inc(arrived[t // GROUP], 16)

            @block.vector
            def _(dve):
                for j in range(NT // GROUP):
                    dve.wait_ge(arrived[j], 32 * GROUP)
                    for k in range(2):
                        for t in range(GROUP * j, GROUP * (j + 1)):
                            dve.scalar_tensor_tensor(x[:, t, :], ys[:, k, t, :], r.weight[:, k, t:t + 1], x[:, t, :],
                                                     ALU.mult, ALU.add).then_inc(added, 1)
                        dve.wait_ge(added, GROUP * (2 * j + k + 1))


GH, GC = 4, 64
GW = D + 2 * GH
QH = 8
QW = D + QH
KVW = QW + D
E2, SH2, EH1, EH2 = 4, 128, 128, 64


def gat_weights(nc, c, w_exts, vectors):
    n = len(w_exts)
    with Mem(nc, "gaw") as m:
        w_t = m.sb("w_t", [P, n, KC, KC, P])
        turn, prod = m.ps("turn", [P, n, KC, KC, P]), m.ps("prod", [P, n, KC, 2 * GH])
        turned, copied, mult, done = (m.sem(s) for s in ("turned", "copied", "mult", "done"))
        with nc.Block() as block:
            @block.vector
            def _(dve):
                for i in range(n):
                    dve.wait_ge(turned, i + 1)
                    dve.tensor_copy(w_t[:, i, :, :, :], turn[:, i, :, :, :]).then_inc(copied, 1)
                dve.wait_ge(mult, 1)
                for i in range(n):
                    dve.tensor_copy(w_exts[i][:, :, D:GW], prod[:, i, :, :]).then_inc(done, 1)
                dve.wait_ge(done, n)

            @block.tensor
            def _(pe):
                for i in range(n):
                    for k in range(KC):
                        for f in range(KC):
                            last = pe.transpose(turn[:, i, f, k, :], w_exts[i][:, k, f * P:(f + 1) * P], c.ident[:, :])
                    last.then_inc(turned, 1)
                for i in range(n):
                    pe.wait_ge(copied, i + 1)
                    for k in range(KC):
                        for f in range(KC):
                            last = pe.matmul(prod[:, i, k, :], w_t[:, i, f, k, :], vectors[i][:, f, :], start=(f == 0), stop=(f == KC - 1))
                last.then_inc(mult, 1)


def gates_to_weights(nc, c, raw, w5):
    with Mem(nc, "gw") as m:
        gates = m.sb("gates", [P, NT, 8])
        peak, total = m.sb("peak", [P, NT]), m.sb("total", [P, NT])
        top, idx_f = m.sb("top", [P, NT, 2]), m.sb("idx_f", [P, NT, 2])
        wt = m.sb("wt", [P, 3, NT])
        chosen = m.sb("chosen", [P, 2, NT, E2])
        chain, ready, expd = m.sem("chain"), m.sem("ready"), m.sem("expd")
        with nc.Block() as block:
            @block.vector
            def _(dve):
                n = [0]

                def step(ins):
                    n[0] += 1
                    ins.then_inc(chain, 1)
                    dve.wait_ge(chain, n[0])

                step(dve.memset(gates[:, :, :], -1.0))
                step(dve.tensor_reduce(peak[:, :], raw[:, :, :], AX.X, ALU.max))
                dve.tensor_tensor(raw[:, :, :], raw[:, :, :], peak[:, :].unsqueeze(2).to_broadcast([P, NT, E2]), ALU.subtract).then_inc(ready, 1)
                dve.wait_ge(expd, 1)
                step(dve.tensor_reduce(total[:, :], gates[:, :, 0:E2], AX.X, ALU.add))
                step(dve.reciprocal(total[:, :], total[:, :]))
                step(dve.tensor_tensor(gates[:, :, 0:E2], gates[:, :, 0:E2], total[:, :].unsqueeze(2).to_broadcast([P, NT, E2]), ALU.mult))

            @block.scalar
            def _(act):
                act.wait_ge(ready, 1)
                act.activation(gates[:, :, 0:E2], raw[:, :, :], ACT.Exp).then_inc(expd, 1)

        top_two(nc, c, "gt2", gates, top, idx_f)
        chain2, ready2, expd2 = m.sem("chain2"), m.sem("ready2"), m.sem("expd2")
        with nc.Block() as block:
            @block.vector
            def _(dve):
                n = [0]

                def step(ins):
                    n[0] += 1
                    ins.then_inc(chain2, 1)
                    dve.wait_ge(chain2, n[0])

                dve.tensor_tensor(wt[:, 0, :], top[:, :, 1], top[:, :, 0], ALU.subtract).then_inc(ready2, 1)
                for k in range(2):
                    step(dve.tensor_tensor(chosen[:, k, :, :], idx_f[:, :, k:k + 1].to_broadcast([P, NT, E2]),
                                           c.iota_f[:, 0:E2].unsqueeze(1).to_broadcast([P, NT, E2]), ALU.is_equal))
                dve.wait_ge(expd2, 1)
                step(dve.tensor_scalar(wt[:, 2, :], wt[:, 1, :], 1.0, None, ALU.add))
                step(dve.reciprocal(wt[:, 0, :], wt[:, 2, :]))
                step(dve.tensor_tensor(wt[:, 1, :], wt[:, 0, :], wt[:, 1, :], ALU.mult))
                for k in range(2):
                    step(dve.tensor_tensor(chosen[:, k, :, :], chosen[:, k, :, :], wt[:, k, :].unsqueeze(2).to_broadcast([P, NT, E2]), ALU.mult))
                step(dve.memset(w5[:, :, E2:E2 + 1], 1.0))
                step(dve.tensor_tensor(w5[:, :, 0:E2], chosen[:, 0, :, :], chosen[:, 1, :, :], ALU.add))

            @block.scalar
            def _(act):
                act.wait_ge(ready2, 1)
                act.activation(wt[:, 1, :], wt[:, 0, :], ACT.Exp).then_inc(expd2, 1)


def shared_and_experts(nc, c, norm, x, w5, w, out):
    with Mem(nc, "f2") as m:
        sw1, sw2, sw3 = m.sb("sw1", [P, KC, D]), m.sb("sw2", [P, KC, SH2]), m.sb("sw3", [P, D])
        ew1, ew2 = m.sb("ew1", [P, E2, KC, EH1]), m.sb("ew2", [P, E2, EH2])
        ew3 = m.sb("ew3", [P, E2 // 2, D])
        bias1 = m.sb("bias1", [P, KC + E2])
        bias2 = m.sb("bias2", [P, 1 + E2 // 2])
        bias3 = m.sb("bias3", [E2 + 1, D])
        pair = m.sb("pair", [E2, E2 // 2, P])
        rows = m.sb("rows", [P, 2, D + E2 + 1])
        x_t = m.sb("x_t", [P, 2, KC, P])
        w_t = m.sb("w_t", [E2 + 1, 2, P])
        h1 = m.sb("h1", [P, 2, KC + E2, P])
        h2 = m.sb("h2", [P, 2, 1 + E2 // 2, P])
        turn = m.ps("turn", [P, 512])
        p1 = m.ps("p1", [P, (KC + E2) // 2, 512])
        p2 = m.ps("p2", [P, 4, P])
        pw = m.ps("pw", [P, E2 // 2, P])
        p3 = m.ps("p3", [P, 2, 512])
        loads = m.sem("loads")
        outd = [m.sem(f"outd{k}") for k in range(NT // GROUP)]
        (built, staged, turned, copied, up1, act1, up2, act2, scaled, down, added) = (
            m.sem(s) for s in ("built", "staged", "turned", "copied", "up1", "act1", "up2", "act2", "scaled", "down", "added"))
        with nc.Block() as block:
            @block.sync
            def _(sp):
                with nc.allow_non_contiguous_dma(reason="per-partition biases, about a thousand numbers"):
                    sp.dma_start(sw1[:, :, :], w.sW1.rearrange("(k p) n -> p k n", p=P)).then_inc(loads, 16)
                    sp.dma_start(sw2[:, :, :], w.sW2.rearrange("(k p) n -> p k n", p=P)).then_inc(loads, 16)
                    sp.dma_start(sw3[:, :], w.sW3).then_inc(loads, 16)
                    sp.dma_start(ew2[:, :, :], w.eW2.rearrange("e p n -> p e n")).then_inc(loads, 16)
                    for t in range(2):
                        sp.dma_start(ew3[t * EH2:(t + 1) * EH2, :, :], w.eW3.rearrange("(j t) p n -> t p j n", t=2)[t]).then_inc(loads, 16)
                        sp.dma_start(bias2[t * EH2:(t + 1) * EH2, 1:1 + E2 // 2], w.eb2.rearrange("(j t) p -> t p j", t=2)[t]).then_inc(loads, 16)
                    sp.dma_start(bias1[:, 0:KC], w.sb1.rearrange("(k p) -> p k", p=P)).then_inc(loads, 16)
                    sp.dma_start(bias1[:, KC:KC + E2], w.eb1.rearrange("e p -> p e")).then_inc(loads, 16)
                    sp.dma_start(bias2[:, 0:1], w.sb2.rearrange("(p o) -> p o", o=1)).then_inc(loads, 16)
                    sp.dma_start(bias3[0:E2, :], w.eb3).then_inc(loads, 16)
                    sp.dma_start(bias3[E2:E2 + 1, :], w.sb3.rearrange("(o n) -> o n", o=1)).then_inc(loads, 16)
                    for e in range(E2):
                        sp.dma_start(ew1[:, e, :, :], w.eW1[e].rearrange("(k p) n -> p k n", p=P)).then_inc(loads, 16)
                for k in range(NT // GROUP):
                    sp.wait_ge(added, GROUP * (k + 1) + 2)
                    full = min(GROUP * (k + 1), N_NODES // P)
                    sp.dma_start(out[GROUP * k * P:full * P, :].rearrange("(t p) f -> p t f", p=P), x[:, GROUP * k:full, :]).then_inc(outd[k], 16)
                rest = N_NODES - (N_NODES // P) * P
                sp.dma_start(out[N_NODES - rest:N_NODES, :], x[0:rest, NT - 1, :]).then_inc(outd[0], 16)
                sp.wait_ge(outd[0], 32)
                for k in range(1, NT // GROUP):
                    sp.wait_ge(outd[k], 16)

            @block.gpsimd
            def _(pool):
                pool.memset(pair[:, :, :], 1.0).then_inc(built, 1)
                pool.wait_ge(built, 1)
                pool.affine_select(out=pair[:, :, :], in_=pair[:, :, :], compare_op=ALU.is_ge, fill=0.0, base=0,
                                   pattern=[[P, E2 // 2], [1, P]], channel_multiplier=-EH2).then_inc(built, 1)
                pool.wait_ge(built, 2)
                pool.affine_select(out=pair[:, :, :], in_=pair[:, :, :], compare_op=ALU.is_ge, fill=0.0, base=EH2 - 1,
                                   pattern=[[-P, E2 // 2], [-1, P]], channel_multiplier=EH2).then_inc(built, 1)

            @block.tensor
            def _(pe):
                pe.sem_inc(down, 2)
                pe.wait_ge(built, 3)
                pe.wait_ge(loads, 16 * N_LOADS)

                def turn_tile(t, s):
                    pe.wait_ge(staged, (t + 1) * 2)
                    for h in range(KC):
                        pe.transpose(turn[:, h * P:(h + 1) * P], rows[:, s, h * P:(h + 1) * P], c.ident[:, :])
                    pe.transpose(turn[0:E2 + 1, KC * P:(KC + 1) * P], rows[:, s, D:], c.ident[:, :]).then_inc(turned, 1)

                def tile(t, s):
                    pe.wait_ge(copied, t * 2 + 2)
                    pe.wait_ge(act1, (t + 1) * (KC + E2))
                    xt = [x_t[:, s, h, :] for h in range(KC)]
                    for q in range(KC + E2):
                        for h in range(KC):
                            lhs = sw1[:, h, q * P:(q + 1) * P] if q < KC else ew1[:, q - KC, h, :]
                            last = pe.matmul(p1[:, q // 2, (q % 2) * P:(q % 2 + 1) * P], lhs, xt[h], start=(h == 0), stop=(h == KC - 1))
                        if q % 2:
                            last.then_inc(up1, 1)
                    pe.wait_ge(scaled, (t + 1) * (E2 // 2))
                    for j in range(E2 // 2):
                        last = pe.matmul(pw[:, j, :], pair[:, j, :], w_t[0:E2, s, :], start=True, stop=True)
                    hh = lambda q: h1[:, s, q, :]
                    pe.wait_ge(act2, (t + 1) * (1 + E2 // 2))
                    for k in range(KC):
                        pe.wait_ge(act1, (t + 1) * (KC + E2) + (k + 1))
                        last = pe.matmul(p2[:, 0, :], sw2[:, k, :], hh(k), start=(k == 0), stop=(k == KC - 1))
                    for e in range(E2):
                        pe.wait_ge(act1, (t + 1) * (KC + E2) + (KC + e + 1))
                        r0 = (e % 2) * EH2
                        last = pe.matmul(p2[r0:r0 + EH2, 1 + e // 2, :], ew2[:, e, :], hh(KC + e), start=True, stop=True)
                    last.then_inc(up2, 1)
                    if not (isinstance(t, int) and t == NT - 1):
                        turn_tile(t + 1, 1 - s)
                    o = p3[:, s, 0:D]
                    pe.wait_ge(down, t + 1)
                    pe.wait_ge(added, t + 1)
                    pe.matmul(o, w_t[:, s, :], bias3[:, :], start=True, stop=False)
                    pe.wait_ge(act2, (t + 1) * (1 + E2 // 2) + 1)
                    pe.matmul(o, h2[:, s, 0, :], sw3[:, :], start=False, stop=False)
                    for j in range(E2 // 2):
                        pe.wait_ge(scaled, (t + 1) * (E2 // 2) + (j + 1))
                        last = pe.matmul(o, h2[:, s, 1 + j, :], ew3[:, j, :], start=False, stop=(j == E2 // 2 - 1))
                    last.then_inc(down, 1)

                turn_tile(0, 0)
                each_tile(pe, tile)

            @block.scalar
            def _(act):
                act.sem_inc(act1, KC + E2)
                act.sem_inc(act2, 1 + E2 // 2)
                act.wait_ge(loads, 16 * N_LOADS)

                def tile(t, s):
                    act.wait_ge(turned, t + 1)
                    act.activation(x_t[:, s, :, :].rearrange("p k n -> p (k n)"), turn[:, 0:D], ACT.Copy).then_inc(copied, 1)
                    act.activation(w_t[:, s, :], turn[0:E2 + 1, KC * P:(KC + 1) * P], ACT.Copy).then_inc(copied, 1)
                    for q in range(KC + E2):
                        if q % 2 == 0:
                            act.wait_ge(up1, t * ((KC + E2) // 2) + (q // 2 + 1))
                        act.activation(h1[:, s, q, :], p1[:, q // 2, (q % 2) * P:(q % 2 + 1) * P], ACT.Relu,
                                       bias=bias1[:, q:q + 1]).then_inc(act1, 1)
                    act.wait_ge(up2, t + 1)
                    for j in range(1 + E2 // 2):
                        act.activation(h2[:, s, j, :], p2[:, j, :], ACT.Relu,
                                       bias=bias2[:, j:j + 1]).then_inc(act2, 1)

                each_tile(act, tile)

            @block.vector
            def _(dve):
                dve.sem_inc(scaled, E2 // 2)
                dve.sem_inc(added, 2)

                def stage(t, s):
                    normalise(dve, rows[:, s, 0:D], *norm, t).then_inc(staged, 1)
                    dve.tensor_copy(rows[:, s, D:], w5[:, bass.ds(t, 1), :].rearrange("p a n -> p (a n)")).then_inc(staged, 1)

                def tile(t, s):
                    dve.wait_ge(turned, t + 1)
                    if not (isinstance(t, int) and t == NT - 1):
                        stage(t + 1, 1 - s)
                    for j in range(E2 // 2):
                        dve.wait_ge(act2, (t + 1) * (1 + E2 // 2) + (j + 2))
                        h = h2[:, s, 1 + j, :]
                        dve.tensor_tensor(h, h, pw[:, j, :], ALU.mult).then_inc(scaled, 1)
                    dve.wait_ge(down, t + 3)
                    xt = x[:, bass.ds(t, 1), :].rearrange("p a f -> p (a f)")
                    dve.tensor_tensor(xt, xt, p3[:, s, 0:D], ALU.add).then_inc(added, 1)

                stage(0, 0)
                each_tile(dve, tile)


N_LOADS = 4 + 4 + 5 + E2


class Names:
    pass


def program(nc, a, out):
    Mem.past.clear()
    dram = lambda name, shape, dt=F32: nc.dram_tensor(name, shape, dt, kind="Internal").ap()
    with Mem(nc, "all") as m:
        c = Names()
        c.lane_f, c.iota_f = m.sb("lane_f", [P, 1]), m.sb("iota_f", [P, WIN])
        c.ident, c.before, c.ones, c.zeros = (m.sb(x, [P, P]) for x in ("ident", "before", "ones", "zeros"))
        c.order_bias, c.ones_b, c.ident_b, c.iota_b = (m.sb(x, [P, P], BF16) for x in ("order_bias", "ones_b", "ident_b", "iota_b"))
        c.iota_h = m.sb("iota_h", [P, WIN], F16)
        c.minus1, c.eps = m.sb("minus1", [P, 1]), m.sb("eps", [P, 1])
        build_constants(nc, c)

        graphs = []
        for name, key, val in (("s", a.src, a.dst), ("d", a.dst, a.src)):
            g = Names()
            g.name = name
            g.order, g.first_chunk = m.sb(f"order_{name}", [P, NT], I32), m.sb(f"first_chunk_{name}", [P, NT + 1], I32)
            g.key_parts, g.sort_keys = dram(f"key_parts_{name}", (2, EROWS * ROWE), BF16), dram(f"sort_keys_{name}", (NPAD,))
            g.tile_of = dram(f"tile_of_{name}", (MAX_CHUNKS,), I32)
            g.neighbours = dram(f"neighbours_{name}", (MAX_WIN, P, WIN), I32)
            g.hist_done, g.windows_known, g.window_ready, g.passed = (
                m.sem(f"{x}_{name}") for x in ("hist_done", "windows_known", "window_ready", "passed"))
            build_neighbour_table(nc, c, g, key, val)
            graphs.append(g)

        x = m.sb("x", [P, NT, D])
        q_rows, kv_rows, att_rows = dram("q_rows", (TABLE_ROWS, QW)), dram("kv_rows", (TABLE_ROWS, KVW)), dram("attended_rows", (TABLE_ROWS, D))
        h_rows = [dram(f"h_rows{i}", (TABLE_ROWS, GW)) for i in range(2)]
        y_rows = dram("y_rows", (MAX_SLOT_TILES + 1, P, D))
        wr, br = m.sb("wr", [P, KC, NE]), m.sb("br", [1, NE])
        gw, gb = m.sb("gw", [P, KC, E2]), m.sb("gb", [1, E2])
        ga = [m.sb(f"ga{i}", [P, KC, GW]) for i in range(2)]
        vectors = [m.sb(f"vectors{i}", [P, KC, 2 * GH]) for i in range(2)]
        by_half = lambda v: v.rearrange("(k p) n -> p k n", p=P)
        one_row = lambda v: v.rearrange("(o n) -> o n", o=1)
        first, qkv = Mem(nc, "first"), Mem(nc, "qkv")
        first.__enter__()
        wo, bo = first.sb("wo", [P, KC, D]), first.sb("bo", [1, D])
        qkv.__enter__()
        qkv_w, qkv_b = qkv.sb("w", [P, KC, 3 * D]), qkv.sb("bias", [P, 3 * D])
        loads = [(qkv_w[:, :, i * D:(i + 1) * D], by_half(v)) for i, v in enumerate((a.Wq, a.Wk, a.Wv))]
        loads += [(qkv_b[:, i * D:(i + 1) * D], one_row(v).to_broadcast([P, D])) for i, v in enumerate((a.bq, a.bk, a.bv))]
        loads += [(wo[:, :, :], by_half(a.Wo)), (bo[:, :], one_row(a.bo)), (wr[:, :, :], by_half(a.Wr)), (br[:, :], one_row(a.br)),
                  (gw[:, :, :], by_half(a.gW)), (gb[:, :], one_row(a.gb))]
        late = []
        for i, (v, s_src, s_dst) in enumerate(((a.gW0, a.a_src0, a.a_dst0), (a.gW1, a.a_src1, a.a_dst1))):
            loads.append((ga[i][:, :, 0:D], by_half(v)))
            for k, s in enumerate((s_src, s_dst)):
                for h in range(GH):
                    late.append((vectors[i][(h % 2) * GC:(h % 2 + 1) * GC, h // 2, k * GH + h:k * GH + h + 1],
                                 s[h, :].rearrange("(c o) -> c o", o=1)))
        prepare(nc, c, a.x, x, loads, late, vectors,
                [(kv_rows[DUMMY:DUMMY + P, :], KVW, slice(D // QH, QW, D // QH + 1)), (q_rows[DUMMY:DUMMY + P, :], QW, None)]
                + [(h_rows[i][DUMMY:DUMMY + P, :], GW, slice(D, D + GH)) for i in range(2)]
                + [(y_rows.rearrange("t p f -> (t p) f")[t * P:(t + 1) * P, :], D, None) for t in range(A_ROWS // P, MAX_SLOT_TILES + 1)])

        project_qkv(nc, c, qkv_w, qkv_b, x, q_rows, kv_rows)
        qkv.__exit__(None, None, None)
        with Mem(nc, "at") as p:
            own = p.sb("own", [P, NT, QW])
            attend(nc, c, graphs[0], "att", QH, own, q_rows, kv_rows, KVW, att_rows, True)
        with Mem(nc, "wo") as p:
            add_product(nc, c, "wop", p.sb("att", [P, NT, D]), att_rows, wo, bo, x)
        first.__exit__(None, None, None)

        xn_rows = dram("xn_rows", (NPAD, D))
        r = Names()
        r.weight, r.slot = m.sb("r_weight", [P, 2, NT]), m.sb("r_slot", [P, 2, NT], I32)
        r.node, r.expert, r.first_tile = m.sb("r_node", [P, SLOT_COLS], I32), m.sb("r_expert", [P, SLOT_COLS], I32), m.sb("r_first_tile", [P, NE + 1], I32)
        with Mem(nc, "ro") as p:
            xt, xn = p.sb("xt", [P, NT, D]), p.sb("xn", [P, NT, D])
            logits = p.sb("logits", [P, NT, NE])
            layernorm(nc, c, "ln1", x, xt)
            layernorm(nc, c, "ln1i", xt, xn)
            project(nc, c, "rop", wr, br, NE, 1, a=xt,
                    take_dve=lambda dve, t, prod: dve.tensor_copy(logits[:, bass.ds(t, 1), :], prod[:, :, 0:NE]),
                    store=lambda sp, k: [sp.dma_start(xn_rows[GROUP * k * P:GROUP * (k + 1) * P, :].rearrange("(t p) f -> p t f", p=P),
                                                      xn[:, GROUP * k:GROUP * (k + 1), :])], n_stores=1)
            route(nc, c, r, logits)
        w = Names()
        w.w1, w.w2, w.b1, w.b2, w.ln_g, w.ln_b = a.W1, a.W2, a.b1, a.b2, a.ln_g, a.ln_b
        experts(nc, c, r, xn_rows, y_rows, w)
        combine(nc, c, r, y_rows.rearrange("t p f -> (t p) f"), x)

        g_rows = dram("g_rows", (TABLE_ROWS, D))
        g = graphs[1]
        with Mem(nc, "gat") as p:
            own = [p.sb(f"own{i}", [P, NT, GW]) for i in range(2)]
            with Mem(nc, "gat0") as q:
                h_out = q.sb("h_out", [P, NT, GW])
                mean, inv = q.sb("mean", [P, NT, 2]), q.sb("inv", [P, NT])
                gat_weights(nc, c, ga, vectors)
                norm_stats(nc, c, "ln2", x, mean, inv)
                project(nc, c, "gap0", ga[0], None, GW, 1, norm=(x, mean, inv),
                        take_dve=lambda dve, t, prod: dve.tensor_copy(h_out[:, bass.ds(t, 1), :], prod[:, :, 0:GW]),
                        store=lambda sp, k: [sp.dma_start(tiles(h_rows[0], GW)[:, table_tiles(k), :], h_out[:, GROUP * k:GROUP * (k + 1), :])], n_stores=1)
            attend(nc, c, g, "gt0", GH, own[0], h_rows[0], h_rows[0], GW, None, False, bias_row=a.gb0)
            project(nc, c, "gap1", ga[1], None, GW, 1, a=own[0][:, :, 0:D],
                    take_dve=lambda dve, t, prod: dve.tensor_copy(own[1][:, bass.ds(t, 1), :], prod[:, :, 0:GW]),
                    scatter=lambda pool, t: pool.indirect_dma_start(
                        out=h_rows[1], out_offset=bass.IndirectOffsetOnAxis(ap=g.order[:, t:t + 1], axis=0), in_=own[1][:, t, :], in_offset=None))
            attend(nc, c, g, "gt1", GH, own[1], None, h_rows[1], GW, g_rows, False, bias_row=a.gb1)

        with Mem(nc, "last") as p:
            mean, inv = p.sb("mean", [P, NT, 2]), p.sb("inv", [P, NT])
            raw, w5 = p.sb("raw", [P, NT, E2]), p.sb("w5", [P, NT, E2 + 1])
            add_rows(nc, c, "addg", x, g_rows)
            norm_stats(nc, c, "ln3", x, mean, inv)
            project(nc, c, "gap", gw, gb, E2, 1, norm=(x, mean, inv),
                    take_dve=lambda dve, t, prod: dve.tensor_copy(raw[:, bass.ds(t, 1), :], prod[:, :, 0:E2]))
            gates_to_weights(nc, c, raw, w5)
            shared_and_experts(nc, c, (x, mean, inv), x, w5, a, out)


def project_qkv(nc, c, wt, bias, x, q_rows, kv_rows):
    with Mem(nc, "qv") as p:
        mean, inv = p.sb("mean", [P, NT, 2]), p.sb("inv", [P, NT])
        q_all, kv_all = p.sb("q_all", [P, NT, QW]), p.sb("kv_all", [P, NT, KVW])
        q_scale = float((D // QH) ** -0.5)
        norm_stats(nc, c, "ln0", x, mean, inv)
        cleared = p.sem("cleared")
        hd = D // QH

        def heads(rows):
            return rows.rearrange("p t (h d) -> p t h d", d=hd + 1)

        with nc.Block() as block:
            @block.vector
            def _(dve):
                dve.memset(heads(kv_all[:, :, 0:QW])[:, :, :, hd], 0.0).then_inc(cleared, 1)
                dve.memset(heads(q_all[:, :, :])[:, :, :, hd], 1.0).then_inc(cleared, 1)
                dve.tensor_scalar(bias[:, 0:D], bias[:, 0:D], q_scale, None, ALU.mult).then_inc(cleared, 1)
                dve.wait_ge(cleared, 3)
        half = 3 * D // 2

        def by_head(cols):
            return cols.rearrange("p (h d) -> p h d", d=hd)

        def take_dve(dve, t, prod):
            q = heads(q_all[:, bass.ds(t, 1), :]).rearrange("p a h d -> p (a h) d")
            k = heads(kv_all[:, bass.ds(t, 1), 0:QW]).rearrange("p a h d -> p (a h) d")
            first = (half - D) // hd
            dve.scalar_tensor_tensor(q[:, :, 0:hd], by_head(prod[:, 0, 0:D]), q_scale, by_head(bias[:, 0:D]), ALU.mult, ALU.add)
            dve.tensor_tensor(k[:, 0:first, 0:hd], by_head(prod[:, 0, D:half]), by_head(bias[:, D:half]), ALU.add)
            dve.tensor_tensor(k[:, first:QH, 0:hd], by_head(prod[:, 1, 0:2 * D - half]), by_head(bias[:, half:2 * D]), ALU.add)
            return dve.tensor_tensor(kv_all[:, bass.ds(t, 1), QW:KVW].rearrange("p a n -> p (a n)"), prod[:, 1, 2 * D - half:half],
                                     bias[:, 2 * D:3 * D], ALU.add)

        project(nc, c, "qkp", wt, None, 3 * D, 2, norm=(x, mean, inv), take_dve=take_dve,
                store=lambda sp, k: [sp.dma_start(tiles(q_rows, QW)[:, table_tiles(k), :], q_all[:, GROUP * k:GROUP * (k + 1), :]),
                                     sp.dma_start(tiles(kv_rows, KVW)[:, table_tiles(k), :], kv_all[:, GROUP * k:GROUP * (k + 1), :])], n_stores=2)


def add_product(nc, c, name, att, att_rows, wt, bias, x):
    def take_dve(dve, t, prod):
        xt = x[:, bass.ds(t, 1), :].rearrange("p a n -> p (a n)")
        return dve.tensor_tensor(xt, xt, prod[:, 0, 0:D], ALU.add)

    project(nc, c, name, wt, bias, D, 1, a=att, take_dve=take_dve,
            load=lambda sp, k: sp.dma_start(att[:, GROUP * k:GROUP * (k + 1), :], tiles(att_rows, D)[:, table_tiles(k), :]))


def add_rows(nc, c, name, x, rows):
    with Mem(nc, name) as m:
        buf = m.sb("buf", [P, NT, D])
        loaded = [m.sem(f"loaded{k}") for k in range(NT // GROUP)]
        added = m.sem("added")
        with nc.Block() as block:
            @block.sync
            def _(sp):
                for k in range(NT // GROUP):
                    sp.dma_start(buf[:, GROUP * k:GROUP * (k + 1), :], tiles(rows, D)[:, table_tiles(k), :]).then_inc(loaded[k], 16)

            @block.vector
            def _(dve):
                for k in range(NT // GROUP):
                    dve.wait_ge(loaded[k], 16)
                    part = x[:, GROUP * k:GROUP * (k + 1), :]
                    dve.tensor_tensor(part, part, buf[:, GROUP * k:GROUP * (k + 1), :], ALU.add).then_inc(added, 1)
                dve.wait_ge(added, NT // GROUP)


ARRAYS = {
    "x": "x", "src": "src", "dst": "dst",
    "Wq": "L0_gnn_Wq", "bq": "L0_gnn_bq", "Wk": "L0_gnn_Wk", "bk": "L0_gnn_bk", "Wv": "L0_gnn_Wv", "bv": "L0_gnn_bv",
    "Wo": "L0_gnn_Wo", "bo": "L0_gnn_bo",
    "Wr": "L0_ffn_Wr", "br": "L0_ffn_br", "ln_g": "L0_ffn_ln_g", "ln_b": "L0_ffn_ln_b",
    "W1": "L0_ffn_W1", "b1": "L0_ffn_b1", "W2": "L0_ffn_W2", "b2": "L0_ffn_b2",
    "gW0": "L1_gnn_W0", "a_src0": "L1_gnn_a_src0", "a_dst0": "L1_gnn_a_dst0", "gb0": "L1_gnn_b0",
    "gW1": "L1_gnn_W1", "a_src1": "L1_gnn_a_src1", "a_dst1": "L1_gnn_a_dst1", "gb1": "L1_gnn_b1",
    "sW1": "L1_ffn_sW1", "sb1": "L1_ffn_sb1", "sW2": "L1_ffn_sW2", "sb2": "L1_ffn_sb2", "sW3": "L1_ffn_sW3", "sb3": "L1_ffn_sb3",
    "eW1": "L1_ffn_eW1", "eb1": "L1_ffn_eb1", "eW2": "L1_ffn_eW2", "eb2": "L1_ffn_eb2", "eW3": "L1_ffn_eW3", "eb3": "L1_ffn_eb3",
    "gW": "L1_ffn_gW", "gb": "L1_ffn_gb",
}


def head_major(v, axis):
    v = np.moveaxis(v, axis, -1)
    v = v.reshape(v.shape[:-1] + (D // QH, QH)).swapaxes(-1, -2).reshape(v.shape)
    return np.ascontiguousarray(np.moveaxis(v, -1, axis))


def kernel(**inputs):
    import concourse.bacc as bacc
    from concourse.bass_utils import run_bass_kernel_spmd

    nc = bacc.Bacc("TRN2", target_bir_lowering=False, num_devices=1)
    arrays, a = {}, Names()
    for name, full in ARRAYS.items():
        v = np.ascontiguousarray(inputs[full])
        if name in ("Wq", "Wk", "Wv", "bq", "bk", "bv"):
            v = head_major(v, v.ndim - 1)
        if name == "Wo":
            v = head_major(v, 0)
        arrays[f"in_{name}"] = v
        vars(a)[name] = nc.dram_tensor(f"in_{name}", v.shape, mybir.dt.from_np(v.dtype), kind="ExternalInput").ap()
    out = nc.dram_tensor("out", (N_NODES, D), F32, kind="ExternalOutput").ap()
    program(nc, a, out)
    r = run_bass_kernel_spmd(nc, [arrays], core_ids=[0])
    return r.results[0]["out"]
```
